# Optimizing a Trainium2 kernel written in Bass

```python
import numpy as np
import jax
import jax.numpy as jnp

def _softmax(x, axis=-1):
    return jax.nn.softmax(x, axis=axis)

def _gelu(x):
    return jax.nn.gelu(x, approximate=True)

def _silu(x):
    return jax.nn.silu(x)

def _sigmoid(x):
    return jax.nn.sigmoid(x)

def _layernorm(x, axis=-1, eps=1e-05):
    m = jnp.mean(x, axis=axis, keepdims=True)
    v = jnp.var(x, axis=axis, keepdims=True)
    return (x - m) / jnp.sqrt(v + eps)

def _scatter_add(tgt, idx, src, axis=0):
    return tgt.at[idx].add(src)

def _segment_sum(src, seg, n):
    return jax.ops.segment_sum(src, seg, n)
kernel_name = 'mk_audio_tower_d1_tok_audfeat4096_r4_a85da6'

def setup_inputs(seed: int=0):
    np.random.seed(seed)
    _w = jnp.asarray

    def _rec_inputs():
        import jax
        import jax.numpy as jnp
        _rk = jax.random.key(seed)
        x = -5.77387e-05 + 0.999872 * jax.random.normal(jax.random.fold_in(_rk, 1), (32, 750, 320), jnp.float32)
        return x
    x = _rec_inputs()

    def _L0_tok_setup():
        import jax, jax.numpy as jnp
        import numpy as np
        STACK_FACTOR = 8
        EPS = 1e-06

        def _rms_norm(x, w):
            var = jnp.mean(jnp.square(x), axis=-1, keepdims=True)
            return x * jax.lax.rsqrt(var + EPS) * w
        key = jax.random.key(seed)
        k0, k1, k2 = jax.random.split(key, 3)
        B, T, C = (16, 375, 320)
        stacked_dim = C * STACK_FACTOR
        hidden = 1024
        out_dim = 1024
        audio_features = jax.random.normal(k0, (B, T, C), dtype=jnp.float32)
        w1 = jax.random.normal(k1, (hidden, stacked_dim), dtype=jnp.float32) * 0.02
        w2 = jax.random.normal(k2, (out_dim, hidden // 2), dtype=jnp.float32) * 0.02
        ln_pre_w = jnp.ones((stacked_dim,), dtype=jnp.float32)
        ln_post_w = jnp.ones((out_dim,), dtype=jnp.float32)
        return {'audio_features': audio_features, 'w1': w1, 'w2': w2, 'ln_pre_w': ln_pre_w, 'ln_post_w': ln_post_w}
    _L0_tok_all = _L0_tok_setup()
    _L0_tok_in = {k: v for k, v in _L0_tok_all.items() if k in ('w1', 'w2', 'ln_pre_w', 'ln_post_w')}
    del _L0_tok_all

    def _L0_attn_setup():
        import math
        import jax, jax.numpy as jnp
        import numpy as np
        H = 32
        NOPE = 64
        ROPE = 64
        VD = 128
        QHD = NOPE + ROPE
        KVR = 64
        EPS = 1e-06

        def _yarn_cos_sin(seq_len, dim=ROPE, base=10000.0, factor=128.0, beta_fast=32.0, beta_slow=1.0, orig_max=2048, mscale=1.0, mscale_all_dim=1.0):

            def corr_dim(r):
                return dim * math.log(orig_max / (r * 2 * math.pi)) / (2 * math.log(base))
            low = max(math.floor(corr_dim(beta_fast)), 0)
            high = min(math.ceil(corr_dim(beta_slow)), dim - 1)
            hi = high + 0.001 if low == high else float(high)
            ramp = np.clip((np.arange(dim // 2, dtype=np.float32) - low) / (hi - low), 0.0, 1.0)
            inv_freq_mask = 1.0 - ramp
            freq_extra = 1.0 / base ** (np.arange(0, dim, 2, dtype=np.float32) / dim)
            freq_inter = freq_extra / factor
            inv_freq = freq_inter * (1.0 - inv_freq_mask) + freq_extra * inv_freq_mask
            t = np.arange(seq_len, dtype=np.float32)
            freqs = np.outer(t, inv_freq)
            emb = np.concatenate([freqs, freqs], axis=-1)

            def gm(s, m):
                return 1.0 if s <= 1 else 0.1 * m * math.log(s) + 1.0
            ms = gm(factor, mscale) / gm(factor, mscale_all_dim)
            return (jnp.asarray(np.cos(emb) * ms), jnp.asarray(np.sin(emb) * ms))

        def _rmsnorm(x, w, eps=EPS):
            var = jnp.mean(jnp.square(x), axis=-1, keepdims=True)
            return x * jax.lax.rsqrt(var + eps) * w

        def _deinterleave(x):
            d = x.shape[-1]
            x = x.reshape(*x.shape[:-1], d // 2, 2)
            return jnp.concatenate([x[..., 0], x[..., 1]], axis=-1)

        def _rotate_half(x):
            d = x.shape[-1] // 2
            return jnp.concatenate([-x[..., d:], x[..., :d]], axis=-1)

        def _apply_rope(x, cos, sin):
            return x * cos + _rotate_half(x) * sin
        key = jax.random.key(seed)
        ks = jax.random.split(key, 6)
        B, S, D = (1, 512, 1024)
        std = 0.02
        return {'x': jax.random.normal(ks[0], (B, S, D), dtype=jnp.float32), 'wq_a': jax.random.normal(ks[1], (256, D), dtype=jnp.float32) * std, 'q_a_ln_w': jnp.ones((256,), dtype=jnp.float32), 'wq_b': jax.random.normal(ks[2], (H * QHD, 256), dtype=jnp.float32) * std, 'wkv_a': jax.random.normal(ks[3], (KVR + ROPE, D), dtype=jnp.float32) * std, 'kv_a_ln_w': jnp.ones((KVR,), dtype=jnp.float32), 'wkv_b': jax.random.normal(ks[4], (H * (NOPE + VD), KVR), dtype=jnp.float32) * std, 'wo': jax.random.normal(ks[5], (D, H * VD), dtype=jnp.float32) * std}
    _L0_attn_all = _L0_attn_setup()
    _L0_attn_in = {k: v for k, v in _L0_attn_all.items() if k in ('wq_a', 'q_a_ln_w', 'wq_b', 'wkv_a', 'kv_a_ln_w', 'wkv_b', 'wo')}
    del _L0_attn_all

    def _L0_ffn_setup():
        import jax, jax.numpy as jnp
        import numpy as np
        SCALING = 32.0 / 16.0
        key = jax.random.key(seed)
        ks = jax.random.split(key, 7)
        B, T, D, O, R, E = (4, 512, 1024, 1024, 16, 8)
        x = jax.random.normal(ks[0], (B, T, D), dtype=jnp.float32)
        base_W = jax.random.normal(ks[1], (O, D), dtype=jnp.float32) * D ** (-0.5)
        base_b = jax.random.normal(ks[2], (O,), dtype=jnp.float32) * 0.01
        router_W = jax.random.normal(ks[3], (2 * E - 1, D), dtype=jnp.float32) * D ** (-0.5)
        router_b = jax.random.normal(ks[4], (2 * E - 1,), dtype=jnp.float32) * 0.01
        A = jax.random.normal(ks[5], (E, R, D), dtype=jnp.float32) * D ** (-0.5)
        Bm = jax.random.normal(ks[6], (E, O, R), dtype=jnp.float32) * R ** (-0.5)
        assigned_idx = 0
        others = [i for i in range(E) if i != assigned_idx]
        expert_map = jnp.array([assigned_idx] * E + others, dtype=jnp.int32)
        return {'x': x, 'base_W': base_W, 'base_b': base_b, 'router_W': router_W, 'router_b': router_b, 'A': A, 'B': Bm, 'expert_map': expert_map}
    _L0_ffn_all = _L0_ffn_setup()
    _L0_ffn_in = {k: v for k, v in _L0_ffn_all.items() if k in ('base_W', 'base_b', 'router_W', 'router_b', 'A', 'B', 'expert_map')}
    del _L0_ffn_all
    return {'x': x, 'L0_tok_w1': _L0_tok_in['w1'], 'L0_tok_w2': _L0_tok_in['w2'], 'L0_tok_ln_pre_w': _L0_tok_in['ln_pre_w'], 'L0_tok_ln_post_w': _L0_tok_in['ln_post_w'], 'L0_attn_wq_a': _L0_attn_in['wq_a'], 'L0_attn_q_a_ln_w': _L0_attn_in['q_a_ln_w'], 'L0_attn_wq_b': _L0_attn_in['wq_b'], 'L0_attn_wkv_a': _L0_attn_in['wkv_a'], 'L0_attn_kv_a_ln_w': _L0_attn_in['kv_a_ln_w'], 'L0_attn_wkv_b': _L0_attn_in['wkv_b'], 'L0_attn_wo': _L0_attn_in['wo'], 'L0_ffn_base_W': _L0_ffn_in['base_W'], 'L0_ffn_base_b': _L0_ffn_in['base_b'], 'L0_ffn_router_W': _L0_ffn_in['router_W'], 'L0_ffn_router_b': _L0_ffn_in['router_b'], 'L0_ffn_A': _L0_ffn_in['A'], 'L0_ffn_B': _L0_ffn_in['B'], 'L0_ffn_expert_map': _L0_ffn_in['expert_map']}

def reference(x, L0_tok_w1, L0_tok_w2, L0_tok_ln_pre_w, L0_tok_ln_post_w, L0_attn_wq_a, L0_attn_q_a_ln_w, L0_attn_wq_b, L0_attn_wkv_a, L0_attn_kv_a_ln_w, L0_attn_wkv_b, L0_attn_wo, L0_ffn_base_W, L0_ffn_base_b, L0_ffn_router_W, L0_ffn_router_b, L0_ffn_A, L0_ffn_B, L0_ffn_expert_map):
    import jax
    import jax.numpy as jnp

    def _L0_tok_ref(audio_features, w1, w2, ln_pre_w, ln_post_w):
        import jax, jax.numpy as jnp
        import numpy as np
        STACK_FACTOR = 8
        EPS = 1e-06

        def _rms_norm(x, w):
            var = jnp.mean(jnp.square(x), axis=-1, keepdims=True)
            return x * jax.lax.rsqrt(var + EPS) * w
        B, T, C = audio_features.shape
        s = STACK_FACTOR
        T_pad = (T + s - 1) // s * s
        x = jnp.pad(audio_features, ((0, 0), (0, T_pad - T), (0, 0)))
        x = x.reshape(B, T_pad // s, C * s)
        x = _rms_norm(x, ln_pre_w)
        h = jnp.einsum('btd,hd->bth', x, w1)
        d = h.shape[-1] // 2
        h = jax.nn.silu(h[..., d:]) * h[..., :d]
        y = jnp.einsum('btd,od->bto', h, w2)
        return _rms_norm(y, ln_post_w)

    def _L0_attn_ref(x, wq_a, q_a_ln_w, wq_b, wkv_a, kv_a_ln_w, wkv_b, wo):
        import math
        import jax, jax.numpy as jnp
        import numpy as np
        H = 32
        NOPE = 64
        ROPE = 64
        VD = 128
        QHD = NOPE + ROPE
        KVR = 64
        EPS = 1e-06

        def _yarn_cos_sin(seq_len, dim=ROPE, base=10000.0, factor=128.0, beta_fast=32.0, beta_slow=1.0, orig_max=2048, mscale=1.0, mscale_all_dim=1.0):

            def corr_dim(r):
                return dim * math.log(orig_max / (r * 2 * math.pi)) / (2 * math.log(base))
            low = max(math.floor(corr_dim(beta_fast)), 0)
            high = min(math.ceil(corr_dim(beta_slow)), dim - 1)
            hi = high + 0.001 if low == high else float(high)
            ramp = np.clip((np.arange(dim // 2, dtype=np.float32) - low) / (hi - low), 0.0, 1.0)
            inv_freq_mask = 1.0 - ramp
            freq_extra = 1.0 / base ** (np.arange(0, dim, 2, dtype=np.float32) / dim)
            freq_inter = freq_extra / factor
            inv_freq = freq_inter * (1.0 - inv_freq_mask) + freq_extra * inv_freq_mask
            t = np.arange(seq_len, dtype=np.float32)
            freqs = np.outer(t, inv_freq)
            emb = np.concatenate([freqs, freqs], axis=-1)

            def gm(s, m):
                return 1.0 if s <= 1 else 0.1 * m * math.log(s) + 1.0
            ms = gm(factor, mscale) / gm(factor, mscale_all_dim)
            return (jnp.asarray(np.cos(emb) * ms), jnp.asarray(np.sin(emb) * ms))

        def _rmsnorm(x, w, eps=EPS):
            var = jnp.mean(jnp.square(x), axis=-1, keepdims=True)
            return x * jax.lax.rsqrt(var + eps) * w

        def _deinterleave(x):
            d = x.shape[-1]
            x = x.reshape(*x.shape[:-1], d // 2, 2)
            return jnp.concatenate([x[..., 0], x[..., 1]], axis=-1)

        def _rotate_half(x):
            d = x.shape[-1] // 2
            return jnp.concatenate([-x[..., d:], x[..., :d]], axis=-1)

        def _apply_rope(x, cos, sin):
            return x * cos + _rotate_half(x) * sin
        B, S, D = x.shape
        m = 0.1 * 1.0 * math.log(128.0) + 1.0
        softmax_scale = QHD ** (-0.5) * m * m
        q = _rmsnorm(x @ wq_a.T, q_a_ln_w) @ wq_b.T
        q = q.reshape(B, S, H, QHD)
        q_nope, q_pe = (q[..., :NOPE], q[..., NOPE:])
        ckv_kpe = x @ wkv_a.T
        ckv, k_pe = (ckv_kpe[..., :KVR], ckv_kpe[..., KVR:])
        kv = _rmsnorm(ckv, kv_a_ln_w) @ wkv_b.T
        kv = kv.reshape(B, S, H, NOPE + VD)
        k_nope, v = (kv[..., :NOPE], kv[..., NOPE:])
        cos, sin = _yarn_cos_sin(S)
        q_pe = _apply_rope(_deinterleave(q_pe), cos[None, :, None, :], sin[None, :, None, :])
        k_pe = _apply_rope(_deinterleave(k_pe), cos[None, :, :], sin[None, :, :])
        q_full = jnp.concatenate([q_nope, q_pe], axis=-1)
        k_full = jnp.concatenate([k_nope, jnp.broadcast_to(k_pe[:, :, None, :], (B, S, H, ROPE))], axis=-1)
        scores = jnp.einsum('bqhd,bkhd->bhqk', q_full, k_full) * softmax_scale
        causal = jnp.tril(jnp.ones((S, S), dtype=bool))
        scores = jnp.where(causal[None, None], scores, jnp.finfo(scores.dtype).min)
        attn = jax.nn.softmax(scores, axis=-1)
        out = jnp.einsum('bhqk,bkhd->bqhd', attn, v).reshape(B, S, H * VD)
        return out @ wo.T

    def _L0_ffn_ref(x, base_W, base_b, router_W, router_b, A, B, expert_map):
        import jax, jax.numpy as jnp
        import numpy as np
        SCALING = 32.0 / 16.0
        E = A.shape[0]
        base_out = jnp.einsum('btd,od->bto', x, base_W) + base_b
        logits = jnp.einsum('btd,nd->btn', x, router_W) + router_b
        probs = jax.nn.softmax(logits, axis=-1)
        topk_p, topk_i = jax.lax.top_k(probs, E)
        mapped = expert_map[topk_i]
        onehot = (mapped[..., None] == jnp.arange(E)).astype(x.dtype)
        w = jnp.einsum('btk,btke->bte', topk_p, onehot)
        h = jnp.einsum('btd,erd->bter', x, A)
        lora = jnp.einsum('bter,eor->bto', h * w[..., None], B) * SCALING
        return base_out + lora
    h = _L0_tok_ref(x, L0_tok_w1, L0_tok_w2, L0_tok_ln_pre_w, L0_tok_ln_post_w)
    h = h + _L0_attn_ref(_layernorm(h, axis=-1), L0_attn_wq_a, L0_attn_q_a_ln_w, L0_attn_wq_b, L0_attn_wkv_a, L0_attn_kv_a_ln_w, L0_attn_wkv_b, L0_attn_wo)
    h = h + _L0_ffn_ref(_layernorm(h, axis=-1), L0_ffn_base_W, L0_ffn_base_b, L0_ffn_router_W, L0_ffn_router_b, L0_ffn_A, L0_ffn_B, L0_ffn_expert_map)
    return h

_drawn_inputs = setup_inputs


def setup_inputs(seed=0):
    import zlib

    import numpy as np

    out = dict(_drawn_inputs(seed))
    spreads = {'L0_tok_ln_pre_w': (1.0, 0.2),
     'L0_tok_ln_post_w': (1.0, 0.2),
     'L0_attn_q_a_ln_w': (1.0, 0.6),
     'L0_attn_kv_a_ln_w': (1.0, 0.6)}
    factors = {'L0_attn_wq_a': 3.227,
     'L0_attn_wq_b': 3.155,
     'L0_ffn_base_b': 8.0,
     'L0_ffn_router_b': 7.112}
    for name, (base, spread) in spreads.items():
        noise = np.random.default_rng([zlib.crc32(name.encode()), seed]).standard_normal(out[name].shape)
        drawn = base * np.exp(spread * noise) if base else spread * noise
        out[name] = jnp.asarray(drawn.astype(out[name].dtype))
    for name, factor in factors.items():
        out[name] = (out[name] * factor).astype(out[name].dtype)
    return out
```

```python
import math
from contextlib import ExitStack

import numpy as np

import concourse.bass as bass
from concourse import mybir

F32 = mybir.dt.float32
F32R = mybir.dt.float32r
BF16 = mybir.dt.bfloat16
I32 = mybir.dt.int32
ALU = mybir.AluOpType
ACT = mybir.ActivationFunctionType
AX = mybir.AxisListType

P = 128
BATCH, SEQ = 32, 94
TOK = BATCH * SEQ
TILES = -(-TOK // P)
TOKP = TILES * P
DIN = 2560
KIN = DIN // P
HID = 512
DM = 1024
KM = DM // P
QR, KR, RO = 256, 64, 64
NH = 32
PAIRS = NH // 2
NOPE, VD = 64, 128
GROUPS, GB = 8, 4
GT = GB * SEQ
EXP, RANK = 8, 16
NR = 2 * EXP - 1
RMS_EPS, LN_EPS = 1e-6, 1e-5
SCALE = float((NOPE + RO) ** -0.5 * (0.1 * math.log(128.0) + 1.0) ** 2)
KCH = 5
NCH = KIN // KCH
MASKED = -1.0e30


def stage(k, m, d, unroll, n):
    place = (m - d) % unroll
    body = k + (m - d - place) // unroll
    item = body * unroll + place
    if isinstance(k, int) and not 0 <= item < n:
        return None
    return item, place, body


def first(item, n):
    return isinstance(item, int) and item < n


def run_steps(eng, n, depth, unroll, body, last=0):
    peel = -(-(depth + 2) // unroll)
    for k in range(peel):
        for m in range(unroll):
            body(k, m)
    with eng.Fori(peel, n // unroll - last) as k:
        for m in range(unroll):
            body(k, m)
    for k in range(n // unroll - last, n // unroll):
        for m in range(unroll):
            body(k, m)
    for s in range(n, n + depth):
        body(s // unroll, s % unroll)


class Link:

    def __init__(self, eng, sem, per_step):
        self.eng, self.sem, self.per_step = eng, sem, per_step
        self.base, self.n = 0, 0

    def step(self, number):
        self.base, self.n = number * self.per_step, 0

    def __call__(self, ins):
        self.n += 1
        ins.then_inc(self.sem, 1)
        self.eng.wait_ge(self.sem, self.base + self.n)

    def settle(self):
        self.n += 1
        self.eng.sem_inc(self.sem, 1)

    def fill(self):
        left = self.per_step - self.n
        assert left >= 0, self.n
        if left:
            self.eng.sem_inc(self.sem, left)


def inv_sqrt(nc, link, v, y, t):
    vi, yi = v.bitcast(I32), y.bitcast(I32)
    link(nc.vector.tensor_scalar(yi, vi, 1, None, ALU.arith_shift_right))
    link(nc.vector.tensor_scalar(yi, yi, -1, 0x5F3759DF, ALU.mult, ALU.add))
    for _ in range(3):
        link(nc.vector.tensor_tensor(t, y, y, ALU.mult))
        link(nc.vector.tensor_tensor(t, t, v, ALU.mult))
        link(nc.vector.tensor_scalar(t, t, -0.5, 1.5, ALU.mult, ALU.add))
        link(nc.vector.tensor_tensor(y, y, t, ALU.mult))


INV_SQRT_LINKS = 14


class Memory:

    whole = None

    def __init__(self, nc, ctx, name):
        self.nc, self.ctx, self.name = nc, ctx, name

    def sb(self, name, shape, dt=F32):
        return self.ctx.enter_context(self.nc.sbuf_tensor(f"{self.name}_{name}", shape, dt))

    def ps(self, name, shape, dt=F32):
        return self.ctx.enter_context(self.nc.psum_tensor(f"{self.name}_{name}", shape, dt))

    def sem(self, name):
        return self.ctx.enter_context(self.nc.semaphore(f"{self.name}_{name}"))

    def stored(self, name, n):
        return [Memory.whole.enter_context(self.nc.semaphore(f"{self.name}_{name}{i}")) for i in range(n)]

    def sems(self, name, n):
        return [self.sem(f"{name}{i}") for i in range(n)]


def fold_weights(nc, d, ident):
    with ExitStack() as ctx:
        mem = Memory(nc, ctx, "fold")
        wqn = [mem.sb(f"wqn{i}", [P, QR]) for i in range(2)]
        wk = [mem.sb(f"wk{i}", [P, KR]) for i in range(2)]
        wqp = [mem.sb(f"wqp{i}", [P, 2, P]) for i in range(2)]
        wv = [mem.sb(f"wv{i}", [P, 2, KR]) for i in range(2)]
        wo = [mem.sb(f"wo{i}", [P, 2, DM]) for i in range(2)]
        qln = mem.sb("qln", [P, 2])
        wq_out = [mem.sb(f"wq_out{i}", [P, 2, 2 * P]) for i in range(2)]
        wv_out = [mem.sb(f"wv_out{i}", [P, DM]) for i in range(2)]
        ps_q = [mem.ps(f"ps_q{i}", [P, 512]) for i in range(2)]
        ps_v = mem.ps("ps_v", [P, DM])
        small_in = mem.sems("small_in", 2)
        wo_in = mem.sems("wo_in", 2)
        qln_in = mem.sem("qln_in")
        q_done = mem.sem("q_done")
        v_done = mem.sem("v_done")
        q_out = mem.sem("q_out")
        v_out = mem.sem("v_out")
        pe_copied = mem.sem("pe_copied")
        q_stored = mem.stored("q_stored", 2)
        v_stored = mem.stored("v_stored", 2)
        block = ctx.enter_context(nc.Block())

        @block.sync
        def _(sp):
            sp.dma_start(qln[:], d["q_ln"]).then_inc(qln_in, 16)

            def body(k, m):
                p, b = 2 * k + m, m
                if not first(p, 2):
                    sp.wait_ge(q_done, p - 1)
                    sp.wait_ge(v_done, p - 1)
                    sp.wait_ge(pe_copied, p - 1)
                sp.dma_start(wqn[b][:], d["wq_nope"][p]).then_inc(small_in[b], 16)
                sp.dma_start(wk[b][:], d["wk"][p]).then_inc(small_in[b], 16)
                sp.dma_start(wqp[b][:], d["wq_rope"][p]).then_inc(small_in[b], 16)
                sp.dma_start(wv[b][:], d["wv"][p]).then_inc(small_in[b], 16)
                sp.dma_start(wo[b][:], d["wo"][p]).then_inc(wo_in[b], 16)

            run_steps(sp, PAIRS, 0, 2, body)

        @block.tensor
        def _(pe):
            def body(k, m):
                s = stage(k, m, 0, 2, PAIRS)
                if s is None:
                    return
                p, b, kb = s
                pe.wait_ge(small_in[b], 64 * kb + 64)
                if not first(p, 1):
                    pe.wait_ge(q_out, p)
                for c in range(2):
                    for h in range(2):
                        rows = slice(64 * h, 64 * h + 64)
                        last = nc.tensor.matmul(ps_q[h][:, 64 * c:64 * c + 64], wqn[b][rows, P * c:P * c + P],
                                                wk[b][rows, :], start=True, stop=True)
                last.then_inc(q_done, 1)
                pe.wait_ge(wo_in[b], 16 * kb + 16)
                if not first(p, 1):
                    pe.wait_ge(v_out, p)
                for n in range(2):
                    for h in range(2):
                        last = nc.tensor.matmul(ps_v[64 * h:64 * h + 64, 512 * n:512 * n + 512], wv[b][:, h, :],
                                                wo[b][:, h, 512 * n:512 * n + 512], start=True, stop=True)
                last.then_inc(v_done, 1)

            run_steps(pe, PAIRS, 0, 2, body)

        @block.scalar
        def _(act):
            act.wait_ge(qln_in, 16)

            def body(k, m):
                s = stage(k, m, 0, 2, PAIRS)
                if s is None:
                    return
                p, b, kb = s
                act.wait_ge(q_done, p + 1)
                if not first(p, 2):
                    act.wait_ge(q_stored[b], 16 * kb)
                for c in range(2):
                    for h in range(2):
                        last = nc.scalar.activation(wq_out[b][:, c, 64 * h:64 * h + 64], ps_q[h][:, 64 * c:64 * c + 64],
                                                    ACT.Copy, scale=qln[:, c:c + 1])
                last.then_inc(q_out, 1)

            run_steps(act, PAIRS, 0, 2, body)

        @block.vector
        def _(dve):
            dve.wait_ge(qln_in, 16)

            def body(k, m):
                s = stage(k, m, 0, 2, PAIRS)
                if s is None:
                    return
                p, b, kb = s
                dve.wait_ge(small_in[b], 64 * kb + 64)
                if not first(p, 2):
                    dve.wait_ge(q_stored[b], 16 * kb)
                for c in range(2):
                    last = nc.vector.tensor_scalar(wq_out[b][:, c, P:2 * P], wqp[b][:, c, :], qln[:, c:c + 1], None,
                                                   ALU.mult)
                last.then_inc(pe_copied, 1)
                dve.wait_ge(v_done, p + 1)
                if not first(p, 2):
                    dve.wait_ge(v_stored[b], 16 * kb)
                nc.vector.tensor_copy(wv_out[b][:], ps_v[:]).then_inc(v_out, 1)

            run_steps(dve, PAIRS, 0, 2, body)

        @block.gpsimd
        def _(pool):
            def body(k, m):
                s = stage(k, m, 0, 2, PAIRS)
                if s is None:
                    return
                p, b, kb = s
                pool.wait_ge(q_out, p + 1)
                pool.wait_ge(pe_copied, p + 1)
                pool.dma_start(d["wq_pair"][p], wq_out[b][:]).then_inc(q_stored[b], 16)
                pool.wait_ge(v_out, p + 1)
                pool.dma_start(d["wvo"][:, p, :], wv_out[b][:]).then_inc(v_stored[b], 16)

            run_steps(pool, PAIRS, 0, 2, body)
            for b in range(2):
                pool.wait_ge(q_stored[b], 16 * PAIRS // 2)
                pool.wait_ge(v_stored[b], 16 * PAIRS // 2)


class Splitter:

    RING = 4

    def __init__(self, nc):
        self.nc = nc
        mem = Memory(nc, Memory.whole, "split")
        self.loaded = mem.sems("loaded", self.RING)
        self.fac_in = mem.sem("fac_in")
        self.hi_done = mem.sem("hi_done")
        self.lo_done = mem.sem("lo_done")
        self.loads = [0] * self.RING
        self.factors = 0
        self.done = 0

    def __call__(self, name, src, hi, lo, blocks, width, factor=None):
        nc = self.nc
        with ExitStack() as ctx:
            mem = Memory(nc, ctx, name)
            ring = self.RING
            raw = [mem.sb(f"raw{i}", [P, width]) for i in range(ring)]
            fac = mem.sb("fac", [P, blocks])
            done, loads = self.done, list(self.loads)
            self.done += blocks
            for n in range(blocks):
                self.loads[n % ring] += 16
            if factor is not None:
                self.factors += 16
            factors = self.factors
            block = ctx.enter_context(nc.Block())

            @block.sync
            def _(sp):
                if factor is not None:
                    sp.dma_start(fac[:], factor).then_inc(self.fac_in, 16)
                for n in range(blocks):
                    if n >= ring:
                        sp.wait_ge(self.lo_done, done + n - ring + 1)
                    sp.dma_start(raw[n % ring][:], src[:, n, :]).then_inc(self.loaded[n % ring], 16)

            @block.scalar
            def _(act):
                if factor is not None:
                    act.wait_ge(self.fac_in, factors)
                for n in range(blocks):
                    act.wait_ge(self.loaded[n % ring], loads[n % ring] + 16 * (n // ring + 1))
                    by = {} if factor is None else {"scale": fac[:, n:n + 1]}
                    nc.scalar.activation(hi[:, n, :], raw[n % ring][:], ACT.Copy, **by).then_inc(self.hi_done, 1)

            @block.vector
            def _(dve):
                if factor is not None:
                    dve.wait_ge(self.fac_in, factors)
                for n in range(blocks):
                    dve.wait_ge(self.hi_done, done + n + 1)
                    if factor is None:
                        ins = nc.vector.tensor_tensor(lo[:, n, :], raw[n % ring][:], hi[:, n, :], ALU.subtract)
                    else:
                        ins = nc.vector.scalar_tensor_tensor(lo[:, n, :], raw[n % ring][:], fac[:, n:n + 1],
                                                             hi[:, n, :], ALU.mult, ALU.subtract)
                    ins.then_inc(self.lo_done, 1)


def three_pass(nc, outs, xhi, xlo, his, los, start, stop, onto=False):
    for x, ws, a, b in ((xlo, his, start, False), (xhi, los, False, False), (xhi, his, False, stop)):
        for o, w in zip(outs, ws):
            last = nc.tensor.matmul(o, x, w, start=a, stop=b, skip_group_check=onto)
    return last


def tok_up(nc, d, split, ident):
    with ExitStack() as ctx:
        mem = Memory(nc, ctx, "up")
        w_hi = mem.sb("w_hi", [P, KIN, 2 * HID], F32R)
        w_lo = mem.sb("w_lo", [P, KIN, 2 * HID], F32R)
        split("w1", d["w1"], w_hi, w_lo, KIN, 2 * HID, d["pre_ln"])
        CW = KCH * P
        raw = [mem.sb(f"raw{c}", [P, KCH, P]) for c in range(NCH)]
        x_hi = [mem.sb(f"x_hi{c}", [P, KCH, P], F32R) for c in range(NCH)]
        x_lo = [mem.sb(f"x_lo{c}", [P, KCH, P], F32R) for c in range(NCH)]
        xs = [mem.sb(f"xs{i}", [P, CW]) for i in range(2)]
        junk = mem.sb("junk", [P, CW], BF16)
        ssq = mem.sb("ssq", [P, NCH])
        r = [mem.sb(f"r{i}", [P, 1]) for i in range(2)]
        var = mem.sb("var", [P, 2])
        sil = [mem.sb(f"sil{i}", [P, HID]) for i in range(2)]
        g = sil
        gt = [mem.sb(f"gt{i}", [P, HID]) for i in range(2)]
        ps_h = [mem.ps(f"ps_h{i}", [P, 2 * HID]) for i in range(2)]
        ps_t = [mem.ps(f"ps_t{i}", [P, HID]) for i in range(2)]
        raw_in = mem.sems("raw_in", NCH)
        xs_in = mem.sems("xs_in", 2)
        hi_done = mem.sem("hi_done")
        lo_done = mem.sem("lo_done")
        x_used = mem.sem("x_used")
        sq_done = mem.sem("sq_done")
        r_done = mem.sem("r_done")
        sil_done = mem.sem("sil_done")
        g_done = mem.sem("g_done")
        t_done = mem.sem("t_done")
        gt_done = mem.sem("gt_done")
        gt_stored = mem.stored("gt_stored", 2)
        link_sem = mem.sem("link")
        block = ctx.enter_context(nc.Block())
        DEPTH = 1

        @block.sync
        def _(sp):
            def body(k, m):
                s = stage(k, m, 0, 2, TILES)
                if s is None:
                    return
                t, _, _ = s
                for c in range(NCH):
                    if not first(t, 1):
                        sp.wait_ge(lo_done, 4 * t + (c - 3))
                    sp.dma_start(raw[c][:], d["x_t"][t, :, KCH * c:KCH * c + KCH, :]).then_inc(raw_in[c], 16)
                    if not (first(t, 1) and c < 2):
                        sp.wait_ge(sq_done, 4 * t + (c - 1))
                    sp.dma_start(xs[c % 2][:], d["x_rows"][t, :, CW * c:CW * c + CW]).then_inc(xs_in[c % 2], 16)

            run_steps(sp, TILES, DEPTH, 2, body)

        @block.scalar
        def _(act):
            def body(k, m):
                s = stage(k, m, 0, 2, TILES)
                if s is not None:
                    t, b, _ = s
                    for c in range(NCH):
                        act.wait_ge(raw_in[c], 16 * t + 16)
                        if not first(t, 1):
                            act.wait_ge(x_used, 4 * t + (c - 3))
                        nc.scalar.activation(x_hi[c][:], raw[c][:], ACT.Copy).then_inc(hi_done, 1)
                        if c == 0 and not first(t, 1):
                            act.wait_ge(r_done, t)
                        act.wait_ge(xs_in[c % 2], 32 * t + 16 * (c // 2) + 16)
                        if not (first(t, 1) and c == 0):
                            act.wait_ge(sq_done, 4 * t + c)
                        nc.scalar.activation(junk[:], xs[c % 2][:], ACT.Square,
                                             accum_out=ssq[:, c:c + 1]).then_inc(sq_done, 1)
                s = stage(k, m, 1, 2, TILES)
                if s is not None:
                    t, b, kb = s
                    act.wait_ge(x_used, 4 * t + 4)
                    act.wait_ge(r_done, t + 1)
                    if not first(t, 2):
                        act.wait_ge(t_done, t - 1)
                    nc.scalar.activation(sil[b][:], ps_h[b][:, HID:2 * HID], ACT.Silu,
                                         scale=r[b][:, 0:1]).then_inc(sil_done, 1)
                    act.wait_ge(t_done, t + 1)
                    if not first(t, 2):
                        act.wait_ge(gt_stored[b], 16 * kb)
                    nc.scalar.activation(gt[b][:], ps_t[b][:], ACT.Copy).then_inc(gt_done, 1)

            run_steps(act, TILES, DEPTH, 2, body)

        @block.vector
        def _(dve):
            link = Link(dve, link_sem, INV_SQRT_LINKS + 2)

            def body(k, m):
                s = stage(k, m, 0, 2, TILES)
                if s is not None:
                    t, b, _ = s
                    link.step(t)
                    for c in range(NCH):
                        dve.wait_ge(hi_done, 4 * t + c + 1)
                        nc.vector.tensor_tensor(x_lo[c][:], raw[c][:], x_hi[c][:], ALU.subtract).then_inc(lo_done, 1)
                s1 = stage(k, m, 1, 2, TILES)
                if s1 is not None:
                    t, b, _ = s1
                    dve.wait_ge(sil_done, t + 1)
                    nc.vector.scalar_tensor_tensor(g[b][:], ps_h[b][:, 0:HID], r[b][:, 0:1], sil[b][:],
                                                   ALU.mult, ALU.mult).then_inc(g_done, 1)
                if s is not None:
                    t, b, _ = s
                    dve.wait_ge(sq_done, 4 * t + 4)
                    link(nc.vector.reduce_sum(var[:, 0:1], ssq[:], AX.X))
                    link(nc.vector.tensor_scalar(var[:, 0:1], var[:, 0:1], 1.0 / DIN, RMS_EPS, ALU.mult, ALU.add))
                    inv_sqrt(nc, link, var[:, 0:1], r[b][:], var[:, 1:2])
                    link.fill()
                    dve.sem_inc(r_done, 1)

            run_steps(dve, TILES, DEPTH, 2, body)

        @block.tensor
        def _(pe):
            def body(k, m):
                s = stage(k, m, 0, 2, TILES)
                s1 = stage(k, m, 1, 2, TILES)
                for c in range(NCH):
                    if s is not None:
                        t, b, _ = s
                        if c == 0 and not first(t, 2):
                            pe.wait_ge(g_done, t - 1)
                        pe.wait_ge(lo_done, 4 * t + c + 1)
                        outs = [ps_h[b][:, 0:HID], ps_h[b][:, HID:2 * HID]]
                        for j in range(KCH):
                            n = KCH * c + j
                            last = three_pass(nc, outs, x_hi[c][:, j, :], x_lo[c][:, j, :],
                                              [w_hi[:, n, 0:HID], w_hi[:, n, HID:2 * HID]],
                                              [w_lo[:, n, 0:HID], w_lo[:, n, HID:2 * HID]], n == 0, n == KIN - 1)
                        last.then_inc(x_used, 1)
                    if c == 0 and s1 is not None:
                        t, b, _ = s1
                        pe.wait_ge(g_done, t + 1)
                        if not first(t, 2):
                            pe.wait_ge(gt_done, t - 1)
                        for j in range(HID // P):
                            last = nc.tensor.transpose(ps_t[b][:, P * j:P * j + P], g[b][:, P * j:P * j + P], ident[:])
                        last.then_inc(t_done, 1)

            run_steps(pe, TILES, DEPTH, 2, body)

        @block.gpsimd
        def _(pool):
            def body(k, m):
                s = stage(k, m, 1, 2, TILES)
                if s is None:
                    return
                t, b, _ = s
                pool.wait_ge(gt_done, t + 1)
                pool.dma_start(d["g_t"][t], gt[b][:]).then_inc(gt_stored[b], 16)

            run_steps(pool, TILES, DEPTH, 2, body)
            for b in range(2):
                pool.wait_ge(gt_stored[b], 16 * TILES // 2)


def tok_down(nc, d, split, ident, qn_hi, qn_lo, k_t):
    W = QR + KR + RO
    with ExitStack() as ctx:
        mem = Memory(nc, ctx, "down")
        w2_hi = mem.sb("w2_hi", [P, 4, DM], F32R)
        w2_lo = mem.sb("w2_lo", [P, 4, DM], F32R)
        wa_hi = mem.sb("wa_hi", [P, KM, W], F32R)
        wa_lo = mem.sb("wa_lo", [P, KM, W], F32R)
        split("w2", d["w2"], w2_hi, w2_lo, 4, DM)
        split("wa", d["wa"], wa_hi, wa_lo, KM, W)
        post = mem.sb("post", [P, DM])
        kvw = mem.sb("kvw", [P, KR])
        g_raw = [mem.sb(f"g_raw{i}", [P, 4, P]) for i in range(2)]
        g_hi = [mem.sb(f"g_hi{i}", [P, 4, P], F32R) for i in range(2)]
        g_lo = [mem.sb(f"g_lo{i}", [P, 4, P], F32R) for i in range(2)]
        junk = mem.sb("junk", [P, DM], BF16)
        junk_a = mem.sb("junk_a", [P, QR + KR], BF16)
        st = [mem.sb(f"st{i}", [P, 4]) for i in range(2)]
        vec = mem.sb("vec", [P, 16])
        bn = mem.sb("bn", [P, 12])
        y = [mem.sb(f"y{i}", [P, DM]) for i in range(2)]
        xn = [mem.sb(f"xn{i}", [P, DM]) for i in range(3)]
        xt_hi = mem.sb("xt_hi", [P, KM, P], F32R)
        xt_lo = mem.sb("xt_lo", [P, KM, P], F32R)
        qk = [mem.sb(f"qk{i}", [P, W]) for i in range(2)]
        ps_y = mem.ps("ps_y", [P, DM])
        ps_x = [mem.ps(f"ps_x{i}", [P, 4, P]) for i in range(2)]
        ps_a = [mem.ps(f"ps_a{i}", [P, 512]) for i in range(2)]
        ps_d = mem.ps("ps_d", [P, 512])
        const_in = mem.sem("const_in")
        g_in = mem.sems("g_in", 2)
        ghi_done = mem.sem("ghi_done")
        glo_done = mem.sem("glo_done")
        y_made = mem.sem("y_made")
        ysq_done = mem.sem("ysq_done")
        y_done = mem.sem("y_done")
        xn_done = mem.sem("xn_done")
        x_turned = mem.sem("x_turned")
        xhi_done = mem.sem("xhi_done")
        xlo_done = mem.sem("xlo_done")
        a_made = mem.sem("a_made")
        asq_done = mem.sem("asq_done")
        qk_done = mem.sem("qk_done")
        qk_turned = mem.sem("qk_turned")
        qhi_done = mem.sem("qhi_done")
        qlo_done = mem.sem("qlo_done")
        y_stored = mem.stored("y_stored", 2)
        link_sem = mem.sem("link")
        block = ctx.enter_context(nc.Block())
        D_Y, D_X, D_A, D_Q = 1, 3, 3, 4
        DEPTH = 4
        U = 6 if TILES % 6 == 0 else 2

        @block.sync
        def _(sp):
            sp.dma_start(post[:], d["post_ln"]).then_inc(const_in, 16)
            sp.dma_start(kvw[:], d["kv_ln"]).then_inc(const_in, 16)

            def body(k, m):
                s = stage(k, m, 0, U, TILES)
                if s is not None:
                    t, u, kb = s
                    if not first(t, 2):
                        sp.wait_ge(glo_done, t - 1)
                    sp.dma_start(g_raw[u % 2][:], d["g_t"][t].rearrange("p (j c) -> p j c", j=4)).then_inc(g_in[u % 2], 16)

            run_steps(sp, TILES, DEPTH, U, body)

        def nth(kb, u):
            return kb * (U // 2) + u // 2 + 1

        @block.gpsimd
        def _(pool):
            def body(k, m):
                s = stage(k, m, D_Y, U, TILES)
                if s is not None:
                    t, u, kb = s
                    pool.wait_ge(y_done, t + 1)
                    pool.dma_start(d["y"][t], y[u % 2][:]).then_inc(y_stored[u % 2], 16)

            run_steps(pool, TILES, DEPTH, U, body)
            for b in range(2):
                pool.wait_ge(y_stored[b], 16 * TILES // 2)

        @block.scalar
        def _(act):
            def body(k, m):
                s = stage(k, m, D_X, U, TILES)
                if s is not None:
                    t, u, kb = s
                    if not first(t, 1):
                        act.wait_ge(a_made, t)
                    for h in range(2):
                        act.wait_ge(x_turned, 2 * t + h + 1)
                        nc.scalar.activation(xt_hi[:, 4 * h:4 * h + 4, :], ps_x[h][:], ACT.Copy).then_inc(xhi_done, 1)
                s = stage(k, m, 0, U, TILES)
                if s is not None:
                    t, u, kb = s
                    act.wait_ge(g_in[u % 2], 16 * nth(kb, u))
                    if not first(t, 2):
                        act.wait_ge(y_made, t - 1)
                    nc.scalar.activation(g_hi[u % 2][:], g_raw[u % 2][:], ACT.Copy).then_inc(ghi_done, 1)
                s = stage(k, m, D_Y, U, TILES)
                if s is not None:
                    t, u, kb = s
                    act.wait_ge(y_made, t + 1)
                    if not first(t, 2):
                        act.wait_ge(xn_done, t - 1)
                    if not first(t, 1):
                        act.wait_ge(ysq_done, t)
                    nc.scalar.activation(junk[:], ps_y[:], ACT.Square, accum_out=st[u % 2][:, 0:1]).then_inc(ysq_done, 1)
                s = stage(k, m, D_A, U, TILES)
                if s is not None:
                    t, u, kb = s
                    act.wait_ge(a_made, t + 1)
                    if not first(t, 2):
                        act.wait_ge(qk_done, t - 1)
                    if not first(t, 1):
                        act.wait_ge(asq_done, t)
                    nc.scalar.activation(junk_a[:, 0:QR], ps_a[u % 2][:, 0:QR], ACT.Square, accum_out=st[u % 2][:, 1:2])
                    nc.scalar.activation(junk_a[:, QR:QR + KR], ps_a[u % 2][:, QR:QR + KR], ACT.Square,
                                         accum_out=st[u % 2][:, 2:3]).then_inc(asq_done, 1)
                s = stage(k, m, D_Q, U, TILES)
                if s is not None:
                    t, u, kb = s
                    act.wait_ge(qk_turned, t + 1)
                    cols = bass.ts(t, P)
                    nc.scalar.activation(qn_hi[:, :, cols], ps_d[:, 0:2 * P].rearrange("p (c n) -> p c n", c=2), ACT.Copy)
                    nc.scalar.activation(k_t[:, cols], ps_d[:, 2 * P:3 * P], ACT.Copy).then_inc(qhi_done, 1)

            run_steps(act, TILES, DEPTH, U, body)

        @block.vector
        def _(dve):
            dve.wait_ge(const_in, 32)
            link = Link(dve, link_sem, 0)
            link.per_step = 1000

            def body(k, m, links):
                step_links = links
                s = stage(k, m, D_X, U, TILES)
                if s is not None:
                    t, u, kb = s
                    for h in range(2):
                        dve.wait_ge(xhi_done, 2 * t + h + 1)
                        nc.vector.tensor_tensor(xt_lo[:, 4 * h:4 * h + 4, :], ps_x[h][:], xt_hi[:, 4 * h:4 * h + 4, :],
                                                ALU.subtract).then_inc(xlo_done, 1)
                s = stage(k, m, 0, U, TILES)
                if s is not None:
                    t, u, kb = s
                    dve.wait_ge(ghi_done, t + 1)
                    nc.vector.tensor_tensor(g_lo[u % 2][:], g_raw[u % 2][:], g_hi[u % 2][:],
                                            ALU.subtract).then_inc(glo_done, 1)
                s = stage(k, m, D_Y, U, TILES)
                if s is not None:
                    t, u, kb = s
                    b = u % 2
                    dve.wait_ge(ysq_done, t + 1)
                    step_links(nc.vector.tensor_scalar(vec[:, 0:1], st[b][:, 0:1], 1.0 / DM, RMS_EPS, ALU.mult, ALU.add))
                    inv_sqrt(nc, step_links, vec[:, 0:1], vec[:, 1:2], vec[:, 2:3])
                    if not first(t, 2):
                        dve.wait_ge(y_stored[b], 16 * nth(kb, u) - 16)
                    ins = nc.vector.scalar_tensor_tensor(y[b][:], ps_y[:], vec[:, 1:2], post[:], ALU.mult, ALU.mult)
                    ins.then_inc(y_done, 1)
                    dve.wait_ge(y_done, t + 1)
                    nc.vector.bn_stats(bn[:, 0:6], y[b][:, 0:512])
                    step_links(nc.vector.bn_stats(bn[:, 6:12], y[b][:, 512:1024]))
                    step_links.settle()
                    step_links(nc.vector.bn_aggr(vec[:, 4:6], bn[:]))
                    step_links(nc.vector.tensor_scalar(vec[:, 6:7], vec[:, 5:6], LN_EPS, None, ALU.add))
                    inv_sqrt(nc, step_links, vec[:, 6:7], vec[:, 7:8], vec[:, 8:9])
                    if not first(t, 3):
                        dve.wait_ge(x_turned, 2 * t - 4)
                    nc.vector.tensor_scalar(xn[u % 3][:], y[b][:], vec[:, 4:5], vec[:, 7:8], ALU.subtract,
                                            ALU.mult).then_inc(xn_done, 1)
                s = stage(k, m, D_A, U, TILES)
                if s is not None:
                    t, u, kb = s
                    b = u % 2
                    dve.wait_ge(asq_done, t + 1)
                    nc.vector.tensor_scalar(vec[:, 9:10], st[b][:, 1:2], 1.0 / QR, RMS_EPS, ALU.mult, ALU.add)
                    step_links(nc.vector.tensor_scalar(vec[:, 10:11], st[b][:, 2:3], 1.0 / KR, RMS_EPS, ALU.mult, ALU.add))
                    inv_sqrt(nc, step_links, vec[:, 9:11], vec[:, 11:13], vec[:, 13:15])
                    if not first(t, 2):
                        dve.wait_ge(qk_turned, t - 1)
                    nc.vector.tensor_scalar(qk[b][:, 0:QR], ps_a[b][:, 0:QR], vec[:, 11:12], None, ALU.mult)
                    nc.vector.scalar_tensor_tensor(qk[b][:, QR:QR + KR], ps_a[b][:, QR:QR + KR], vec[:, 12:13],
                                                   kvw[:], ALU.mult, ALU.mult)
                    nc.vector.tensor_copy(qk[b][:, QR + KR:W], ps_a[b][:, QR + KR:W]).then_inc(qk_done, 1)
                s = stage(k, m, D_Q, U, TILES)
                if s is not None:
                    t, u, kb = s
                    cols = bass.ts(t, P)
                    dve.wait_ge(qhi_done, t + 1)
                    nc.vector.tensor_tensor(qn_lo[:, :, cols], ps_d[:, 0:2 * P].rearrange("p (c n) -> p c n", c=2),
                                            qn_hi[:, :, cols], ALU.subtract).then_inc(qlo_done, 1)

            LINKS = 3 * INV_SQRT_LINKS + 6
            link.per_step = LINKS

            def step(k, m):
                link.step(k * U + m)
                body(k, m, link)
                link.fill()

            run_steps(dve, TILES, DEPTH, U, step)

        @block.tensor
        def _(pe):
            def body(k, m):
                s = stage(k, m, D_X, U, TILES)
                if s is not None:
                    t, u, kb = s
                    pe.wait_ge(xn_done, t + 1)
                    for h in range(2):
                        if not first(t, 1):
                            pe.wait_ge(xlo_done, 2 * t + (h - 1))
                        for j in range(4):
                            n = 4 * h + j
                            last = nc.tensor.transpose(ps_x[h][:, j, :], xn[u % 3][:, P * n:P * n + P], ident[:])
                        last.then_inc(x_turned, 1)
                s = stage(k, m, D_Y, U, TILES)
                if s is not None:
                    t, u, kb = s
                    pe.wait_ge(glo_done, t + 1)
                    if not first(t, 1):
                        pe.wait_ge(y_done, t)
                    outs = [ps_y[:, 0:512], ps_y[:, 512:1024]]
                    for n in range(4):
                        last = three_pass(nc, outs, g_hi[u % 2][:, n, :], g_lo[u % 2][:, n, :],
                                          [w2_hi[:, n, 0:512], w2_hi[:, n, 512:1024]],
                                          [w2_lo[:, n, 0:512], w2_lo[:, n, 512:1024]], n == 0, n == 3)
                    last.then_inc(y_made, 1)
                s = stage(k, m, D_A, U, TILES)
                if s is not None:
                    t, u, kb = s
                    if not first(t, 2):
                        pe.wait_ge(qk_done, t - 1)
                    for n in range(KM):
                        if n % 4 == 0:
                            pe.wait_ge(xlo_done, 2 * t + n // 4 + 1)
                        last = three_pass(nc, [ps_a[u % 2][:, 0:W]], xt_hi[:, n, :], xt_lo[:, n, :],
                                          [wa_hi[:, n, :]], [wa_lo[:, n, :]], n == 0, n == KM - 1)
                    last.then_inc(a_made, 1)
                s = stage(k, m, D_Q, U, TILES)
                if s is not None:
                    t, u, kb = s
                    pe.wait_ge(qk_done, t + 1)
                    if not first(t, 1):
                        pe.wait_ge(qlo_done, t)
                    for j in range(3):
                        last = nc.tensor.transpose(ps_d[:, P * j:P * j + P], qk[u % 2][:, P * j:P * j + P], ident[:])
                    last.then_inc(qk_turned, 1)

            run_steps(pe, TILES, DEPTH, U, body)


def attention(nc, d, ident, qn_hi, qn_lo, k_t):
    with ExitStack() as ctx:
        mem = Memory(nc, ctx, "attn")
        cos = mem.sb("cos", [P, GT])
        sin = mem.sb("sin", [P, GT])
        k_tb = mem.sb("k_tb", [P, TOK])
        v = mem.sb("v", [P, BATCH, KR])
        ident16 = mem.sb("ident16", [P, SEQ], BF16)
        mask = mem.sb("mask", [P, GT], BF16)
        swap = [p ^ 1 for p in range(32)]
        attention_keys(nc, d, ident, k_t, k_tb, v, cos, sin, ident16, mask, swap)

        w_raw = [mem.sb(f"w_raw{i}", [P, 2, 2 * P]) for i in range(2)]
        w_hi = [mem.sb(f"w_hi{i}", [P, 2, 2 * P], F32R) for i in range(2)]
        w_lo = [mem.sb(f"w_lo{i}", [P, 2, 2 * P], F32R) for i in range(2)]
        q_a = [mem.sb(f"q_a{i}", [P, GT]) for i in range(2)]
        q_b = [mem.sb(f"q_b{i}", [P, GT]) for i in range(2)]
        by_cos = mem.sb("by_cos", [P, GT])
        swapped = mem.sb("swapped", [P, GT])
        by_sin = mem.sb("by_sin", [P, GT])
        top = mem.sb("top", [P, 8])
        bias = [mem.sb(f"bias{i}", [P, 8]) for i in range(2)]
        total = [mem.sb(f"total{i}", [P, 8]) for i in range(2)]
        share = [mem.sb(f"share{i}", [P, 8]) for i in range(2)]
        NPR = 4
        prob = [mem.sb(f"prob{i}", [P, 2, GT]) for i in range(NPR)]
        prob_t = [mem.sb(f"prob_t{i}", [P, 2, GT]) for i in range(2)]
        o_t = [mem.sb(f"o_t{i}", [P, GT]) for i in range(2)]
        zero = mem.sb("zero", [P, PAIRS, TOKP - TOK])
        ps_l = mem.ps("ps_l", [P, 512])
        ps_r = mem.ps("ps_r", [P, 512])
        ps_s = mem.ps("ps_s", [P, 2, 512])
        ps_t = mem.ps("ps_t", [P, 2, 512])
        ps_o = mem.ps("ps_o", [P, 512])
        w_in = mem.sems("w_in", 2)
        w_hi_done = mem.sem("w_hi_done")
        w_lo_done = mem.sem("w_lo_done")
        rope_made = mem.sem("rope_made")
        latent_made = mem.sem("latent_made")
        latent_done = mem.sem("latent_done")
        swap_done = mem.sem("swap_done")
        sin_done = mem.sem("sin_done")
        rope_done = mem.sem("rope_done")
        scored = mem.sem("scored")
        top_done = mem.sem("top_done")
        bias_done = mem.sem("bias_done")
        exp_done = mem.sem("exp_done")
        share_done = mem.sem("share_done")
        prob_done = mem.sem("prob_done")
        turned = mem.sem("turned")
        prob_t_done = mem.sem("prob_t_done")
        weighed = mem.sem("weighed")
        o_done = mem.sem("o_done")
        o_stored = mem.stored("o_stored", 2)
        zeroed = mem.sem("zeroed")
        pad_stored = mem.stored("pad_stored", 1)[0]
        block = ctx.enter_context(nc.Block())

        N = PAIRS * GROUPS
        U = 2 * GROUPS
        D_S, D_N, D_T, D_V = 1, 2, 3, 4
        DEPTH = D_V
        PREP = 4

        def weights_of(k, m):
            if m % GROUPS != PREP:
                return None
            return stage(k, m // GROUPS, -1, 2, PAIRS)

        def bodied(n, kb, u, per):
            return kb * (U // per) + u // per + n

        @block.sync
        def _(sp):
            for p in range(2):
                sp.dma_start(w_raw[p][:], d["wq_pair"][p]).then_inc(w_in[p], 16)

            with sp.Fori(1, PAIRS // 2) as k:
                for w in range(2):
                    sp.wait_ge(w_lo_done, 2 * k + w - 1)
                    sp.dma_start(w_raw[w][:], d["wq_pair"][2 * k + w]).then_inc(w_in[w], 16)

        @block.tensor
        def _(pe):
            def body(k, m):
                s = stage(k, m, 0, U, N)
                if s is not None:
                    j, u, kb = s
                    w, g = u // GROUPS, u % GROUPS
                    if g == 0:
                        pe.wait_ge(w_lo_done, 2 * kb + w + 1)
                    cols = slice(GT * g, GT * g + GT)
                    for ps, at, sem, free in ((ps_r, P, rope_made, swap_done), (ps_l, 0, latent_made, latent_done)):
                        if not first(j, 1):
                            pe.wait_ge(free, j)
                        for c in range(2):
                            wh, wl = w_hi[w][:, c, at:at + P], w_lo[w][:, c, at:at + P]
                            nc.tensor.matmul(ps[:, 0:GT], wl, qn_hi[:, c, cols], start=(c == 0), stop=False)
                            nc.tensor.matmul(ps[:, 0:GT], wh, qn_lo[:, c, cols], start=False, stop=False)
                            last = nc.tensor.matmul(ps[:, 0:GT], wh, qn_hi[:, c, cols], start=False, stop=(c == 1))
                        last.then_inc(sem, 1)
                s = stage(k, m, D_S, U, N)
                if s is not None:
                    j, u, kb = s
                    g = u % GROUPS
                    if not first(j, 1):
                        pe.wait_ge(exp_done, j)
                    for h in range(2):
                        nc.tensor.matmul(ps_s[0:SEQ, h, 0:GT], ident16[:], mask[:], start=True, stop=False)
                    pe.wait_ge(latent_done, j + 1)
                    pe.wait_ge(rope_done, j + 1)
                    for h, (q, keys) in enumerate(((q_a[u % 2], k_t), (q_b[u % 2], k_tb))):
                        for b in range(GB):
                            at = GT * g + SEQ * b
                            last = nc.tensor.matmul(ps_s[0:SEQ, h, SEQ * b:SEQ * b + SEQ], q[:, SEQ * b:SEQ * b + SEQ],
                                                    keys[:, at:at + SEQ], start=False, stop=(b == GB - 1))
                    last.then_inc(scored, 1)
                s = stage(k, m, D_T, U, N)
                if s is not None:
                    j, u, kb = s
                    pe.wait_ge(prob_done, j + 1)
                    if not first(j, 1):
                        pe.wait_ge(prob_t_done, j)
                    for h in range(2):
                        for b in range(GB):
                            part = slice(SEQ * b, SEQ * b + SEQ)
                            last = nc.tensor.transpose(ps_t[0:SEQ, h, part], prob[u % NPR][0:SEQ, h, part],
                                                       ident[0:SEQ, 0:SEQ])
                    last.then_inc(turned, 1)
                s = stage(k, m, D_V, U, N)
                if s is not None:
                    j, u, kb = s
                    g = u % GROUPS
                    pe.wait_ge(prob_t_done, j + 1)
                    if not first(j, 1):
                        pe.wait_ge(o_done, j)
                    for b in range(GB):
                        for h in range(2):
                            last = nc.tensor.matmul(ps_o[64 * h:64 * h + 64, SEQ * b:SEQ * b + SEQ],
                                                    v[0:96, GB * g + b, :], prob_t[u % 2][0:96, h, SEQ * b:SEQ * b + SEQ],
                                                    start=True, stop=True)
                    last.then_inc(weighed, 1)

            run_steps(pe, N, DEPTH, U, body)

        @block.scalar
        def _(act):
            for i in range(1):
                act.wait_ge(w_in[0], 16)
                nc.scalar.activation(w_hi[0][:], w_raw[0][:], ACT.Copy).then_inc(w_hi_done, 1)

            def body(k, m):
                s = stage(k, m, 0, U, N)
                if s is not None:
                    j, u, kb = s
                    act.wait_ge(latent_made, j + 1)
                    if not first(j, 2):
                        act.wait_ge(scored, j - 1)
                    nc.scalar.activation(q_a[u % 2][0:64, :], ps_l[0:64, 0:GT], ACT.Copy)
                    nc.scalar.activation(q_b[u % 2][64:P, :], ps_l[64:P, 0:GT], ACT.Copy).then_inc(latent_done, 1)
                    s = weights_of(k, m)
                    if s is not None:
                        p, w, kb = s
                        act.wait_ge(w_in[w], 16 * kb + 16)
                        if not first(p, 2):
                            act.wait_ge(latent_made, GROUPS * (p - 1))
                        nc.scalar.activation(w_hi[w][:], w_raw[w][:], ACT.Copy).then_inc(w_hi_done, 1)
                s = stage(k, m, D_S, U, N)
                if s is not None:
                    j, u, kb = s
                    act.wait_ge(bias_done, j + 1)
                    if not first(j, NPR):
                        act.wait_ge(turned, j - NPR + 1)
                    for h in range(2):
                        for b in range(GB):
                            n = GB * h + b
                            part = slice(SEQ * b, SEQ * b + SEQ)
                            last = nc.scalar.activation(prob[u % NPR][0:SEQ, h, part], ps_s[0:SEQ, h, part], ACT.Exp,
                                                        bias=bias[u % 2][0:SEQ, n:n + 1], scale=SCALE,
                                                        accum_out=total[u % 2][0:SEQ, n:n + 1])
                    last.then_inc(exp_done, 1)
                s = stage(k, m, D_T, U, N)
                if s is not None:
                    j, u, kb = s
                    act.wait_ge(turned, j + 1)
                    if not first(j, 2):
                        act.wait_ge(weighed, j - 1)
                    nc.scalar.activation(prob_t[u % 2][0:SEQ, :, :], ps_t[0:SEQ, :, 0:GT],
                                         ACT.Copy).then_inc(prob_t_done, 1)

            act.wait_ge(zeroed, 3)
            run_steps(act, N, DEPTH, U, body, last=1)

        @block.vector
        def _(dve):
            for i in range(2):
                nc.vector.memset(prob_t[i][64:P], 0.0).then_inc(zeroed, 1)
            nc.vector.memset(zero[:], 0.0).then_inc(zeroed, 1)

            def split(w, p):
                dve.wait_ge(w_hi_done, p + 1)
                nc.vector.tensor_tensor(w_lo[w][:], w_raw[w][:], w_hi[w][:], ALU.subtract).then_inc(w_lo_done, 1)

            split(0, 0)

            def body(k, m):
                s = stage(k, m, 0, U, N)
                if s is not None:
                    j, u, kb = s
                    dve.wait_ge(rope_made, j + 1)
                    if not first(j, 1):
                        dve.wait_ge(sin_done, j)
                        dve.wait_ge(rope_done, j)
                    nc.vector.tensor_tensor(by_cos[:], ps_r[:, 0:GT], cos[:], ALU.mult)
                    nc.vector.stream_shuffle(swapped[:], ps_r[:, 0:GT], swap).then_inc(swap_done, 1)
                s = stage(k, m, D_S, U, N)
                if s is not None:
                    j, u, kb = s
                    dve.wait_ge(scored, j + 1)
                    nc.vector.tensor_reduce(top[0:SEQ, :].rearrange("p (h b) -> p h b", h=2),
                                            ps_s[0:SEQ, :, 0:GT].rearrange("p h (b k) -> p h b k", b=GB), AX.X,
                                            ALU.max).then_inc(top_done, 1)
                    dve.wait_ge(top_done, j + 1)
                    if not first(j, 2):
                        dve.wait_ge(exp_done, j - 1)
                    nc.vector.tensor_scalar(bias[u % 2][0:SEQ, :], top[0:SEQ, :], -SCALE, None,
                                            ALU.mult).then_inc(bias_done, 1)
                s = stage(k, m, 0, U, N)
                if s is not None:
                    j, u, kb = s
                    dve.wait_ge(sin_done, j + 1)
                    if not first(j, 2):
                        dve.wait_ge(scored, j - 1)
                    nc.vector.tensor_tensor(q_b[u % 2][0:64, :], by_cos[0:64, :], by_sin[0:64, :], ALU.add)
                    nc.vector.tensor_tensor(q_a[u % 2][64:P, :], by_cos[64:P, :], by_sin[64:P, :],
                                            ALU.add).then_inc(rope_done, 1)
                    s = weights_of(k, m)
                    if s is not None:
                        p, w, kb = s
                        split(w, p)
                s = stage(k, m, D_N, U, N)
                if s is not None:
                    j, u, kb = s
                    dve.wait_ge(exp_done, j + 1)
                    if not first(j, 2):
                        dve.wait_ge(prob_done, j - 1)
                    nc.vector.reciprocal(share[u % 2][0:SEQ, :], total[u % 2][0:SEQ, :]).then_inc(share_done, 1)
                s = stage(k, m, D_V, U, N)
                if s is not None:
                    j, u, kb = s
                    dve.wait_ge(weighed, j + 1)
                    if not first(j, 2):
                        dve.wait_ge(o_stored[u % 2], 16 * bodied(0, kb, u, 2))
                    nc.vector.tensor_copy(o_t[u % 2][:], ps_o[:, 0:GT]).then_inc(o_done, 1)

            run_steps(dve, N, DEPTH, U, body, last=1)

        @block.gpsimd
        def _(pool):
            pool.wait_ge(zeroed, 3)
            pool.dma_start(d["o_t"][:, :, TOK:TOKP], zero[:]).then_inc(pad_stored, 16)

            def body(k, m):
                s = stage(k, m, 0, U, N)
                if s is not None:
                    j, u, kb = s
                    pool.wait_ge(swap_done, j + 1)
                    if not first(j, 1):
                        pool.wait_ge(rope_done, j)
                    nc.gpsimd.tensor_tensor(by_sin[:], swapped[:], sin[:], ALU.mult).then_inc(sin_done, 1)
                s = stage(k, m, D_N, U, N)
                if s is not None:
                    j, u, kb = s
                    pool.wait_ge(share_done, j + 1)
                    p4 = prob[u % NPR][0:SEQ, :, :].rearrange("p h (b k) -> p (h b) k", b=GB)
                    nc.gpsimd.tensor_tensor(p4, p4, share[u % 2][0:SEQ, :].unsqueeze(2).broadcast_to((SEQ, 8, SEQ)),
                                            ALU.mult).then_inc(prob_done, 1)
                s = stage(k, m, D_V, U, N)
                if s is not None:
                    j, u, kb = s
                    g = u % GROUPS
                    pair = 2 * kb + u // GROUPS
                    pool.wait_ge(o_done, j + 1)
                    pool.dma_start(d["o_t"][:, pair, GT * g:GT * g + GT], o_t[u % 2][:]).then_inc(o_stored[u % 2], 16)

            run_steps(pool, N, DEPTH, U, body)
            pool.wait_ge(pad_stored, 16)
            for b in range(2):
                pool.wait_ge(o_stored[b], 16 * N // 2)


def attention_keys(nc, d, ident, k_t, k_tb, v, cos, sin, ident16, mask, swap):
    with ExitStack() as ctx:
        mem = Memory(nc, ctx, "keys")
        by_cos = mem.sb("by_cos", [P, TOK])
        swapped = mem.sb("swapped", [P, TOK])
        ps_v = [mem.ps(f"ps_v{i}", [P, 8, KR]) for i in range(4)]
        const_in = mem.sem("const_in")
        link_sem = mem.sem("link")
        v_made = mem.sem("v_made")
        v_zero = mem.sem("v_zero")
        done = mem.sem("done")
        block = ctx.enter_context(nc.Block())
        R = slice(64, P)

        @block.sync
        def _(sp):
            sp.dma_start(cos[:], d["cos"]).then_inc(const_in, 16)
            sp.dma_start(sin[:], d["sin"]).then_inc(const_in, 16)
            sp.dma_start(ident16[:], d["ident16"]).then_inc(const_in, 16)
            sp.dma_start(mask[:], d["mask"]).then_inc(const_in, 16)
            sp.wait_ge(const_in, 64)

        @block.vector
        def _(dve):
            link = Link(dve, link_sem, 0)
            nc.vector.memset(v[64:P], 0.0).then_inc(v_zero, 1)
            dve.wait_ge(const_in, 64)

            def over(x):
                return x.rearrange("p (g n) -> p g n", g=GROUPS)

            def table(x):
                return x.unsqueeze(1).broadcast_to((64, GROUPS, GT))

            link(nc.vector.stream_shuffle(swapped[R, :], k_t[R, 0:TOK], swap))
            link(nc.vector.tensor_tensor(over(swapped[R, :]), over(swapped[R, :]), table(sin[R, :]), ALU.mult))
            link(nc.vector.tensor_tensor(over(by_cos[R, :]), over(k_t[R, 0:TOK]), table(cos[R, :]), ALU.mult))
            nc.vector.tensor_tensor(k_t[R, 0:TOK], by_cos[R, :], swapped[R, :], ALU.add)
            nc.vector.tensor_tensor(k_tb[0:64, :], by_cos[R, :], swapped[R, :], ALU.add).then_inc(done, 1)

        @block.tensor
        def _(pe):
            for b in range(BATCH):
                last = nc.tensor.transpose(ps_v[b // 8][0:SEQ, b % 8, :], k_t[0:KR, SEQ * b:SEQ * b + SEQ],
                                           ident[0:KR, 0:KR])
            last.then_inc(v_made, 1)

        @block.scalar
        def _(act):
            nc.scalar.activation(k_tb[R, :], k_t[0:64, 0:TOK], ACT.Copy).then_inc(done, 1)
            act.wait_ge(v_made, 1)
            act.wait_ge(v_zero, 1)
            for i in range(4):
                nc.scalar.activation(v[0:SEQ, 8 * i:8 * i + 8, :], ps_v[i][0:SEQ], ACT.Copy).then_inc(done, 1)


def attn_out(nc, d, split, ident):
    CH = 4
    NC = PAIRS // CH
    with ExitStack() as ctx:
        mem = Memory(nc, ctx, "out")
        w_hi = mem.sb("w_hi", [P, PAIRS, DM], F32R)
        w_lo = mem.sb("w_lo", [P, PAIRS, DM], F32R)
        split("wvo", d["wvo"], w_hi, w_lo, PAIRS, DM)
        raw = [mem.sb(f"raw{c}", [P, CH, P]) for c in range(NC)]
        x_hi = [mem.sb(f"x_hi{c}", [P, CH, P], F32R) for c in range(NC)]
        x_lo = [mem.sb(f"x_lo{c}", [P, CH, P], F32R) for c in range(NC)]
        y = [mem.sb(f"y{i}", [P, DM]) for i in range(2)]
        h = [mem.sb(f"h{i}", [P, DM]) for i in range(2)]
        ps_h = [mem.ps(f"ps_h{i}", [P, DM]) for i in range(2)]
        raw_in = mem.sems("raw_in", NC)
        y_in = mem.sems("y_in", 2)
        hi_done = mem.sem("hi_done")
        lo_done = mem.sem("lo_done")
        x_used = mem.sem("x_used")
        h_done = mem.sem("h_done")
        h_stored = mem.stored("h_stored", 2)
        block = ctx.enter_context(nc.Block())
        DEPTH = 1

        @block.sync
        def _(sp):
            def body(k, m):
                s = stage(k, m, 0, 2, TILES)
                if s is None:
                    return
                t, b, kb = s
                for c in range(NC):
                    if not first(t, 1):
                        sp.wait_ge(lo_done, NC * t + (c - NC + 1))
                    sp.dma_start(raw[c][:], d["o_t"][:, CH * c:CH * c + CH, bass.ts(t, P)]).then_inc(raw_in[c], 16)
                if not first(t, 2):
                    sp.wait_ge(h_done, t - 1)
                sp.dma_start(y[b][:], d["y"][t]).then_inc(y_in[b], 16)

            run_steps(sp, TILES, DEPTH, 2, body)

        @block.scalar
        def _(act):
            def body(k, m):
                s = stage(k, m, 0, 2, TILES)
                if s is None:
                    return
                t, b, kb = s
                for c in range(NC):
                    act.wait_ge(raw_in[c], 16 * t + 16)
                    if not first(t, 1):
                        act.wait_ge(x_used, NC * t + (c - NC + 1))
                    nc.scalar.activation(x_hi[c][:], raw[c][:], ACT.Copy).then_inc(hi_done, 1)

            run_steps(act, TILES, DEPTH, 2, body)

        @block.vector
        def _(dve):
            def body(k, m):
                s = stage(k, m, 0, 2, TILES)
                if s is not None:
                    t, b, kb = s
                    for c in range(NC):
                        dve.wait_ge(hi_done, NC * t + c + 1)
                        nc.vector.tensor_tensor(x_lo[c][:], raw[c][:], x_hi[c][:], ALU.subtract).then_inc(lo_done, 1)
                s = stage(k, m, 1, 2, TILES)
                if s is not None:
                    t, b, kb = s
                    dve.wait_ge(x_used, NC * t + NC)
                    dve.wait_ge(y_in[b], 16 * kb + 16)
                    if not first(t, 2):
                        dve.wait_ge(h_stored[b], 16 * kb)
                    nc.vector.tensor_tensor(h[b][:], ps_h[b][:], y[b][:], ALU.add).then_inc(h_done, 1)

            run_steps(dve, TILES, DEPTH, 2, body)

        @block.tensor
        def _(pe):
            def body(k, m):
                s = stage(k, m, 0, 2, TILES)
                if s is None:
                    return
                t, b, kb = s
                outs = [ps_h[b][:, 0:512], ps_h[b][:, 512:1024]]
                if not first(t, 2):
                    pe.wait_ge(h_done, t - 1)
                for c in range(NC):
                    pe.wait_ge(lo_done, NC * t + c + 1)
                    for j in range(CH):
                        n = CH * c + j
                        last = three_pass(nc, outs, x_hi[c][:, j, :], x_lo[c][:, j, :],
                                          [w_hi[:, n, 0:512], w_hi[:, n, 512:1024]],
                                          [w_lo[:, n, 0:512], w_lo[:, n, 512:1024]], n == 0, n == PAIRS - 1)
                    last.then_inc(x_used, 1)

            run_steps(pe, TILES, DEPTH, 2, body)

        @block.gpsimd
        def _(pool):
            def body(k, m):
                s = stage(k, m, 1, 2, TILES)
                if s is None:
                    return
                t, b, kb = s
                pool.wait_ge(h_done, t + 1)
                pool.dma_start(d["h"][t], h[b][:]).then_inc(h_stored[b], 16)

            run_steps(pool, TILES, DEPTH, 2, body)
            for b in range(2):
                pool.wait_ge(h_stored[b], 16 * TILES // 2)


ER = EXP * RANK
FW = DM + ER + NR + 1
CUT = [0, 390, 780, FW]
A_AT = DM - CUT[2]
R_AT = A_AT + ER


def ffn(nc, d, split, ident):
    with ExitStack() as ctx:
        mem = Memory(nc, ctx, "ffn")
        w_hi = mem.sb("w_hi", [P, KM, FW], F32R)
        w_lo = mem.sb("w_lo", [P, KM, FW], F32R)
        b_hi = mem.sb("b_hi", [P, 1, DM], F32R)
        b_lo = mem.sb("b_lo", [P, 1, DM], F32R)
        split("wf", d["wf"], w_hi, w_lo, KM, FW)
        split("wb", d["lora_b"], b_hi, b_lo, 1, DM)
        bias = mem.sb("bias", [P, DM])
        rbias = mem.sb("rbias", [P, NR])
        lower = mem.sb("lower", [P, NR, NR])
        numbers = mem.sb("numbers", [P, EXP, NR])
        emap = mem.sb("emap", [P, NR], I32)
        emapf = mem.sb("emapf", [P, NR])
        place = mem.sb("place", [P, EXP, NR])
        h = [mem.sb(f"h{i}", [P, DM]) for i in range(3)]
        res = [mem.sb(f"res{i}", [P, DM]) for i in range(3)]
        o = [mem.sb(f"o{i}", [P, DM]) for i in range(2)]
        xn = [mem.sb(f"xn{i}", [P, DM]) for i in range(2)]
        xt_hi = [mem.sb(f"xt_hi{i}", [P, KM, P], F32R) for i in range(2)]
        xt_lo = [mem.sb(f"xt_lo{i}", [P, KM, P], F32R) for i in range(2)]
        bn = mem.sb("bn", [P, 12])
        vec = mem.sb("vec", [P, 16])
        lg = mem.sb("lg", [P, NR])
        ex = mem.sb("ex", [P, NR])
        pr = mem.sb("pr", [P, NR])
        over = mem.sb("over", [P, NR, NR])
        tie = mem.sb("tie", [P, NR, NR])
        rank = mem.sb("rank", [P, NR])
        kept = mem.sb("kept", [P, NR])
        pick = mem.sb("pick", [P, EXP, NR])
        we = mem.sb("we", [P, EXP])
        hw = mem.sb("hw", [P, ER])
        ht_hi = mem.sb("ht_hi", [P, P], F32R)
        ht_lo = mem.sb("ht_lo", [P, P], F32R)
        ps_o = [[mem.ps(f"ps_o{i}_{c}", [P, 512]) for c in range(3)] for i in range(2)]
        ps_x = [mem.ps(f"ps_x{i}", [P, 4, P]) for i in range(2)]
        const_in = mem.sem("const_in")
        h_in = mem.sems("h_in", 3)
        xn_done = mem.sem("xn_done")
        x_turned = mem.sem("x_turned")
        xhi_done = mem.sem("xhi_done")
        xlo_done = mem.sem("xlo_done")
        base_made = mem.sem("base_made")
        logits_done = mem.sem("logits_done")
        exp_done = mem.sem("exp_done")
        hw_done = mem.sem("hw_done")
        hw_turned = mem.sem("hw_turned")
        hhi_done = mem.sem("hhi_done")
        hlo_done = mem.sem("hlo_done")
        lora_made = mem.sem("lora_made")
        res_done = mem.sem("res_done")
        o_done = mem.sem("o_done")
        o_stored = mem.stored("o_stored", 2)
        link_sem = mem.sem("link")
        block = ctx.enter_context(nc.Block())
        D_X, D_M, D_L = 1, 2, 3
        DEPTH = 4
        U = 6

        def nth(kb, u, per):
            return kb * (U // per) + u // per + 1

        @block.sync
        def _(sp):
            for dst, name in ((bias, "base_b"), (rbias, "router_b"), (lower, "lower"), (numbers, "numbers"),
                              (emap, "emap")):
                sp.dma_start(dst[:], d[name]).then_inc(const_in, 16)

            def body(k, m):
                s = stage(k, m, 0, U, TILES)
                if s is None:
                    return
                t, u, kb = s
                if not first(t, 3):
                    sp.wait_ge(res_done, t - 2)
                    sp.wait_ge(xn_done, t - 2)
                sp.dma_start(h[u % 3][:], d["h"][t]).then_inc(h_in[u % 3], 16)

            run_steps(sp, TILES, DEPTH, U, body)

        @block.gpsimd
        def _(pool):
            pool.wait_ge(const_in, 80)

            def body(k, m):
                s = stage(k, m, 0, U, TILES)
                if s is not None:
                    t, u, kb = s
                    pool.wait_ge(h_in[u % 3], 16 * nth(kb, u, 3))
                    if not first(t, 3):
                        pool.wait_ge(o_done, t - 2)
                    nc.gpsimd.tensor_tensor(res[u % 3][:], h[u % 3][:], bias[:], ALU.add).then_inc(res_done, 1)
                s = stage(k, m, D_L + 1, U, TILES)
                if s is not None:
                    t, u, kb = s
                    pool.wait_ge(o_done, t + 1)
                    pool.dma_start(d["out"][t], o[u % 2][:]).then_inc(o_stored[u % 2], 16)

            run_steps(pool, TILES, DEPTH, U, body)
            for b in range(2):
                pool.wait_ge(o_stored[b], 16 * TILES // 2)

        @block.scalar
        def _(act):
            def body(k, m):
                s = stage(k, m, D_L, U, TILES)
                if s is not None:
                    t, u, kb = s
                    act.wait_ge(logits_done, t + 1)
                    nc.scalar.activation(ex[:], lg[:], ACT.Exp, bias=vec[:, 4:5],
                                         accum_out=vec[:, 5:6]).then_inc(exp_done, 1)
                    act.wait_ge(hw_turned, t + 1)
                    if not first(t, 1):
                        act.wait_ge(lora_made, t)
                    nc.scalar.activation(ht_hi[:], ps_x[0][:, 0, :], ACT.Copy).then_inc(hhi_done, 1)
                s = stage(k, m, D_X, U, TILES)
                if s is not None:
                    t, u, kb = s
                    if not first(t, 2):
                        act.wait_ge(base_made, t - 1)
                    for c in range(2):
                        act.wait_ge(x_turned, 2 * t + c + 1)
                        nc.scalar.activation(xt_hi[u % 2][:, 4 * c:4 * c + 4, :], ps_x[c][:],
                                             ACT.Copy).then_inc(xhi_done, 1)

            run_steps(act, TILES, DEPTH, U, body)

        @block.vector
        def _(dve):
            link = Link(dve, link_sem, 0)
            PER = INV_SQRT_LINKS + 4 + 11
            link.per_step = PER
            dve.wait_ge(const_in, 80)
            link.step(0)
            link(nc.vector.tensor_copy(emapf[:], emap[:]))
            link(nc.vector.tensor_tensor(place[:], emapf[:].unsqueeze(1).broadcast_to((P, EXP, NR)), numbers[:],
                                         ALU.is_equal))
            link(nc.vector.tensor_scalar(place[:], place[:], 2.0, None, ALU.mult))
            START = link.n

            def body(k, m):
                s = stage(k, m, D_L, U, TILES)
                if s is not None:
                    t, u, kb = s
                    ps = ps_o[u % 2][2]
                    dve.wait_ge(base_made, t + 1)
                    link(nc.vector.tensor_tensor(lg[:], ps[:, R_AT:R_AT + NR], rbias[:], ALU.add))
                    link(nc.vector.tensor_reduce(vec[:, 3:4], lg[:], AX.X, ALU.max))
                    nc.vector.tensor_scalar(vec[:, 4:5], vec[:, 3:4], -1.0, None, ALU.mult).then_inc(logits_done, 1)
                    dve.wait_ge(exp_done, t + 1)
                    link(nc.vector.reciprocal(vec[:, 6:7], vec[:, 5:6]))
                    link(nc.vector.tensor_scalar(pr[:], ex[:], vec[:, 6:7], None, ALU.mult))
                    pj = pr[:].unsqueeze(1).broadcast_to((P, NR, NR))
                    pi = pr[:].unsqueeze(2).broadcast_to((P, NR, NR))
                    nc.vector.tensor_tensor(over[:], pj, pi, ALU.is_gt)
                    link(nc.vector.tensor_tensor(tie[:], pj, pi, ALU.is_equal))
                    link(nc.vector.tensor_tensor(tie[:], tie[:], lower[:], ALU.mult))
                    link(nc.vector.tensor_tensor(over[:], over[:], tie[:], ALU.add))
                    link(nc.vector.tensor_reduce(rank[:], over[:], AX.X, ALU.add))
                    link(nc.vector.scalar_tensor_tensor(kept[:], rank[:], float(EXP) - 0.5, pr[:], ALU.is_lt, ALU.mult))
                    link(nc.vector.tensor_tensor(pick[:], kept[:].unsqueeze(1).broadcast_to((P, EXP, NR)), place[:],
                                                 ALU.mult))
                    if not first(t, 1):
                        dve.wait_ge(hw_turned, t)
                    nc.vector.tensor_reduce(we[:], pick[:], AX.X, ALU.add).then_inc(link_sem, 1)
                    link.n += 1
                    dve.wait_ge(link_sem, link.base + link.n)
                    nc.vector.tensor_tensor(hw[:].rearrange("p (e r) -> p e r", e=EXP),
                                            ps[:, A_AT:A_AT + ER].rearrange("p (e r) -> p e r", e=EXP),
                                            we[:].unsqueeze(2).broadcast_to((P, EXP, RANK)), ALU.mult).then_inc(hw_done, 1)
                s = stage(k, m, 0, U, TILES)
                if s is not None:
                    t, u, kb = s
                    hh = h[u % 3]
                    dve.wait_ge(h_in[u % 3], 16 * nth(kb, u, 3))
                    nc.vector.bn_stats(bn[:, 0:6], hh[:, 0:512])
                    link(nc.vector.bn_stats(bn[:, 6:12], hh[:, 512:1024]))
                    link.settle()
                    link(nc.vector.bn_aggr(vec[:, 8:10], bn[:]))
                    link(nc.vector.tensor_scalar(vec[:, 10:11], vec[:, 9:10], LN_EPS, None, ALU.add))
                    inv_sqrt(nc, link, vec[:, 10:11], vec[:, 11:12], vec[:, 12:13])
                    if not first(t, 2):
                        dve.wait_ge(x_turned, 2 * t - 2)
                    nc.vector.tensor_scalar(xn[u % 2][:], hh[:], vec[:, 8:9], vec[:, 11:12], ALU.subtract,
                                            ALU.mult).then_inc(xn_done, 1)
                s = stage(k, m, D_L, U, TILES)
                if s is not None:
                    t, u, kb = s
                    dve.wait_ge(hhi_done, t + 1)
                    nc.vector.tensor_tensor(ht_lo[:], ps_x[0][:, 0, :], ht_hi[:], ALU.subtract).then_inc(hlo_done, 1)
                    dve.wait_ge(lora_made, t + 1)
                    dve.wait_ge(res_done, t + 1)
                    if not first(t, 2):
                        dve.wait_ge(o_stored[u % 2], 16 * nth(kb, u, 2) - 16)
                    for c in range(3):
                        a, e = CUT[c], min(CUT[c + 1], DM)
                        last = nc.vector.tensor_tensor(o[u % 2][:, a:e], ps_o[u % 2][c][:, 0:e - a],
                                                       res[u % 3][:, a:e], ALU.add)
                    last.then_inc(o_done, 1)
                s = stage(k, m, D_X, U, TILES)
                if s is not None:
                    t, u, kb = s
                    for c in range(2):
                        dve.wait_ge(xhi_done, 2 * t + c + 1)
                        nc.vector.tensor_tensor(xt_lo[u % 2][:, 4 * c:4 * c + 4, :], ps_x[c][:],
                                                xt_hi[u % 2][:, 4 * c:4 * c + 4, :], ALU.subtract).then_inc(xlo_done, 1)

            def step(k, m):
                link.step(k * U + m)
                link.base = link.base + START
                body(k, m)
                link.fill()

            run_steps(dve, TILES, DEPTH, U, step)

        @block.tensor
        def _(pe):
            def base(s, half):
                t, u, kb = s
                for n in range(4 * half, 4 * half + 4):
                    if n % 4 == 0:
                        pe.wait_ge(xlo_done, 2 * t + half + 1)
                    last = three_pass(nc, [ps_o[u % 2][c][:, 0:CUT[c + 1] - CUT[c]] for c in range(3)],
                                      xt_hi[u % 2][:, n, :], xt_lo[u % 2][:, n, :],
                                      [w_hi[:, n, CUT[c]:CUT[c + 1]] for c in range(3)],
                                      [w_lo[:, n, CUT[c]:CUT[c + 1]] for c in range(3)], n == 0, n == KM - 1)
                if half:
                    last.then_inc(base_made, 1)

            def body(k, m):
                s = stage(k, m, D_M, U, TILES)
                if s is not None:
                    if not first(s[0], 2):
                        pe.wait_ge(o_done, s[0] - 1)
                    base(s, 0)
                sl = stage(k, m, D_L, U, TILES)
                if sl is not None:
                    t, u, kb = sl
                    pe.wait_ge(hw_done, t + 1)
                    if isinstance(t, int):
                        pe.wait_ge(xlo_done, min(2 * t + 4, 2 * TILES))
                    else:
                        pe.wait_ge(xlo_done, 2 * t + 4)
                    nc.tensor.transpose(ps_x[0][:, 0, :], hw[:], ident[:]).then_inc(hw_turned, 1)
                if s is not None:
                    base(s, 1)
                if sl is not None:
                    t, u, kb = sl
                    pe.wait_ge(hlo_done, t + 1)
                    ends = [(CUT[c], min(CUT[c + 1], DM)) for c in range(3)]
                    last = three_pass(nc, [ps_o[u % 2][c][:, 0:e - a] for c, (a, e) in enumerate(ends)], ht_hi[:],
                                      ht_lo[:], [b_hi[:, 0, a:e] for a, e in ends], [b_lo[:, 0, a:e] for a, e in ends],
                                      False, True, onto=True)
                    last.then_inc(lora_made, 1)
                s = stage(k, m, D_X, U, TILES)
                if s is not None:
                    t, u, kb = s
                    pe.wait_ge(xn_done, t + 1)
                    if sl is not None:
                        pe.wait_ge(hlo_done, sl[0] + 1)
                    for c in range(2):
                        if not first(t, 1):
                            pe.wait_ge(xlo_done, 2 * t + (c - 1))
                        for j in range(4):
                            n = 4 * c + j
                            last = nc.tensor.transpose(ps_x[c][:, j, :], xn[u % 2][:, P * n:P * n + P], ident[:])
                        last.then_inc(x_turned, 1)

            run_steps(pe, TILES, DEPTH, U, body)


def build(nc, d):
    with ExitStack() as ctx:
        Memory.whole = ctx
        mem = Memory(nc, ctx, "all")
        ident = mem.sb("ident", [P, P])
        ident_in = mem.sem("ident_in")
        with nc.Block() as block:
            @block.sync
            def _(sp):
                sp.dma_start(ident[:], d["ident"]).then_inc(ident_in, 16)
                sp.wait_ge(ident_in, 16)
        split = Splitter(nc)
        fold_weights(nc, d, ident)
        tok_up(nc, d, split, ident)
        with ExitStack() as kept:
            mem = Memory(nc, kept, "kept")
            qn_hi = mem.sb("qn_hi", [P, 2, TOKP], F32R)
            qn_lo = mem.sb("qn_lo", [P, 2, TOKP], F32R)
            k_t = mem.sb("k_t", [P, TOKP])
            tok_down(nc, d, split, ident, qn_hi, qn_lo, k_t)
            attention(nc, d, ident, qn_hi, qn_lo, k_t)
        attn_out(nc, d, split, ident)
        ffn(nc, d, split, ident)


def rope_tables():
    dim, base, factor, orig = RO, 10000.0, 128.0, 2048

    def corr(rot):
        return dim * math.log(orig / (rot * 2 * math.pi)) / (2 * math.log(base))

    low, high = max(math.floor(corr(32.0)), 0), min(math.ceil(corr(1.0)), dim - 1)
    hi = high + 0.001 if low == high else float(high)
    ramp = np.clip((np.arange(dim // 2, dtype=np.float32) - low) / (hi - low), 0.0, 1.0)
    keep = 1.0 - ramp
    extra = 1.0 / base ** (np.arange(0, dim, 2, dtype=np.float32) / dim)
    freq = extra / factor * (1.0 - keep) + extra * keep
    angle = np.outer(np.arange(512, dtype=np.float32), freq)[:SEQ]
    row = np.arange(P) % RO
    cos = np.cos(angle)[:, row // 2].T
    sin = np.sin(angle)[:, row // 2].T * np.where(row % 2 == 0, -1.0, 1.0)[:, None]
    return (np.ascontiguousarray(np.tile(cos, (1, GB)), dtype=np.float32),
            np.ascontiguousarray(np.tile(sin, (1, GB)), dtype=np.float32))


def blocks(w):
    return w.reshape(-1, P, w.shape[1]).transpose(1, 0, 2)


def kernel(x, L0_tok_w1, L0_tok_w2, L0_tok_ln_pre_w, L0_tok_ln_post_w, L0_attn_wq_a, L0_attn_q_a_ln_w,
           L0_attn_wq_b, L0_attn_wkv_a, L0_attn_kv_a_ln_w, L0_attn_wkv_b, L0_attn_wo, L0_ffn_base_W,
           L0_ffn_base_b, L0_ffn_router_W, L0_ffn_router_b, L0_ffn_A, L0_ffn_B, L0_ffn_expert_map):
    import ml_dtypes
    import concourse.bacc as bacc
    from concourse.bass_utils import run_bass_kernel_spmd

    f32 = np.float32
    rows = np.zeros((BATCH, SEQ * 8, 320), f32)
    rows[:, :750] = np.asarray(x)
    flat = np.zeros((TOKP, DIN), f32)
    flat[:TOK] = rows.reshape(TOK, DIN)
    x_rows = flat.reshape(TILES, P, DIN)
    x_t = x_rows.reshape(TILES, P, KIN, P).transpose(0, 3, 2, 1)

    wq_b = np.asarray(L0_attn_wq_b).reshape(PAIRS, 2, NOPE + RO, QR)
    wkv_b = np.asarray(L0_attn_wkv_b).reshape(PAIRS, 2, NOPE + VD, KR)
    wq_rope = wq_b[:, ::-1, NOPE:, :]
    wq_rope = wq_rope.reshape(PAIRS, 2 * RO, 2, P).transpose(0, 3, 2, 1)
    wo = np.asarray(L0_attn_wo).T.reshape(PAIRS, 2, VD, DM).transpose(0, 2, 1, 3)
    wf = np.zeros((DM, FW), f32)
    wf[:, :DM] = np.asarray(L0_ffn_base_W).T
    wf[:, DM:DM + ER] = np.asarray(L0_ffn_A).reshape(ER, DM).T
    wf[:, DM + ER:DM + ER + NR] = np.asarray(L0_ffn_router_W).T
    cos, sin = rope_tables()
    q, key = np.arange(SEQ)[:, None], np.arange(SEQ)[None, :]
    mask = np.zeros((P, GT), f32)
    mask[:SEQ] = np.tile(np.where(key <= q, 0.0, MASKED), (1, GB))
    ident16 = np.eye(P, SEQ, dtype=f32)
    i, j = np.arange(NR)[:, None], np.arange(NR)[None, :]

    def on_all(a):
        return np.broadcast_to(np.asarray(a)[None], (P, *np.asarray(a).shape))

    arrays = {
        "x_rows": x_rows,
        "x_t": x_t,
        "w1": blocks(np.asarray(L0_tok_w1).T),
        "pre_ln": np.asarray(L0_tok_ln_pre_w).reshape(KIN, P).T,
        "w2": blocks(np.asarray(L0_tok_w2).T),
        "post_ln": on_all(L0_tok_ln_post_w),
        "wa": blocks(np.concatenate([np.asarray(L0_attn_wq_a).T, np.asarray(L0_attn_wkv_a).T], axis=1)),
        "q_ln": np.asarray(L0_attn_q_a_ln_w).reshape(2, P).T,
        "kv_ln": on_all(L0_attn_kv_a_ln_w),
        "wq_nope": wq_b[:, :, :NOPE].reshape(PAIRS, P, QR),
        "wq_rope": wq_rope,
        "wk": wkv_b[:, :, :NOPE].reshape(PAIRS, P, KR),
        "wv": wkv_b[:, :, NOPE:].transpose(0, 2, 1, 3),
        "wo": wo,
        "wf": blocks(wf),
        "lora_b": np.asarray(L0_ffn_B).transpose(0, 2, 1).reshape(P, 1, DM),
        "base_b": on_all(L0_ffn_base_b),
        "router_b": on_all(L0_ffn_router_b),
        "emap": on_all(np.asarray(L0_ffn_expert_map)),
        "cos": cos,
        "sin": sin,
        "mask": mask.astype(ml_dtypes.bfloat16),
        "ident16": ident16.astype(ml_dtypes.bfloat16),
        "ident": np.eye(P, dtype=f32),
        "lower": on_all((j < i).astype(f32)),
        "numbers": on_all(np.tile(np.arange(EXP, dtype=f32)[:, None], (1, NR))),
    }
    arrays = {n: np.ascontiguousarray(a) for n, a in arrays.items()}
    nc = bacc.Bacc("TRN2", target_bir_lowering=False, num_devices=1)
    d = {n: nc.dram_tensor(n, a.shape, mybir.dt.from_np(a.dtype), kind="ExternalInput").ap()
         for n, a in arrays.items()}
    for n, shape in (("wq_pair", (PAIRS, P, 2, 2 * P)), ("wvo", (P, PAIRS, DM)), ("g_t", (TILES, P, HID)),
                     ("y", (TILES, P, DM)), ("o_t", (P, PAIRS, TOKP)), ("h", (TILES, P, DM))):
        d[n] = nc.dram_tensor(n, shape, F32, kind="Internal").ap()
    d["out"] = nc.dram_tensor("out", (TILES, P, DM), F32, kind="ExternalOutput").ap()
    build(nc, d)
    r = run_bass_kernel_spmd(nc, [arrays], core_ids=[0])
    return r.results[0]["out"].reshape(TOKP, DM)[:TOK].reshape(BATCH, SEQ, DM)
```

```python
import math
from contextlib import ExitStack

import numpy as np

import concourse.bass as bass
from concourse import mybir

F32 = mybir.dt.float32
F32R = mybir.dt.float32r
BF16 = mybir.dt.bfloat16
I32 = mybir.dt.int32
ALU = mybir.AluOpType
ACT = mybir.ActivationFunctionType
AX = mybir.AxisListType

P = 128
BATCH, SEQ = 32, 94
TOK = BATCH * SEQ
TILES = -(-TOK // P)
TOKP = TILES * P
DIN = 2560
KIN = DIN // P
HID = 512
DM = 1024
KM = DM // P
QR, KR, RO = 256, 64, 64
NH = 32
PAIRS = NH // 2
NOPE, VD = 64, 128
GROUPS, GB = 8, 4
GT = GB * SEQ
EXP, RANK = 8, 16
NR = 2 * EXP - 1
RMS_EPS, LN_EPS = 1e-6, 1e-5
SCALE = float((NOPE + RO) ** -0.5 * (0.1 * math.log(128.0) + 1.0) ** 2)
KCH = 5
NCH = KIN // KCH
MASKED = -1.0e30


def stage(k, m, d, unroll, n):
    place = (m - d) % unroll
    body = k + (m - d - place) // unroll
    item = body * unroll + place
    if isinstance(k, int) and not 0 <= item < n:
        return None
    return item, place, body


def first(item, n):
    return isinstance(item, int) and item < n


def run_steps(eng, n, depth, unroll, body, last=0):
    peel = -(-(depth + 2) // unroll)
    for k in range(peel):
        for m in range(unroll):
            body(k, m)
    with eng.Fori(peel, n // unroll - last) as k:
        for m in range(unroll):
            body(k, m)
    for k in range(n // unroll - last, n // unroll):
        for m in range(unroll):
            body(k, m)
    for s in range(n, n + depth):
        body(s // unroll, s % unroll)


class Link:

    def __init__(self, eng, sem, per_step):
        self.eng, self.sem, self.per_step = eng, sem, per_step
        self.base, self.n = 0, 0

    def step(self, number):
        self.base, self.n = number * self.per_step, 0

    def __call__(self, ins):
        self.n += 1
        ins.then_inc(self.sem, 1)
        self.eng.wait_ge(self.sem, self.base + self.n)

    def settle(self):
        self.n += 1
        self.eng.sem_inc(self.sem, 1)

    def fill(self):
        left = self.per_step - self.n
        assert left >= 0, self.n
        if left:
            self.eng.sem_inc(self.sem, left)


def inv_sqrt(nc, link, v, y, t):
    vi, yi = v.bitcast(I32), y.bitcast(I32)
    link(nc.vector.tensor_scalar(yi, vi, 1, None, ALU.arith_shift_right))
    link(nc.vector.tensor_scalar(yi, yi, -1, 0x5F3759DF, ALU.mult, ALU.add))
    for _ in range(3):
        link(nc.vector.tensor_tensor(t, y, y, ALU.mult))
        link(nc.vector.tensor_tensor(t, t, v, ALU.mult))
        link(nc.vector.tensor_scalar(t, t, -0.5, 1.5, ALU.mult, ALU.add))
        link(nc.vector.tensor_tensor(y, y, t, ALU.mult))


INV_SQRT_LINKS = 14


class Memory:

    whole = None

    def __init__(self, nc, ctx, name):
        self.nc, self.ctx, self.name = nc, ctx, name

    def sb(self, name, shape, dt=F32):
        return self.ctx.enter_context(self.nc.sbuf_tensor(f"{self.name}_{name}", shape, dt))

    def ps(self, name, shape, dt=F32):
        return self.ctx.enter_context(self.nc.psum_tensor(f"{self.name}_{name}", shape, dt))

    def sem(self, name):
        return self.ctx.enter_context(self.nc.semaphore(f"{self.name}_{name}"))

    def stored(self, name, n):
        return [Memory.whole.enter_context(self.nc.semaphore(f"{self.name}_{name}{i}")) for i in range(n)]

    def sems(self, name, n):
        return [self.sem(f"{name}{i}") for i in range(n)]


class Splitter:

    RING = 4

    def __init__(self, nc):
        self.nc = nc
        mem = Memory(nc, Memory.whole, "split")
        self.loaded = mem.sems("loaded", self.RING)
        self.hi_done = mem.sem("hi_done")
        self.lo_done = mem.sem("lo_done")
        self.loads = [0] * self.RING
        self.done = 0

    def pieces(self, raw, pieces):
        part = WeightPieces()
        part.of, part.raw, part.pieces = self, raw, pieces
        part.before, part.loads = self.done, list(self.loads)
        self.done += len(pieces)
        for n in range(len(pieces)):
            self.loads[n % self.RING] += 16
        return part


class WeightPieces:
    def load(self, sp, n):
        src, hi, _, _ = self.pieces[n]
        if n >= self.of.RING:
            sp.wait_ge(self.of.lo_done, self.before + n - self.of.RING + 1)
        sp.dma_start(self.at(n), src).then_inc(self.of.loaded[n % self.of.RING], 16)

    def at(self, n):
        return self.raw[n % self.of.RING][:, 0:self.pieces[n][0].shape[-1]]

    def split_hi(self, act, n):
        _, hi, _, factor = self.pieces[n]
        r = self.of.RING
        act.wait_ge(self.of.loaded[n % r], self.loads[n % r] + 16 * (n // r + 1))
        by = {} if factor is None else {"scale": factor}
        self.of.nc.scalar.activation(hi, self.at(n), ACT.Copy, **by).then_inc(self.of.hi_done, 1)

    def split_lo(self, dve, n):
        _, hi, lo, factor = self.pieces[n]
        nc = self.of.nc
        dve.wait_ge(self.of.hi_done, self.before + n + 1)
        if factor is None:
            ins = nc.vector.tensor_tensor(lo, self.at(n), hi, ALU.subtract)
        else:
            ins = nc.vector.scalar_tensor_tensor(lo, self.at(n), factor, hi, ALU.mult, ALU.subtract)
        ins.then_inc(self.of.lo_done, 1)

    def wait(self, pe, n):
        pe.wait_ge(self.of.lo_done, self.before + n + 1)


def three_pass(nc, outs, xhi, xlo, his, los, start, stop, onto=False):
    for x, ws, a, b in ((xlo, his, start, False), (xhi, los, False, False), (xhi, his, False, stop)):
        for o, w in zip(outs, ws):
            last = nc.tensor.matmul(o, x, w, start=a, stop=b, skip_group_check=onto)
    return last


def tok_up(nc, d, split, ident):
    with ExitStack() as ctx:
        mem = Memory(nc, ctx, "up")
        w_hi = mem.sb("w_hi", [P, KIN, 2 * HID], F32R)
        w_lo = mem.sb("w_lo", [P, KIN, 2 * HID], F32R)
        CW = KCH * P
        raw = [mem.sb(f"raw{c}", [P, KCH, P]) for c in range(NCH)]
        x_hi = [mem.sb(f"x_hi{c}", [P, KCH, P], F32R) for c in range(NCH)]
        x_lo = [mem.sb(f"x_lo{c}", [P, KCH, P], F32R) for c in range(NCH)]
        xs = [mem.sb(f"xs{i}", [P, CW]) for i in range(2)]
        junk = mem.sb("junk", [P, CW], BF16)
        ssq = mem.sb("ssq", [P, NCH])
        r = [mem.sb(f"r{i}", [P, 1]) for i in range(2)]
        var = mem.sb("var", [P, 2])
        sil = [mem.sb(f"sil{i}", [P, HID]) for i in range(2)]
        g = sil
        gt = [mem.sb(f"gt{i}", [P, HID]) for i in range(2)]
        fac = mem.sb("fac", [P, KIN])
        w1 = split.pieces([*sil, *gt], [(d["w1"][:, n, a:a + HID], w_hi[:, n, a:a + HID], w_lo[:, n, a:a + HID],
                                         fac[:, n:n + 1]) for n in range(KIN) for a in (0, HID)])
        PER = 2 * KCH
        ps_h = [mem.ps(f"ps_h{i}", [P, 2 * HID]) for i in range(2)]
        ps_t = [mem.ps(f"ps_t{i}", [P, HID]) for i in range(2)]
        raw_in = mem.sems("raw_in", NCH)
        xs_in = mem.sems("xs_in", 2)
        hi_done = mem.sem("hi_done")
        lo_done = mem.sem("lo_done")
        x_used = mem.sem("x_used")
        sq_done = mem.sem("sq_done")
        r_done = mem.sem("r_done")
        sil_done = mem.sem("sil_done")
        g_done = mem.sem("g_done")
        t_done = mem.sem("t_done")
        gt_done = mem.sem("gt_done")
        gt_stored = mem.stored("gt_stored", 2)
        link_sem = mem.sem("link")
        fac_in = mem.sem("fac_in")
        block = ctx.enter_context(nc.Block())
        DEPTH = 1

        @block.sync
        def _(sp):
            sp.dma_start(fac[:], d["pre_ln"]).then_inc(fac_in, 16)

            def body(k, m):
                s = stage(k, m, 0, 2, TILES)
                if s is None:
                    return
                t, _, _ = s
                for c in range(NCH):
                    if not first(t, 1):
                        sp.wait_ge(lo_done, 4 * t + (c - 3))
                    sp.dma_start(raw[c][:], d["x_t"][t, :, KCH * c:KCH * c + KCH, :]).then_inc(raw_in[c], 16)
                    if not (first(t, 1) and c < 2):
                        sp.wait_ge(sq_done, 4 * t + (c - 1))
                    if first(t, 1):
                        for n in range(PER * c, PER * c + PER):
                            w1.load(sp, n)
                    sp.dma_start(xs[c % 2][:], d["x_rows"][t, :, CW * c:CW * c + CW]).then_inc(xs_in[c % 2], 16)

            run_steps(sp, TILES, DEPTH, 2, body)

        @block.scalar
        def _(act):
            act.wait_ge(fac_in, 16)

            def body(k, m):
                s = stage(k, m, 0, 2, TILES)
                if s is not None:
                    t, b, _ = s
                    for c in range(NCH):
                        act.wait_ge(raw_in[c], 16 * t + 16)
                        if not first(t, 1):
                            act.wait_ge(x_used, 4 * t + (c - 3))
                        nc.scalar.activation(x_hi[c][:], raw[c][:], ACT.Copy).then_inc(hi_done, 1)
                        if first(t, 1):
                            for n in range(PER * c, PER * c + PER):
                                w1.split_hi(act, n)
                        if c == 0 and not first(t, 1):
                            act.wait_ge(r_done, t)
                        act.wait_ge(xs_in[c % 2], 32 * t + 16 * (c // 2) + 16)
                        if not (first(t, 1) and c == 0):
                            act.wait_ge(sq_done, 4 * t + c)
                        nc.scalar.activation(junk[:], xs[c % 2][:], ACT.Square,
                                             accum_out=ssq[:, c:c + 1]).then_inc(sq_done, 1)
                s = stage(k, m, 1, 2, TILES)
                if s is not None:
                    t, b, kb = s
                    act.wait_ge(x_used, 4 * t + 4)
                    act.wait_ge(r_done, t + 1)
                    if not first(t, 2):
                        act.wait_ge(t_done, t - 1)
                    nc.scalar.activation(sil[b][:], ps_h[b][:, HID:2 * HID], ACT.Silu,
                                         scale=r[b][:, 0:1]).then_inc(sil_done, 1)
                    act.wait_ge(t_done, t + 1)
                    if not first(t, 2):
                        act.wait_ge(gt_stored[b], 16 * kb)
                    nc.scalar.activation(gt[b][:], ps_t[b][:], ACT.Copy).then_inc(gt_done, 1)

            run_steps(act, TILES, DEPTH, 2, body)

        @block.vector
        def _(dve):
            link = Link(dve, link_sem, INV_SQRT_LINKS + 2)
            dve.wait_ge(fac_in, 16)

            def body(k, m):
                s = stage(k, m, 0, 2, TILES)
                if s is not None:
                    t, b, _ = s
                    link.step(t)
                    for c in range(NCH):
                        dve.wait_ge(hi_done, 4 * t + c + 1)
                        nc.vector.tensor_tensor(x_lo[c][:], raw[c][:], x_hi[c][:], ALU.subtract).then_inc(lo_done, 1)
                        if first(t, 1):
                            for n in range(PER * c, PER * c + PER):
                                w1.split_lo(dve, n)
                s1 = stage(k, m, 1, 2, TILES)
                if s1 is not None:
                    t, b, _ = s1
                    dve.wait_ge(sil_done, t + 1)
                    nc.vector.scalar_tensor_tensor(g[b][:], ps_h[b][:, 0:HID], r[b][:, 0:1], sil[b][:],
                                                   ALU.mult, ALU.mult).then_inc(g_done, 1)
                if s is not None:
                    t, b, _ = s
                    dve.wait_ge(sq_done, 4 * t + 4)
                    link(nc.vector.reduce_sum(var[:, 0:1], ssq[:], AX.X))
                    link(nc.vector.tensor_scalar(var[:, 0:1], var[:, 0:1], 1.0 / DIN, RMS_EPS, ALU.mult, ALU.add))
                    inv_sqrt(nc, link, var[:, 0:1], r[b][:], var[:, 1:2])
                    link.fill()
                    dve.sem_inc(r_done, 1)

            run_steps(dve, TILES, DEPTH, 2, body)

        @block.tensor
        def _(pe):
            def body(k, m):
                s = stage(k, m, 0, 2, TILES)
                s1 = stage(k, m, 1, 2, TILES)
                for c in range(NCH):
                    if s is not None:
                        t, b, _ = s
                        if c == 0 and not first(t, 2):
                            pe.wait_ge(g_done, t - 1)
                        pe.wait_ge(lo_done, 4 * t + c + 1)
                        outs = [ps_h[b][:, 0:HID], ps_h[b][:, HID:2 * HID]]
                        for j in range(KCH):
                            n = KCH * c + j
                            if first(t, 1):
                                w1.wait(pe, 2 * n + 1)
                            last = three_pass(nc, outs, x_hi[c][:, j, :], x_lo[c][:, j, :],
                                              [w_hi[:, n, 0:HID], w_hi[:, n, HID:2 * HID]],
                                              [w_lo[:, n, 0:HID], w_lo[:, n, HID:2 * HID]], n == 0, n == KIN - 1)
                        last.then_inc(x_used, 1)
                    if c == 0 and s1 is not None:
                        t, b, _ = s1
                        pe.wait_ge(g_done, t + 1)
                        if not first(t, 2):
                            pe.wait_ge(gt_done, t - 1)
                        for j in range(HID // P):
                            last = nc.tensor.transpose(ps_t[b][:, P * j:P * j + P], g[b][:, P * j:P * j + P], ident[:])
                        last.then_inc(t_done, 1)

            run_steps(pe, TILES, DEPTH, 2, body)

        @block.gpsimd
        def _(pool):
            def body(k, m):
                s = stage(k, m, 1, 2, TILES)
                if s is None:
                    return
                t, b, _ = s
                pool.wait_ge(gt_done, t + 1)
                pool.dma_start(d["g_t"][t], gt[b][:]).then_inc(gt_stored[b], 16)

            run_steps(pool, TILES, DEPTH, 2, body)
            for b in range(2):
                pool.wait_ge(gt_stored[b], 16 * TILES // 2)


def refine(nc, link, v, y, t):
    link(nc.vector.scalar_tensor_tensor(t, y, y, v, ALU.mult, ALU.mult))
    link(nc.vector.tensor_scalar(t, t, -0.5, 1.5, ALU.mult, ALU.add))
    link(nc.vector.tensor_tensor(y, y, t, ALU.mult))


def tok_down(nc, d, split, ident, qn_hi, qn_lo, k_t):
    W = QR + KR + RO
    with ExitStack() as ctx:
        mem = Memory(nc, ctx, "down")
        w2_hi = mem.sb("w2_hi", [P, 4, DM], F32R)
        w2_lo = mem.sb("w2_lo", [P, 4, DM], F32R)
        wa_hi = mem.sb("wa_hi", [P, KM, W], F32R)
        wa_lo = mem.sb("wa_lo", [P, KM, W], F32R)
        post = mem.sb("post", [P, DM])
        kvw = mem.sb("kvw", [P, KR])
        g_raw = [mem.sb(f"g_raw{i}", [P, 4, P]) for i in range(2)]
        g_hi = [mem.sb(f"g_hi{i}", [P, 4, P], F32R) for i in range(2)]
        g_lo = [mem.sb(f"g_lo{i}", [P, 4, P], F32R) for i in range(2)]
        junk = mem.sb("junk", [P, DM], BF16)
        junk_a = mem.sb("junk_a", [P, QR + KR], BF16)
        ms = [mem.sb(f"ms{i}", [P, 3]) for i in range(2)]
        root = [mem.sb(f"root{i}", [P, 4]) for i in range(2)]
        vec = [mem.sb(f"vec{i}", [P, 16]) for i in range(2)]
        bn = mem.sb("bn", [P, 12])
        z = mem.sb("z", [P, DM])
        y = [mem.sb(f"y{i}", [P, DM]) for i in range(2)]
        xn = [mem.sb(f"xn{i}", [P, DM]) for i in range(2)]
        xt_hi = mem.sb("xt_hi", [P, KM, P], F32R)
        xt_lo = mem.sb("xt_lo", [P, KM, P], F32R)
        qk = [mem.sb(f"qk{i}", [P, W]) for i in range(2)]
        wqn = [mem.sb(f"wqn{i}", [P, QR]) for i in range(2)]
        wk = [mem.sb(f"wk{i}", [P, KR]) for i in range(2)]
        wqp = [mem.sb(f"wqp{i}", [P, 2, P]) for i in range(2)]
        wv = [mem.sb(f"wv{i}", [P, 2, KR]) for i in range(2)]
        wo = [mem.sb(f"wo{i}", [P, 2, DM]) for i in range(2)]
        qln = mem.sb("qln", [P, 2])
        wq_out = [mem.sb(f"wq_out{i}", [P, 2, 2 * P]) for i in range(2)]
        wv_out = [mem.sb(f"wv_out{i}", [P, DM]) for i in range(2)]
        NW = 4 + KM
        ws = split.pieces([wo[i][:, h, :] for i in range(2) for h in range(2)],
                          [(d["w2"][:, n, :], w2_hi[:, n, :], w2_lo[:, n, :], None) for n in range(4)] +
                          [(d["wa"][:, n, :], wa_hi[:, n, :], wa_lo[:, n, :], None) for n in range(KM)])
        ps_y = mem.ps("ps_y", [P, DM])
        ps_x = [mem.ps(f"ps_x{i}", [P, 4, P]) for i in range(2)]
        ps_a = [mem.ps(f"ps_a{i}", [P, 512]) for i in range(2)]
        ps_d = mem.ps("ps_d", [P, 512])
        ps_f = mem.ps("ps_f", [P, 512])
        eps = mem.sb("eps", [P, 1])
        eps_set = mem.sem("eps_set")
        const_in = mem.sem("const_in")
        g_in = mem.sems("g_in", 2)
        ghi_done = mem.sem("ghi_done")
        glo_done = mem.sem("glo_done")
        y_made = mem.sem("y_made")
        ysq_done = mem.sem("ysq_done")
        yroot_done = mem.sem("yroot_done")
        z_done = mem.sem("z_done")
        r_done = mem.sem("r_done")
        y_done = mem.sem("y_done")
        yvar_done = mem.sem("yvar_done")
        yvroot_done = mem.sem("yvroot_done")
        xn_done = mem.sem("xn_done")
        x_turned = mem.sem("x_turned")
        xhi_done = mem.sem("xhi_done")
        xlo_done = mem.sem("xlo_done")
        a_made = mem.sem("a_made")
        asq_done = mem.sem("asq_done")
        aroot_done = mem.sem("aroot_done")
        avar_done = mem.sem("avar_done")
        qk_done = mem.sem("qk_done")
        qk_turned = mem.sem("qk_turned")
        qhi_done = mem.sem("qhi_done")
        qlo_done = mem.sem("qlo_done")
        y_stored = mem.stored("y_stored", 2)
        fold_in = mem.sems("fold_in", 2)
        fa_made = mem.sem("fa_made")
        f_made = mem.sem("f_made")
        f_out = mem.sem("f_out")
        rope_out = mem.sem("rope_out")
        wq_stored = mem.stored("wq_stored", 2)
        wv_stored = mem.stored("wv_stored", 2)
        link_sem = mem.sem("link")
        block = ctx.enter_context(nc.Block())
        D_Y, D_X, D_A, D_Q = 1, 3, 3, 4
        DEPTH = 4
        U = 6
        FOLD = {0: 0, 1: 1, 3: 2, 4: 3}
        assert PAIRS == TILES // U * len(FOLD)

        def fold(k, m):
            if m not in FOLD or (isinstance(k, int) and k * U + m >= TILES):
                return None
            f = FOLD[m]
            return k * len(FOLD) + f, f % 2, k * (len(FOLD) // 2) + f // 2

        def nth(kb, u):
            return kb * (U // 2) + u // 2 + 1

        @block.sync
        def _(sp):
            sp.dma_start(post[:], d["post_ln"]).then_inc(const_in, 16)
            sp.dma_start(kvw[:], d["kv_ln"]).then_inc(const_in, 16)
            sp.dma_start(qln[:], d["q_ln"]).then_inc(const_in, 16)

            def body(k, m):
                s = stage(k, m, 0, U, TILES)
                if s is not None:
                    t, u, kb = s
                    if not first(t, 2):
                        sp.wait_ge(glo_done, t - 1)
                    sp.dma_start(g_raw[u % 2][:], d["g_t"][t].rearrange("p (j c) -> p j c", j=4)).then_inc(g_in[u % 2], 16)
                    if first(t, 1):
                        for n in range(NW):
                            ws.load(sp, n)
                s = fold(k, m)
                if s is not None:
                    p, b, turn = s
                    if first(p, 2):
                        ws.wait(sp, NW - 1)
                    else:
                        sp.wait_ge(wv_stored[b], 16 * turn)
                    for dst, name in ((wqn, "wq_nope"), (wk, "wk"), (wqp, "wq_rope"), (wv, "wv"), (wo, "wo")):
                        sp.dma_start(dst[b][:], d[name][p]).then_inc(fold_in[b], 16)

            run_steps(sp, TILES, DEPTH, U, body)

        @block.gpsimd
        def _(pool):
            nc.gpsimd.memset(eps[:], RMS_EPS).then_inc(eps_set, 1)
            pool.wait_ge(const_in, 48)

            def body(k, m):
                s = fold(k, m)
                if s is not None:
                    p, b, turn = s
                    pool.wait_ge(fold_in[b], 80 * turn + 80)
                    if not first(p, 2):
                        pool.wait_ge(wq_stored[b], 16 * turn)
                    nc.gpsimd.tensor_tensor(wq_out[b][:, :, P:2 * P], wqp[b][:], qln[:].unsqueeze(2).broadcast_to((P, 2, P)),
                                            ALU.mult).then_inc(rope_out, 1)
                s1 = stage(k, m, D_Y, U, TILES)
                if s1 is not None:
                    t, u, kb = s1
                    pool.wait_ge(y_done, t + 1)
                    pool.dma_start(d["y"][t], y[u % 2][:]).then_inc(y_stored[u % 2], 16)
                if s is not None:
                    p, b, turn = s
                    pool.wait_ge(rope_out, p + 1)
                    pool.wait_ge(f_out, 3 * p + 1)
                    pool.dma_start(d["wq_pair"][p], wq_out[b][:]).then_inc(wq_stored[b], 16)
                    pool.wait_ge(f_out, 3 * p + 3)
                    pool.dma_start(d["wvo"][:, p, :], wv_out[b][:]).then_inc(wv_stored[b], 16)

            run_steps(pool, TILES, DEPTH, U, body)
            for b in range(2):
                pool.wait_ge(y_stored[b], 16 * TILES // 2)
                pool.wait_ge(wq_stored[b], 16 * PAIRS // 2)
                pool.wait_ge(wv_stored[b], 16 * PAIRS // 2)

        @block.scalar
        def _(act):
            act.wait_ge(const_in, 48)
            act.wait_ge(eps_set, 1)

            def fold_half(f, n):
                p, b, turn = f
                act.wait_ge(f_made, 3 * p + 2 + n)
                if n == 0 and not first(p, 2):
                    act.wait_ge(wv_stored[b], 16 * turn)
                nc.scalar.activation(wv_out[b][:, 512 * n:512 * n + 512], ps_f[:], ACT.Copy).then_inc(f_out, 1)

            def body(k, m):
                s = stage(k, m, D_X, U, TILES)
                if s is not None:
                    t, u, kb = s
                    if not first(t, 1):
                        act.wait_ge(a_made, t)
                    for h in range(2):
                        act.wait_ge(x_turned, 2 * t + h + 1)
                        nc.scalar.activation(xt_hi[:, 4 * h:4 * h + 4, :], ps_x[h][:], ACT.Copy).then_inc(xhi_done, 1)
                s = stage(k, m, 0, U, TILES)
                if s is not None:
                    t, u, kb = s
                    act.wait_ge(g_in[u % 2], 16 * nth(kb, u))
                    if not first(t, 2):
                        act.wait_ge(y_made, t - 1)
                    nc.scalar.activation(g_hi[u % 2][:], g_raw[u % 2][:], ACT.Copy).then_inc(ghi_done, 1)
                    if first(t, 1):
                        for n in range(NW):
                            ws.split_hi(act, n)
                f = fold(k, m)
                if f is not None:
                    p, b, turn = f
                    act.wait_ge(f_made, 3 * p + 1)
                    if not first(p, 2):
                        act.wait_ge(wq_stored[b], 16 * turn)
                    for c in range(2):
                        last = nc.scalar.activation(wq_out[b][:, c, 0:P], ps_f[:, P * c:P * c + P], ACT.Copy,
                                                    scale=qln[:, c:c + 1])
                    last.then_inc(f_out, 1)
                s = stage(k, m, D_Y, U, TILES)
                if s is not None:
                    t, u, kb = s
                    b = u % 2
                    act.wait_ge(y_made, t + 1)
                    if not first(t, 1):
                        act.wait_ge(ysq_done, t)
                    if not first(t, 2):
                        act.wait_ge(xn_done, t - 1)
                    act.wait_ge(z_done, t + 1)
                    nc.scalar.activation(junk[:], ps_y[:], ACT.Square, scale=DM ** -0.5,
                                         accum_out=ms[b][:, 0:1]).then_inc(ysq_done, 1)
                    act.wait_ge(ysq_done, t + 1)
                    nc.scalar.activation(root[b][:, 0:1], ms[b][:, 0:1], ACT.Sqrt, bias=eps[:, 0:1]).then_inc(yroot_done, 1)
                if f is not None:
                    fold_half(f, 0)
                if s is not None:
                    act.wait_ge(r_done, t + 1)
                    if not first(t, 2):
                        act.wait_ge(y_stored[b], 16 * nth(kb, u) - 16)
                    nc.scalar.activation(y[b][:], z[:], ACT.Copy, scale=vec[b][:, 1:2]).then_inc(y_done, 1)
                    act.wait_ge(yvar_done, t + 1)
                    nc.scalar.activation(root[b][:, 3:4], vec[b][:, 6:7], ACT.Sqrt).then_inc(yvroot_done, 1)
                s = stage(k, m, D_A, U, TILES)
                if s is not None:
                    t, u, kb = s
                    b = u % 2
                    act.wait_ge(a_made, t + 1)
                    if not first(t, 2):
                        act.wait_ge(qk_done, t - 1)
                    if not first(t, 1):
                        act.wait_ge(asq_done, 2 * t)
                    nc.scalar.activation(junk_a[:, 0:QR], ps_a[b][:, 0:QR], ACT.Square, scale=QR ** -0.5,
                                         accum_out=ms[b][:, 1:2]).then_inc(asq_done, 1)
                    nc.scalar.activation(junk_a[:, QR:QR + KR], ps_a[b][:, QR:QR + KR], ACT.Square, scale=KR ** -0.5,
                                         accum_out=ms[b][:, 2:3]).then_inc(asq_done, 1)
                    act.wait_ge(asq_done, 2 * t + 2)
                    nc.scalar.activation(root[b][:, 1:3], ms[b][:, 1:3], ACT.Sqrt, bias=eps[:, 0:1]).then_inc(aroot_done, 1)
                if f is not None:
                    fold_half(f, 1)
                s = stage(k, m, D_Q, U, TILES)
                if s is not None:
                    t, u, kb = s
                    act.wait_ge(qk_turned, t + 1)
                    cols = bass.ts(t, P)
                    nc.scalar.activation(qn_hi[:, :, cols], ps_d[:, 0:2 * P].rearrange("p (c n) -> p c n", c=2),
                                         ACT.Copy).then_inc(qhi_done, 1)
                    nc.scalar.activation(k_t[:, cols], ps_d[:, 2 * P:3 * P], ACT.Copy).then_inc(qhi_done, 1)

            run_steps(act, TILES, DEPTH, U, body)

        @block.vector
        def _(dve):
            dve.wait_ge(const_in, 48)
            link = Link(dve, link_sem, 22)

            def body(k, m):
                s = stage(k, m, D_X, U, TILES)
                if s is not None:
                    t, u, kb = s
                    for h in range(2):
                        dve.wait_ge(xhi_done, 2 * t + h + 1)
                        nc.vector.tensor_tensor(xt_lo[:, 4 * h:4 * h + 4, :], ps_x[h][:], xt_hi[:, 4 * h:4 * h + 4, :],
                                                ALU.subtract).then_inc(xlo_done, 1)
                s = stage(k, m, 0, U, TILES)
                if s is not None:
                    t, u, kb = s
                    dve.wait_ge(ghi_done, t + 1)
                    nc.vector.tensor_tensor(g_lo[u % 2][:], g_raw[u % 2][:], g_hi[u % 2][:],
                                            ALU.subtract).then_inc(glo_done, 1)
                    if first(t, 1):
                        for n in range(NW):
                            ws.split_lo(dve, n)
                s = stage(k, m, D_Y, U, TILES)
                if s is not None:
                    t, u, kb = s
                    b = u % 2
                    v = vec[b]
                    dve.wait_ge(y_made, t + 1)
                    if not first(t, 1):
                        dve.wait_ge(y_done, t)
                        dve.wait_ge(xn_done, t)
                    nc.vector.tensor_tensor(z[:], ps_y[:], post[:], ALU.mult).then_inc(z_done, 1)
                    dve.wait_ge(z_done, t + 1)
                    nc.vector.bn_stats(bn[:, 0:6], z[:, 0:512])
                    link(nc.vector.bn_stats(bn[:, 6:12], z[:, 512:1024]))
                    dve.wait_ge(yroot_done, t + 1)
                    if not first(t, 2):
                        dve.wait_ge(yvroot_done, t - 1)
                    nc.vector.tensor_scalar(v[:, 0:1], ms[b][:, 0:1], RMS_EPS, None, ALU.add)
                    link(nc.vector.reciprocal(v[:, 1:2], root[b][:, 0:1]))
                    refine(nc, link, v[:, 0:1], v[:, 1:2], v[:, 2:3])
                    dve.sem_inc(r_done, 1)
                    link.settle()
                    link(nc.vector.bn_aggr(v[:, 4:6], bn[:]))
                    link(nc.vector.scalar_tensor_tensor(v[:, 3:4], v[:, 1:2], v[:, 1:2], v[:, 5:6], ALU.mult, ALU.mult))
                    nc.vector.tensor_scalar(v[:, 6:7], v[:, 3:4], LN_EPS, None, ALU.add).then_inc(yvar_done, 1)
                    dve.wait_ge(yvroot_done, t + 1)
                    link(nc.vector.reciprocal(v[:, 7:8], root[b][:, 3:4]))
                    refine(nc, link, v[:, 6:7], v[:, 7:8], v[:, 8:9])
                    link(nc.vector.tensor_tensor(v[:, 7:8], v[:, 7:8], v[:, 1:2], ALU.mult))
                    if not first(t, 2):
                        dve.wait_ge(x_turned, 2 * t - 2)
                    nc.vector.tensor_scalar(xn[b][:], z[:], v[:, 4:5], v[:, 7:8], ALU.subtract,
                                            ALU.mult).then_inc(xn_done, 1)
                s = stage(k, m, D_A, U, TILES)
                if s is not None:
                    t, u, kb = s
                    b = u % 2
                    v = vec[b]
                    dve.wait_ge(aroot_done, t + 1)
                    nc.vector.tensor_scalar(v[:, 9:11], ms[b][:, 1:3], RMS_EPS, None, ALU.add)
                    link(nc.vector.reciprocal(v[:, 11:13], root[b][:, 1:3]))
                    link(nc.vector.tensor_tensor(v[:, 13:15], v[:, 11:13], v[:, 11:13], ALU.mult))
                    link(nc.vector.tensor_tensor(v[:, 13:15], v[:, 13:15], v[:, 9:11], ALU.mult))
                    link(nc.vector.tensor_scalar(v[:, 13:15], v[:, 13:15], -0.5, 1.5, ALU.mult, ALU.add))
                    link(nc.vector.tensor_tensor(v[:, 11:13], v[:, 11:13], v[:, 13:15], ALU.mult))
                    if not first(t, 2):
                        dve.wait_ge(qk_turned, t - 1)
                    nc.vector.tensor_scalar(qk[b][:, 0:QR], ps_a[b][:, 0:QR], v[:, 11:12], None, ALU.mult)
                    nc.vector.scalar_tensor_tensor(qk[b][:, QR:QR + KR], ps_a[b][:, QR:QR + KR], v[:, 12:13],
                                                   kvw[:], ALU.mult, ALU.mult)
                    nc.vector.tensor_copy(qk[b][:, QR + KR:W], ps_a[b][:, QR + KR:W]).then_inc(qk_done, 1)
                s = stage(k, m, D_Q, U, TILES)
                if s is not None:
                    t, u, kb = s
                    cols = bass.ts(t, P)
                    dve.wait_ge(qhi_done, 2 * t + 2)
                    nc.vector.tensor_tensor(qn_lo[:, :, cols], ps_d[:, 0:2 * P].rearrange("p (c n) -> p c n", c=2),
                                            qn_hi[:, :, cols], ALU.subtract).then_inc(qlo_done, 1)

            def step(k, m):
                link.step(k * U + m)
                body(k, m)
                link.fill()

            run_steps(dve, TILES, DEPTH, U, step)

        @block.tensor
        def _(pe):
            def fold_q(f, h):
                p, b, turn = f
                if h == 0:
                    pe.wait_ge(fold_in[b], 80 * turn + 80)
                    if not first(p, 1):
                        pe.wait_ge(f_out, 3 * p)
                else:
                    pe.wait_ge(fa_made, p + 1)
                rows = slice(64 * h, 64 * h + 64)
                for c in range(2):
                    at = P * c + 64 * h
                    last = nc.tensor.matmul(ps_f[:, at:at + 64], wqn[b][rows, P * c:P * c + P], wk[b][rows, :],
                                            start=True, stop=True)
                last.then_inc(f_made if h == 1 else fa_made, 1)

            def fold_v(f, n):
                p, b, turn = f
                pe.wait_ge(f_out, 3 * p + 1 + n)
                for h in range(2):
                    last = nc.tensor.matmul(ps_f[64 * h:64 * h + 64, :], wv[b][:, h, :],
                                            wo[b][:, h, 512 * n:512 * n + 512], start=True, stop=True)
                last.then_inc(f_made, 1)

            def body(k, m):
                f = fold(k, m)
                s = stage(k, m, D_X, U, TILES)
                if s is not None:
                    t, u, kb = s
                    pe.wait_ge(xn_done, t + 1)
                    for h in range(2):
                        if not first(t, 1):
                            pe.wait_ge(xlo_done, 2 * t + (h - 1))
                        for j in range(4):
                            n = 4 * h + j
                            last = nc.tensor.transpose(ps_x[h][:, j, :], xn[u % 2][:, P * n:P * n + P], ident[:])
                        last.then_inc(x_turned, 1)
                if f is not None:
                    fold_q(f, 0)
                s = stage(k, m, D_Y, U, TILES)
                if s is not None:
                    t, u, kb = s
                    pe.wait_ge(glo_done, t + 1)
                    if not first(t, 1):
                        pe.wait_ge(z_done, t)
                        pe.wait_ge(ysq_done, t)
                    outs = [ps_y[:, 0:512], ps_y[:, 512:1024]]
                    for n in range(4):
                        if n == 2 and f is not None:
                            fold_q(f, 1)
                        if first(t, 1):
                            ws.wait(pe, n)
                        last = three_pass(nc, outs, g_hi[u % 2][:, n, :], g_lo[u % 2][:, n, :],
                                          [w2_hi[:, n, 0:512], w2_hi[:, n, 512:1024]],
                                          [w2_lo[:, n, 0:512], w2_lo[:, n, 512:1024]], n == 0, n == 3)
                    last.then_inc(y_made, 1)
                elif f is not None:
                    fold_q(f, 1)
                if f is not None:
                    fold_v(f, 0)
                s = stage(k, m, D_A, U, TILES)
                if s is not None:
                    t, u, kb = s
                    if not first(t, 2):
                        pe.wait_ge(qk_done, t - 1)
                    for n in range(KM):
                        if n % 4 == 0:
                            pe.wait_ge(xlo_done, 2 * t + n // 4 + 1)
                        if first(t, 1):
                            ws.wait(pe, 4 + n)
                        last = three_pass(nc, [ps_a[u % 2][:, 0:W]], xt_hi[:, n, :], xt_lo[:, n, :],
                                          [wa_hi[:, n, :]], [wa_lo[:, n, :]], n == 0, n == KM - 1)
                    last.then_inc(a_made, 1)
                if f is not None:
                    fold_v(f, 1)
                s = stage(k, m, D_Q, U, TILES)
                if s is not None:
                    t, u, kb = s
                    pe.wait_ge(qk_done, t + 1)
                    if not first(t, 1):
                        pe.wait_ge(qlo_done, t)
                        pe.wait_ge(qhi_done, 2 * t)
                    for j in range(3):
                        last = nc.tensor.transpose(ps_d[:, P * j:P * j + P], qk[u % 2][:, P * j:P * j + P], ident[:])
                    last.then_inc(qk_turned, 1)

            run_steps(pe, TILES, DEPTH, U, body)


def attention(nc, d, ident, qn_hi, qn_lo, k_t):
    with ExitStack() as ctx:
        mem = Memory(nc, ctx, "attn")
        cos = mem.sb("cos", [P, GT])
        sin = mem.sb("sin", [P, GT])
        k_tb = mem.sb("k_tb", [P, TOK])
        v = mem.sb("v", [P, BATCH, KR])
        mask = mem.sb("mask", [P, SEQ])
        swap = [p ^ 1 for p in range(32)]
        attention_keys(nc, d, ident, k_t, k_tb, v, cos, sin, mask, swap)

        w_raw = [mem.sb(f"w_raw{i}", [P, 2, 2 * P]) for i in range(2)]
        w_hi = [mem.sb(f"w_hi{i}", [P, 2, 2 * P], F32R) for i in range(2)]
        w_lo = [mem.sb(f"w_lo{i}", [P, 2, 2 * P], F32R) for i in range(2)]
        q_a = [mem.sb(f"q_a{i}", [P, GT]) for i in range(2)]
        q_b = [mem.sb(f"q_b{i}", [P, GT]) for i in range(2)]
        by_cos = mem.sb("by_cos", [P, GT])
        swapped = mem.sb("swapped", [P, GT])
        by_sin = mem.sb("by_sin", [P, GT])
        top = mem.sb("top", [P, 8])
        bias = [mem.sb(f"bias{i}", [P, 8]) for i in range(2)]
        total = [mem.sb(f"total{i}", [P, 8]) for i in range(2)]
        share = [mem.sb(f"share{i}", [P, 8]) for i in range(2)]
        NPR = 4
        prob = [mem.sb(f"prob{i}", [P, 2, GT]) for i in range(NPR)]
        prob_t = [mem.sb(f"prob_t{i}", [P, 2, GT]) for i in range(2)]
        o_t = [mem.sb(f"o_t{i}", [P, GT]) for i in range(2)]
        zero = mem.sb("zero", [P, PAIRS, TOKP - TOK])
        ps_l = mem.ps("ps_l", [P, 512])
        ps_r = mem.ps("ps_r", [P, 512])
        ps_s = mem.ps("ps_s", [P, 2, 512])
        ps_t = mem.ps("ps_t", [P, 2, 512])
        ps_o = mem.ps("ps_o", [P, 512])
        w_in = mem.sems("w_in", 2)
        w_hi_done = mem.sem("w_hi_done")
        w_lo_done = mem.sem("w_lo_done")
        rope_made = mem.sem("rope_made")
        latent_made = mem.sem("latent_made")
        latent_done = mem.sem("latent_done")
        swap_done = mem.sem("swap_done")
        sin_done = mem.sem("sin_done")
        rope_a_done = mem.sem("rope_a_done")
        rope_b_done = mem.sem("rope_b_done")
        scored = mem.sem("scored")
        masked = mem.sem("masked")
        top_done = mem.sem("top_done")
        bias_done = mem.sem("bias_done")
        exp_done = mem.sem("exp_done")
        share_done = mem.sem("share_done")
        prob_done = mem.sem("prob_done")
        turned = mem.sem("turned")
        prob_t_done = mem.sem("prob_t_done")
        weighed = mem.sem("weighed")
        o_done = mem.sem("o_done")
        o_stored = mem.sems("o_stored", 2)
        zeroed = mem.sem("zeroed")
        pad_stored = mem.stored("pad_stored", 1)[0]
        block = ctx.enter_context(nc.Block())

        N = PAIRS * GROUPS
        U = 2 * GROUPS
        D_S, D_N, D_T, D_V, D_O = 1, 2, 4, 5, 6
        DEPTH = D_O
        PREP = 4

        def weights_of(k, m):
            if m % GROUPS != PREP:
                return None
            return stage(k, m // GROUPS, -1, 2, PAIRS)

        def bodied(n, kb, u, per):
            return kb * (U // per) + u // per + n

        @block.sync
        def _(sp):
            sp.dma_start(w_raw[0][:], d["wq_pair"][0]).then_inc(w_in[0], 16)

            def body(k, m):
                s = stage(k, m // GROUPS, -1, 2, PAIRS) if m % GROUPS == 0 else None
                if s is not None:
                    p, w, kb = s
                    if not first(p, 2):
                        sp.wait_ge(w_lo_done, p - 1)
                    sp.dma_start(w_raw[w][:], d["wq_pair"][p]).then_inc(w_in[w], 16)
                s = stage(k, m, D_O, U, N)
                if s is not None:
                    j, u, kb = s
                    g = u % GROUPS
                    sp.wait_ge(o_done, j + 1)
                    sp.dma_start(d["o_t"][:, 2 * kb + u // GROUPS, GT * g:GT * g + GT],
                                 o_t[u % 2][:]).then_inc(o_stored[u % 2], 16)

            run_steps(sp, N, DEPTH, U, body, last=1)
            for b in range(2):
                sp.wait_ge(o_stored[b], 16 * N // 2)

        @block.tensor
        def _(pe):
            def body(k, m):
                s = stage(k, m, 0, U, N)
                if s is not None:
                    j, u, kb = s
                    w, g = u // GROUPS, u % GROUPS
                    if g == 0:
                        pe.wait_ge(w_lo_done, 2 * kb + w + 1)
                    cols = slice(GT * g, GT * g + GT)
                    for ps, at, sem, free in ((ps_r, P, rope_made, swap_done), (ps_l, 0, latent_made, latent_done)):
                        if not first(j, 1):
                            pe.wait_ge(free, j)
                        for c in range(2):
                            wh, wl = w_hi[w][:, c, at:at + P], w_lo[w][:, c, at:at + P]
                            nc.tensor.matmul(ps[:, 0:GT], wl, qn_hi[:, c, cols], start=(c == 0), stop=False)
                            nc.tensor.matmul(ps[:, 0:GT], wh, qn_lo[:, c, cols], start=False, stop=False)
                            last = nc.tensor.matmul(ps[:, 0:GT], wh, qn_hi[:, c, cols], start=False, stop=(c == 1))
                        last.then_inc(sem, 1)
                s = stage(k, m, D_S, U, N)
                if s is not None:
                    j, u, kb = s
                    g = u % GROUPS
                    if not first(j, 1):
                        pe.wait_ge(masked, j)
                    pe.wait_ge(latent_done, j + 1)
                    pe.wait_ge(rope_a_done, j + 1)
                    pe.wait_ge(rope_b_done, j + 1)
                    for h, (q, keys) in enumerate(((q_a[u % 2], k_t), (q_b[u % 2], k_tb))):
                        for b in range(GB):
                            at = GT * g + SEQ * b
                            last = nc.tensor.matmul(ps_s[0:SEQ, h, SEQ * b:SEQ * b + SEQ], q[:, SEQ * b:SEQ * b + SEQ],
                                                    keys[:, at:at + SEQ], start=True, stop=True)
                    last.then_inc(scored, 1)
                s = stage(k, m, D_T, U, N)
                if s is not None:
                    j, u, kb = s
                    pe.wait_ge(prob_done, j + 1)
                    if not first(j, 1):
                        pe.wait_ge(prob_t_done, j)
                    for h in range(2):
                        for b in range(GB):
                            part = slice(SEQ * b, SEQ * b + SEQ)
                            last = nc.tensor.transpose(ps_t[0:SEQ, h, part], prob[u % NPR][0:SEQ, h, part],
                                                       ident[0:SEQ, 0:SEQ])
                    last.then_inc(turned, 1)
                s = stage(k, m, D_V, U, N)
                if s is not None:
                    j, u, kb = s
                    g = u % GROUPS
                    pe.wait_ge(prob_t_done, j + 1)
                    if not first(j, 1):
                        pe.wait_ge(o_done, j)
                    for b in range(GB):
                        for h in range(2):
                            last = nc.tensor.matmul(ps_o[64 * h:64 * h + 64, SEQ * b:SEQ * b + SEQ],
                                                    v[0:96, GB * g + b, :], prob_t[u % 2][0:96, h, SEQ * b:SEQ * b + SEQ],
                                                    start=True, stop=True)
                    last.then_inc(weighed, 1)

            run_steps(pe, N, DEPTH, U, body)

        @block.scalar
        def _(act):
            for i in range(1):
                act.wait_ge(w_in[0], 16)
                nc.scalar.activation(w_hi[0][:], w_raw[0][:], ACT.Copy).then_inc(w_hi_done, 1)

            def body(k, m):
                s = stage(k, m, 0, U, N)
                if s is not None:
                    j, u, kb = s
                    act.wait_ge(latent_made, j + 1)
                    if not first(j, 2):
                        act.wait_ge(scored, j - 1)
                    nc.scalar.activation(q_a[u % 2][0:64, :], ps_l[0:64, 0:GT], ACT.Copy)
                    nc.scalar.activation(q_b[u % 2][64:P, :], ps_l[64:P, 0:GT], ACT.Copy).then_inc(latent_done, 1)
                    s = weights_of(k, m)
                    if s is not None:
                        p, w, kb = s
                        act.wait_ge(w_in[w], 16 * kb + 16)
                        if not first(p, 2):
                            act.wait_ge(latent_made, GROUPS * (p - 1))
                        nc.scalar.activation(w_hi[w][:], w_raw[w][:], ACT.Copy).then_inc(w_hi_done, 1)
                s = stage(k, m, D_T, U, N)
                if s is not None:
                    j, u, kb = s
                    act.wait_ge(turned, j + 1)
                    if not first(j, 2):
                        act.wait_ge(weighed, j - 1)
                    nc.scalar.activation(prob_t[u % 2][0:SEQ, :, :], ps_t[0:SEQ, :, 0:GT],
                                         ACT.Copy).then_inc(prob_t_done, 1)
                s = stage(k, m, D_S, U, N)
                if s is not None:
                    j, u, kb = s
                    act.wait_ge(bias_done, j + 1)
                    for h in range(2):
                        for b in range(GB):
                            n = GB * h + b
                            part = slice(SEQ * b, SEQ * b + SEQ)
                            last = nc.scalar.activation(prob[u % NPR][0:SEQ, h, part], prob[u % NPR][0:SEQ, h, part], ACT.Exp,
                                                        bias=bias[u % 2][0:SEQ, n:n + 1], scale=SCALE,
                                                        accum_out=total[u % 2][0:SEQ, n:n + 1])
                    last.then_inc(exp_done, 1)

            act.wait_ge(zeroed, 3)
            run_steps(act, N, DEPTH, U, body, last=1)

        @block.vector
        def _(dve):
            for i in range(2):
                nc.vector.memset(prob_t[i][64:P], 0.0).then_inc(zeroed, 1)
            nc.vector.memset(zero[:], 0.0).then_inc(zeroed, 1)

            def split(w, p):
                dve.wait_ge(w_hi_done, p + 1)
                nc.vector.tensor_tensor(w_lo[w][:], w_raw[w][:], w_hi[w][:], ALU.subtract).then_inc(w_lo_done, 1)

            split(0, 0)

            def body(k, m):
                s = stage(k, m, 0, U, N)
                if s is not None:
                    j, u, kb = s
                    dve.wait_ge(rope_made, j + 1)
                    if not first(j, 1):
                        dve.wait_ge(rope_a_done, j)
                        dve.wait_ge(rope_b_done, j)
                    nc.vector.tensor_tensor(by_cos[:], ps_r[:, 0:GT], cos[:], ALU.mult)
                    nc.vector.stream_shuffle(swapped[:], ps_r[:, 0:GT], swap).then_inc(swap_done, 1)
                    s = weights_of(k, m)
                    if s is not None:
                        p, w, kb = s
                        split(w, p)
                s = stage(k, m, D_O, U, N)
                if s is not None:
                    j, u, kb = s
                    dve.wait_ge(weighed, j + 1)
                    if not first(j, 2):
                        dve.wait_ge(o_stored[u % 2], 16 * bodied(0, kb, u, 2))
                    nc.vector.tensor_copy(o_t[u % 2][:], ps_o[:, 0:GT]).then_inc(o_done, 1)
                s = stage(k, m, D_S, U, N)
                if s is not None:
                    j, u, kb = s
                    dve.wait_ge(scored, j + 1)
                    if not first(j, NPR):
                        dve.wait_ge(turned, j - NPR + 1)
                    p4 = prob[u % NPR][0:SEQ, :, :].rearrange("p h (b k) -> p h b k", b=GB)
                    nc.vector.tensor_tensor(p4, ps_s[0:SEQ, :, 0:GT].rearrange("p h (b k) -> p h b k", b=GB),
                                            mask[0:SEQ, :].unsqueeze(1).unsqueeze(1).broadcast_to((SEQ, 2, GB, SEQ)),
                                            ALU.add).then_inc(masked, 1)
                s = stage(k, m, 0, U, N)
                if s is not None:
                    j, u, kb = s
                    dve.wait_ge(sin_done, j + 1)
                    if not first(j, 2):
                        dve.wait_ge(scored, j - 1)
                    nc.vector.tensor_tensor(q_b[u % 2][0:64, :], by_cos[0:64, :], by_sin[0:64, :],
                                            ALU.add).then_inc(rope_b_done, 1)
                s = stage(k, m, D_S, U, N)
                if s is not None:
                    j, u, kb = s
                    p4 = prob[u % NPR][0:SEQ, :, :].rearrange("p h (b k) -> p h b k", b=GB)
                    dve.wait_ge(masked, j + 1)
                    nc.vector.tensor_reduce(top[0:SEQ, :].rearrange("p (h b) -> p h b", h=2), p4, AX.X,
                                            ALU.max).then_inc(top_done, 1)
                    dve.wait_ge(top_done, j + 1)
                    if not first(j, 2):
                        dve.wait_ge(exp_done, j - 1)
                    nc.vector.tensor_scalar(bias[u % 2][0:SEQ, :], top[0:SEQ, :], -SCALE, None,
                                            ALU.mult).then_inc(bias_done, 1)
                s = stage(k, m, D_N, U, N)
                if s is not None:
                    j, u, kb = s
                    dve.wait_ge(exp_done, j + 1)
                    if not first(j, 2):
                        dve.wait_ge(prob_done, j - 1)
                    nc.vector.reciprocal(share[u % 2][0:SEQ, :], total[u % 2][0:SEQ, :]).then_inc(share_done, 1)

            run_steps(dve, N, DEPTH, U, body, last=1)

        @block.gpsimd
        def _(pool):
            pool.wait_ge(zeroed, 3)
            pool.dma_start(d["o_t"][:, :, TOK:TOKP], zero[:]).then_inc(pad_stored, 16)

            def body(k, m):
                s = stage(k, m, 0, U, N)
                if s is not None:
                    j, u, kb = s
                    pool.wait_ge(swap_done, j + 1)
                    if not first(j, 1):
                        pool.wait_ge(rope_b_done, j)
                    nc.gpsimd.tensor_tensor(by_sin[:], swapped[:], sin[:], ALU.mult).then_inc(sin_done, 1)
                    pool.wait_ge(sin_done, j + 1)
                    if not first(j, 2):
                        pool.wait_ge(scored, j - 1)
                    nc.gpsimd.tensor_tensor(q_a[u % 2][64:P, :], by_cos[64:P, :], by_sin[64:P, :],
                                            ALU.add).then_inc(rope_a_done, 1)
                s = stage(k, m, D_N, U, N)
                if s is not None:
                    j, u, kb = s
                    pool.wait_ge(share_done, j + 1)
                    pool.wait_ge(rope_a_done, min(j + D_N + 1, N) if isinstance(j, int) else j + D_N + 1)
                    p4 = prob[u % NPR][0:SEQ, :, :].rearrange("p h (b k) -> p (h b) k", b=GB)
                    nc.gpsimd.tensor_tensor(p4, p4, share[u % 2][0:SEQ, :].unsqueeze(2).broadcast_to((SEQ, 8, SEQ)),
                                            ALU.mult).then_inc(prob_done, 1)

            run_steps(pool, N, DEPTH, U, body)
            pool.wait_ge(pad_stored, 16)


def attention_keys(nc, d, ident, k_t, k_tb, v, cos, sin, mask, swap):
    with ExitStack() as ctx:
        mem = Memory(nc, ctx, "keys")
        by_cos = mem.sb("by_cos", [P, TOK])
        swapped = mem.sb("swapped", [P, TOK])
        ps_v = [mem.ps(f"ps_v{i}", [P, 8, KR]) for i in range(4)]
        const_in = mem.sem("const_in")
        link_sem = mem.sem("link")
        v_made = mem.sem("v_made")
        v_zero = mem.sem("v_zero")
        done = mem.sem("done")
        block = ctx.enter_context(nc.Block())
        R = slice(64, P)

        @block.sync
        def _(sp):
            sp.dma_start(cos[:], d["cos"]).then_inc(const_in, 16)
            sp.dma_start(sin[:], d["sin"]).then_inc(const_in, 16)
            sp.dma_start(mask[:], d["mask"]).then_inc(const_in, 16)
            sp.wait_ge(const_in, 48)

        @block.vector
        def _(dve):
            link = Link(dve, link_sem, 0)
            nc.vector.memset(v[64:P], 0.0).then_inc(v_zero, 1)
            dve.wait_ge(const_in, 48)

            def over(x):
                return x.rearrange("p (g n) -> p g n", g=GROUPS)

            def table(x):
                return x.unsqueeze(1).broadcast_to((64, GROUPS, GT))

            link(nc.vector.stream_shuffle(swapped[R, :], k_t[R, 0:TOK], swap))
            link(nc.vector.tensor_tensor(over(swapped[R, :]), over(swapped[R, :]), table(sin[R, :]), ALU.mult))
            link(nc.vector.tensor_tensor(over(by_cos[R, :]), over(k_t[R, 0:TOK]), table(cos[R, :]), ALU.mult))
            nc.vector.tensor_tensor(k_t[R, 0:TOK], by_cos[R, :], swapped[R, :], ALU.add)
            nc.vector.tensor_tensor(k_tb[0:64, :], by_cos[R, :], swapped[R, :], ALU.add).then_inc(done, 1)

        @block.tensor
        def _(pe):
            for b in range(BATCH):
                last = nc.tensor.transpose(ps_v[b // 8][0:SEQ, b % 8, :], k_t[0:KR, SEQ * b:SEQ * b + SEQ],
                                           ident[0:KR, 0:KR])
            last.then_inc(v_made, 1)

        @block.scalar
        def _(act):
            nc.scalar.activation(k_tb[R, :], k_t[0:64, 0:TOK], ACT.Copy).then_inc(done, 1)
            act.wait_ge(v_made, 1)
            act.wait_ge(v_zero, 1)
            for i in range(4):
                nc.scalar.activation(v[0:SEQ, 8 * i:8 * i + 8, :], ps_v[i][0:SEQ], ACT.Copy).then_inc(done, 1)


def attn_out(nc, d, split, ident):
    CH = 4
    NC = PAIRS // CH
    with ExitStack() as ctx:
        mem = Memory(nc, ctx, "out")
        w_hi = mem.sb("w_hi", [P, PAIRS, DM], F32R)
        w_lo = mem.sb("w_lo", [P, PAIRS, DM], F32R)
        stage_w = [mem.sb(f"stage{i}", [P, DM]) for i in range(split.RING)]
        wvo = split.pieces(stage_w, [(d["wvo"][:, n, :], w_hi[:, n, :], w_lo[:, n, :], None) for n in range(PAIRS)])
        raw = [mem.sb(f"raw{c}", [P, CH, P]) for c in range(NC)]
        x_hi = [mem.sb(f"x_hi{c}", [P, CH, P], F32R) for c in range(NC)]
        x_lo = [mem.sb(f"x_lo{c}", [P, CH, P], F32R) for c in range(NC)]
        y = [mem.sb(f"y{i}", [P, DM]) for i in range(2)]
        h = [mem.sb(f"h{i}", [P, DM]) for i in range(2)]
        ps_h = [mem.ps(f"ps_h{i}", [P, DM]) for i in range(2)]
        raw_in = mem.sems("raw_in", NC)
        y_in = mem.sems("y_in", 2)
        hi_done = mem.sem("hi_done")
        lo_done = mem.sem("lo_done")
        x_used = mem.sem("x_used")
        h_done = mem.sem("h_done")
        h_stored = mem.stored("h_stored", 2)
        block = ctx.enter_context(nc.Block())
        DEPTH = 1

        @block.sync
        def _(sp):
            def body(k, m):
                s = stage(k, m, 0, 2, TILES)
                if s is None:
                    return
                t, b, kb = s
                for c in range(NC):
                    if not first(t, 1):
                        sp.wait_ge(lo_done, NC * t + (c - NC + 1))
                    sp.dma_start(raw[c][:], d["o_t"][:, CH * c:CH * c + CH, bass.ts(t, P)]).then_inc(raw_in[c], 16)
                    if first(t, 1):
                        for n in range(CH * c, CH * c + CH):
                            wvo.load(sp, n)
                if not first(t, 2):
                    sp.wait_ge(h_done, t - 1)
                sp.dma_start(y[b][:], d["y"][t]).then_inc(y_in[b], 16)

            run_steps(sp, TILES, DEPTH, 2, body)

        @block.scalar
        def _(act):
            def body(k, m):
                s = stage(k, m, 0, 2, TILES)
                if s is None:
                    return
                t, b, kb = s
                for c in range(NC):
                    act.wait_ge(raw_in[c], 16 * t + 16)
                    if not first(t, 1):
                        act.wait_ge(x_used, NC * t + (c - NC + 1))
                    nc.scalar.activation(x_hi[c][:], raw[c][:], ACT.Copy).then_inc(hi_done, 1)
                    if first(t, 1):
                        for n in range(CH * c, CH * c + CH):
                            wvo.split_hi(act, n)

            run_steps(act, TILES, DEPTH, 2, body)

        @block.vector
        def _(dve):
            def body(k, m):
                s = stage(k, m, 0, 2, TILES)
                if s is not None:
                    t, b, kb = s
                    for c in range(NC):
                        dve.wait_ge(hi_done, NC * t + c + 1)
                        nc.vector.tensor_tensor(x_lo[c][:], raw[c][:], x_hi[c][:], ALU.subtract).then_inc(lo_done, 1)
                        if first(t, 1):
                            for n in range(CH * c, CH * c + CH):
                                wvo.split_lo(dve, n)
                s = stage(k, m, 1, 2, TILES)
                if s is not None:
                    t, b, kb = s
                    dve.wait_ge(x_used, NC * t + NC)
                    dve.wait_ge(y_in[b], 16 * kb + 16)
                    if not first(t, 2):
                        dve.wait_ge(h_stored[b], 16 * kb)
                    nc.vector.tensor_tensor(h[b][:], ps_h[b][:], y[b][:], ALU.add).then_inc(h_done, 1)

            run_steps(dve, TILES, DEPTH, 2, body)

        @block.tensor
        def _(pe):
            def body(k, m):
                s = stage(k, m, 0, 2, TILES)
                if s is None:
                    return
                t, b, kb = s
                outs = [ps_h[b][:, 0:512], ps_h[b][:, 512:1024]]
                if not first(t, 2):
                    pe.wait_ge(h_done, t - 1)
                for c in range(NC):
                    pe.wait_ge(lo_done, NC * t + c + 1)
                    for j in range(CH):
                        n = CH * c + j
                        if first(t, 1):
                            wvo.wait(pe, n)
                        last = three_pass(nc, outs, x_hi[c][:, j, :], x_lo[c][:, j, :],
                                          [w_hi[:, n, 0:512], w_hi[:, n, 512:1024]],
                                          [w_lo[:, n, 0:512], w_lo[:, n, 512:1024]], n == 0, n == PAIRS - 1)
                    last.then_inc(x_used, 1)

            run_steps(pe, TILES, DEPTH, 2, body)

        @block.gpsimd
        def _(pool):
            def body(k, m):
                s = stage(k, m, 1, 2, TILES)
                if s is None:
                    return
                t, b, kb = s
                pool.wait_ge(h_done, t + 1)
                pool.dma_start(d["h"][t], h[b][:]).then_inc(h_stored[b], 16)

            run_steps(pool, TILES, DEPTH, 2, body)
            for b in range(2):
                pool.wait_ge(h_stored[b], 16 * TILES // 2)


ER = EXP * RANK
FW = DM + ER + NR + 1
CUT = [0, 390, 780, FW]
A_AT = DM - CUT[2]
R_AT = A_AT + ER


def ffn(nc, d, split, ident):
    with ExitStack() as ctx:
        mem = Memory(nc, ctx, "ffn")
        w_hi = mem.sb("w_hi", [P, KM, FW], F32R)
        w_lo = mem.sb("w_lo", [P, KM, FW], F32R)
        b_hi = mem.sb("b_hi", [P, 1, DM], F32R)
        b_lo = mem.sb("b_lo", [P, 1, DM], F32R)
        stage_w = [mem.sb(f"stage{i}", [P, FW]) for i in range(split.RING)]
        wf = split.pieces(stage_w, [(d["wf"][:, n, :], w_hi[:, n, :], w_lo[:, n, :], None) for n in range(KM)] +
                          [(d["lora_b"][:, 0, :], b_hi[:, 0, :], b_lo[:, 0, :], None)])
        bias = mem.sb("bias", [P, DM])
        rbias = mem.sb("rbias", [P, NR])
        lower = mem.sb("lower", [P, NR, NR])
        numbers = mem.sb("numbers", [P, EXP, NR])
        emap = mem.sb("emap", [P, NR], I32)
        emapf = mem.sb("emapf", [P, NR])
        place = mem.sb("place", [P, EXP, NR])
        h = [mem.sb(f"h{i}", [P, DM]) for i in range(3)]
        res = [mem.sb(f"res{i}", [P, DM]) for i in range(3)]
        o = [mem.sb(f"o{i}", [P, DM]) for i in range(2)]
        xn = [mem.sb(f"xn{i}", [P, DM]) for i in range(2)]
        xt_hi = [mem.sb(f"xt_hi{i}", [P, KM, P], F32R) for i in range(2)]
        xt_lo = [mem.sb(f"xt_lo{i}", [P, KM, P], F32R) for i in range(2)]
        bn = mem.sb("bn", [P, 12])
        vec = mem.sb("vec", [P, 16])
        lg = mem.sb("lg", [P, NR])
        ex = mem.sb("ex", [P, NR])
        pr = mem.sb("pr", [P, NR])
        over = mem.sb("over", [P, NR, NR])
        tie = mem.sb("tie", [P, NR, NR])
        rank = mem.sb("rank", [P, NR])
        kept = mem.sb("kept", [P, NR])
        pick = mem.sb("pick", [P, EXP, NR])
        we = mem.sb("we", [P, EXP])
        hw = mem.sb("hw", [P, ER])
        ht_hi = mem.sb("ht_hi", [P, P], F32R)
        ht_lo = mem.sb("ht_lo", [P, P], F32R)
        ps_o = [[mem.ps(f"ps_o{i}_{c}", [P, 512]) for c in range(3)] for i in range(2)]
        ps_x = [mem.ps(f"ps_x{i}", [P, 4, P]) for i in range(2)]
        const_in = mem.sem("const_in")
        h_in = mem.sems("h_in", 3)
        xn_done = mem.sem("xn_done")
        x_turned = mem.sem("x_turned")
        xhi_done = mem.sem("xhi_done")
        xlo_done = mem.sem("xlo_done")
        base_made = mem.sem("base_made")
        logits_done = mem.sem("logits_done")
        exp_done = mem.sem("exp_done")
        hw_done = mem.sem("hw_done")
        hw_turned = mem.sem("hw_turned")
        hhi_done = mem.sem("hhi_done")
        hlo_done = mem.sem("hlo_done")
        lora_made = mem.sem("lora_made")
        res_done = mem.sem("res_done")
        o_done = mem.sem("o_done")
        o_stored = mem.stored("o_stored", 2)
        link_sem = mem.sem("link")
        block = ctx.enter_context(nc.Block())
        D_X, D_M, D_L = 1, 2, 3
        DEPTH = 4
        U = 6

        def nth(kb, u, per):
            return kb * (U // per) + u // per + 1

        @block.sync
        def _(sp):
            for dst, name in ((bias, "base_b"), (rbias, "router_b"), (lower, "lower"), (numbers, "numbers"),
                              (emap, "emap")):
                sp.dma_start(dst[:], d[name]).then_inc(const_in, 16)

            def body(k, m):
                s = stage(k, m, 0, U, TILES)
                if s is None:
                    return
                t, u, kb = s
                if not first(t, 3):
                    sp.wait_ge(res_done, t - 2)
                    sp.wait_ge(xn_done, t - 2)
                sp.dma_start(h[u % 3][:], d["h"][t]).then_inc(h_in[u % 3], 16)
                if first(t, 1):
                    for n in range(KM + 1):
                        wf.load(sp, n)

            run_steps(sp, TILES, DEPTH, U, body)

        @block.gpsimd
        def _(pool):
            pool.wait_ge(const_in, 80)

            def body(k, m):
                s = stage(k, m, 0, U, TILES)
                if s is not None:
                    t, u, kb = s
                    pool.wait_ge(h_in[u % 3], 16 * nth(kb, u, 3))
                    if not first(t, 3):
                        pool.wait_ge(o_done, t - 2)
                    nc.gpsimd.tensor_tensor(res[u % 3][:], h[u % 3][:], bias[:], ALU.add).then_inc(res_done, 1)
                s = stage(k, m, D_L + 1, U, TILES)
                if s is not None:
                    t, u, kb = s
                    pool.wait_ge(o_done, t + 1)
                    pool.dma_start(d["out"][t], o[u % 2][:]).then_inc(o_stored[u % 2], 16)

            run_steps(pool, TILES, DEPTH, U, body)
            for b in range(2):
                pool.wait_ge(o_stored[b], 16 * TILES // 2)

        @block.scalar
        def _(act):
            for n in range(KM + 1):
                wf.split_hi(act, n)

            def body(k, m):
                s = stage(k, m, D_L, U, TILES)
                if s is not None:
                    t, u, kb = s
                    act.wait_ge(logits_done, t + 1)
                    nc.scalar.activation(ex[:], lg[:], ACT.Exp, bias=vec[:, 4:5],
                                         accum_out=vec[:, 5:6]).then_inc(exp_done, 1)
                    act.wait_ge(hw_turned, t + 1)
                    if not first(t, 1):
                        act.wait_ge(lora_made, t)
                    nc.scalar.activation(ht_hi[:], ps_x[0][:, 0, :], ACT.Copy).then_inc(hhi_done, 1)
                s = stage(k, m, D_X, U, TILES)
                if s is not None:
                    t, u, kb = s
                    if not first(t, 2):
                        act.wait_ge(base_made, t - 1)
                    for c in range(2):
                        act.wait_ge(x_turned, 2 * t + c + 1)
                        nc.scalar.activation(xt_hi[u % 2][:, 4 * c:4 * c + 4, :], ps_x[c][:],
                                             ACT.Copy).then_inc(xhi_done, 1)

            run_steps(act, TILES, DEPTH, U, body)

        @block.vector
        def _(dve):
            link = Link(dve, link_sem, 0)
            PER = INV_SQRT_LINKS + 4 + 11
            link.per_step = PER
            dve.wait_ge(const_in, 80)
            link.step(0)
            link(nc.vector.tensor_copy(emapf[:], emap[:]))
            link(nc.vector.tensor_tensor(place[:], emapf[:].unsqueeze(1).broadcast_to((P, EXP, NR)), numbers[:],
                                         ALU.is_equal))
            link(nc.vector.tensor_scalar(place[:], place[:], 2.0, None, ALU.mult))
            START = link.n

            def body(k, m):
                s = stage(k, m, D_L, U, TILES)
                if s is not None:
                    t, u, kb = s
                    ps = ps_o[u % 2][2]
                    dve.wait_ge(base_made, t + 1)
                    link(nc.vector.tensor_tensor(lg[:], ps[:, R_AT:R_AT + NR], rbias[:], ALU.add))
                    link(nc.vector.tensor_reduce(vec[:, 3:4], lg[:], AX.X, ALU.max))
                    nc.vector.tensor_scalar(vec[:, 4:5], vec[:, 3:4], -1.0, None, ALU.mult).then_inc(logits_done, 1)
                    dve.wait_ge(exp_done, t + 1)
                    link(nc.vector.reciprocal(vec[:, 6:7], vec[:, 5:6]))
                    link(nc.vector.tensor_scalar(pr[:], ex[:], vec[:, 6:7], None, ALU.mult))
                    pj = pr[:].unsqueeze(1).broadcast_to((P, NR, NR))
                    pi = pr[:].unsqueeze(2).broadcast_to((P, NR, NR))
                    nc.vector.tensor_tensor(over[:], pj, pi, ALU.is_gt)
                    link(nc.vector.tensor_tensor(tie[:], pj, pi, ALU.is_equal))
                    link(nc.vector.tensor_tensor(tie[:], tie[:], lower[:], ALU.mult))
                    link(nc.vector.tensor_tensor(over[:], over[:], tie[:], ALU.add))
                    link(nc.vector.tensor_reduce(rank[:], over[:], AX.X, ALU.add))
                    link(nc.vector.scalar_tensor_tensor(kept[:], rank[:], float(EXP) - 0.5, pr[:], ALU.is_lt, ALU.mult))
                    link(nc.vector.tensor_tensor(pick[:], kept[:].unsqueeze(1).broadcast_to((P, EXP, NR)), place[:],
                                                 ALU.mult))
                    if not first(t, 1):
                        dve.wait_ge(hw_turned, t)
                    nc.vector.tensor_reduce(we[:], pick[:], AX.X, ALU.add).then_inc(link_sem, 1)
                    link.n += 1
                    dve.wait_ge(link_sem, link.base + link.n)
                    nc.vector.tensor_tensor(hw[:].rearrange("p (e r) -> p e r", e=EXP),
                                            ps[:, A_AT:A_AT + ER].rearrange("p (e r) -> p e r", e=EXP),
                                            we[:].unsqueeze(2).broadcast_to((P, EXP, RANK)), ALU.mult).then_inc(hw_done, 1)
                s = stage(k, m, 0, U, TILES)
                if s is not None:
                    t, u, kb = s
                    hh = h[u % 3]
                    dve.wait_ge(h_in[u % 3], 16 * nth(kb, u, 3))
                    nc.vector.bn_stats(bn[:, 0:6], hh[:, 0:512])
                    link(nc.vector.bn_stats(bn[:, 6:12], hh[:, 512:1024]))
                    link.settle()
                    link(nc.vector.bn_aggr(vec[:, 8:10], bn[:]))
                    link(nc.vector.tensor_scalar(vec[:, 10:11], vec[:, 9:10], LN_EPS, None, ALU.add))
                    inv_sqrt(nc, link, vec[:, 10:11], vec[:, 11:12], vec[:, 12:13])
                    if not first(t, 2):
                        dve.wait_ge(x_turned, 2 * t - 2)
                    nc.vector.tensor_scalar(xn[u % 2][:], hh[:], vec[:, 8:9], vec[:, 11:12], ALU.subtract,
                                            ALU.mult).then_inc(xn_done, 1)
                    if first(t, 1):
                        for n in range(KM + 1):
                            wf.split_lo(dve, n)
                s = stage(k, m, D_L, U, TILES)
                if s is not None:
                    t, u, kb = s
                    dve.wait_ge(hhi_done, t + 1)
                    nc.vector.tensor_tensor(ht_lo[:], ps_x[0][:, 0, :], ht_hi[:], ALU.subtract).then_inc(hlo_done, 1)
                    dve.wait_ge(lora_made, t + 1)
                    dve.wait_ge(res_done, t + 1)
                    if not first(t, 2):
                        dve.wait_ge(o_stored[u % 2], 16 * nth(kb, u, 2) - 16)
                    for c in range(3):
                        a, e = CUT[c], min(CUT[c + 1], DM)
                        last = nc.vector.tensor_tensor(o[u % 2][:, a:e], ps_o[u % 2][c][:, 0:e - a],
                                                       res[u % 3][:, a:e], ALU.add)
                    last.then_inc(o_done, 1)
                s = stage(k, m, D_X, U, TILES)
                if s is not None:
                    t, u, kb = s
                    for c in range(2):
                        dve.wait_ge(xhi_done, 2 * t + c + 1)
                        nc.vector.tensor_tensor(xt_lo[u % 2][:, 4 * c:4 * c + 4, :], ps_x[c][:],
                                                xt_hi[u % 2][:, 4 * c:4 * c + 4, :], ALU.subtract).then_inc(xlo_done, 1)

            def step(k, m):
                link.step(k * U + m)
                link.base = link.base + START
                body(k, m)
                link.fill()

            run_steps(dve, TILES, DEPTH, U, step)

        @block.tensor
        def _(pe):
            def base(s, half):
                t, u, kb = s
                for n in range(4 * half, 4 * half + 4):
                    if n % 4 == 0:
                        pe.wait_ge(xlo_done, 2 * t + half + 1)
                    if first(t, 1):
                        wf.wait(pe, n)
                    last = three_pass(nc, [ps_o[u % 2][c][:, 0:CUT[c + 1] - CUT[c]] for c in range(3)],
                                      xt_hi[u % 2][:, n, :], xt_lo[u % 2][:, n, :],
                                      [w_hi[:, n, CUT[c]:CUT[c + 1]] for c in range(3)],
                                      [w_lo[:, n, CUT[c]:CUT[c + 1]] for c in range(3)], n == 0, n == KM - 1)
                if half:
                    last.then_inc(base_made, 1)

            def body(k, m):
                s = stage(k, m, D_M, U, TILES)
                if s is not None:
                    if not first(s[0], 2):
                        pe.wait_ge(o_done, s[0] - 1)
                    base(s, 0)
                sl = stage(k, m, D_L, U, TILES)
                if sl is not None:
                    t, u, kb = sl
                    pe.wait_ge(hw_done, t + 1)
                    if isinstance(t, int):
                        pe.wait_ge(xlo_done, min(2 * t + 4, 2 * TILES))
                    else:
                        pe.wait_ge(xlo_done, 2 * t + 4)
                    nc.tensor.transpose(ps_x[0][:, 0, :], hw[:], ident[:]).then_inc(hw_turned, 1)
                if s is not None:
                    base(s, 1)
                if sl is not None:
                    t, u, kb = sl
                    pe.wait_ge(hlo_done, t + 1)
                    if first(t, 1):
                        wf.wait(pe, KM)
                    ends = [(CUT[c], min(CUT[c + 1], DM)) for c in range(3)]
                    last = three_pass(nc, [ps_o[u % 2][c][:, 0:e - a] for c, (a, e) in enumerate(ends)], ht_hi[:],
                                      ht_lo[:], [b_hi[:, 0, a:e] for a, e in ends], [b_lo[:, 0, a:e] for a, e in ends],
                                      False, True, onto=True)
                    last.then_inc(lora_made, 1)
                s = stage(k, m, D_X, U, TILES)
                if s is not None:
                    t, u, kb = s
                    pe.wait_ge(xn_done, t + 1)
                    if sl is not None:
                        pe.wait_ge(hlo_done, sl[0] + 1)
                    for c in range(2):
                        if not first(t, 1):
                            pe.wait_ge(xlo_done, 2 * t + (c - 1))
                        for j in range(4):
                            n = 4 * c + j
                            last = nc.tensor.transpose(ps_x[c][:, j, :], xn[u % 2][:, P * n:P * n + P], ident[:])
                        last.then_inc(x_turned, 1)

            run_steps(pe, TILES, DEPTH, U, body)


def build(nc, d):
    with ExitStack() as ctx:
        Memory.whole = ctx
        mem = Memory(nc, ctx, "all")
        ident = mem.sb("ident", [P, P])
        ident_in = mem.sem("ident_in")
        with nc.Block() as block:
            @block.sync
            def _(sp):
                sp.dma_start(ident[:], d["ident"]).then_inc(ident_in, 16)
                sp.wait_ge(ident_in, 16)
        split = Splitter(nc)
        tok_up(nc, d, split, ident)
        with ExitStack() as kept:
            mem = Memory(nc, kept, "kept")
            qn_hi = mem.sb("qn_hi", [P, 2, TOKP], F32R)
            qn_lo = mem.sb("qn_lo", [P, 2, TOKP], F32R)
            k_t = mem.sb("k_t", [P, TOKP])
            tok_down(nc, d, split, ident, qn_hi, qn_lo, k_t)
            attention(nc, d, ident, qn_hi, qn_lo, k_t)
        attn_out(nc, d, split, ident)
        ffn(nc, d, split, ident)


def rope_tables():
    dim, base, factor, orig = RO, 10000.0, 128.0, 2048

    def corr(rot):
        return dim * math.log(orig / (rot * 2 * math.pi)) / (2 * math.log(base))

    low, high = max(math.floor(corr(32.0)), 0), min(math.ceil(corr(1.0)), dim - 1)
    hi = high + 0.001 if low == high else float(high)
    ramp = np.clip((np.arange(dim // 2, dtype=np.float32) - low) / (hi - low), 0.0, 1.0)
    keep = 1.0 - ramp
    extra = 1.0 / base ** (np.arange(0, dim, 2, dtype=np.float32) / dim)
    freq = extra / factor * (1.0 - keep) + extra * keep
    angle = np.outer(np.arange(512, dtype=np.float32), freq)[:SEQ]
    row = np.arange(P) % RO
    cos = np.cos(angle)[:, row // 2].T
    sin = np.sin(angle)[:, row // 2].T * np.where(row % 2 == 0, -1.0, 1.0)[:, None]
    return (np.ascontiguousarray(np.tile(cos, (1, GB)), dtype=np.float32),
            np.ascontiguousarray(np.tile(sin, (1, GB)), dtype=np.float32))


def blocks(w):
    return w.reshape(-1, P, w.shape[1]).transpose(1, 0, 2)


def kernel(x, L0_tok_w1, L0_tok_w2, L0_tok_ln_pre_w, L0_tok_ln_post_w, L0_attn_wq_a, L0_attn_q_a_ln_w,
           L0_attn_wq_b, L0_attn_wkv_a, L0_attn_kv_a_ln_w, L0_attn_wkv_b, L0_attn_wo, L0_ffn_base_W,
           L0_ffn_base_b, L0_ffn_router_W, L0_ffn_router_b, L0_ffn_A, L0_ffn_B, L0_ffn_expert_map):
    import concourse.bacc as bacc
    from concourse.bass_utils import run_bass_kernel_spmd

    f32 = np.float32
    rows = np.zeros((BATCH, SEQ * 8, 320), f32)
    rows[:, :750] = np.asarray(x)
    flat = np.zeros((TOKP, DIN), f32)
    flat[:TOK] = rows.reshape(TOK, DIN)
    x_rows = flat.reshape(TILES, P, DIN)
    x_t = x_rows.reshape(TILES, P, KIN, P).transpose(0, 3, 2, 1)

    wq_b = np.asarray(L0_attn_wq_b).reshape(PAIRS, 2, NOPE + RO, QR)
    wkv_b = np.asarray(L0_attn_wkv_b).reshape(PAIRS, 2, NOPE + VD, KR)
    wq_rope = wq_b[:, ::-1, NOPE:, :]
    wq_rope = wq_rope.reshape(PAIRS, 2 * RO, 2, P).transpose(0, 3, 2, 1)
    wo = np.asarray(L0_attn_wo).T.reshape(PAIRS, 2, VD, DM).transpose(0, 2, 1, 3)
    wf = np.zeros((DM, FW), f32)
    wf[:, :DM] = np.asarray(L0_ffn_base_W).T
    wf[:, DM:DM + ER] = np.asarray(L0_ffn_A).reshape(ER, DM).T
    wf[:, DM + ER:DM + ER + NR] = np.asarray(L0_ffn_router_W).T
    cos, sin = rope_tables()
    q, key = np.arange(SEQ)[:, None], np.arange(SEQ)[None, :]
    mask = np.zeros((P, SEQ), f32)
    mask[:SEQ] = np.where(key <= q, 0.0, MASKED)
    i, j = np.arange(NR)[:, None], np.arange(NR)[None, :]

    def on_all(a):
        return np.broadcast_to(np.asarray(a)[None], (P, *np.asarray(a).shape))

    arrays = {
        "x_rows": x_rows,
        "x_t": x_t,
        "w1": blocks(np.asarray(L0_tok_w1).T),
        "pre_ln": np.asarray(L0_tok_ln_pre_w).reshape(KIN, P).T,
        "w2": blocks(np.asarray(L0_tok_w2).T),
        "post_ln": on_all(L0_tok_ln_post_w),
        "wa": blocks(np.concatenate([np.asarray(L0_attn_wq_a).T, np.asarray(L0_attn_wkv_a).T], axis=1)),
        "q_ln": np.asarray(L0_attn_q_a_ln_w).reshape(2, P).T,
        "kv_ln": on_all(L0_attn_kv_a_ln_w),
        "wq_nope": wq_b[:, :, :NOPE].reshape(PAIRS, P, QR),
        "wq_rope": wq_rope,
        "wk": wkv_b[:, :, :NOPE].reshape(PAIRS, P, KR),
        "wv": wkv_b[:, :, NOPE:].transpose(0, 2, 1, 3),
        "wo": wo,
        "wf": blocks(wf),
        "lora_b": np.asarray(L0_ffn_B).transpose(0, 2, 1).reshape(P, 1, DM),
        "base_b": on_all(L0_ffn_base_b),
        "router_b": on_all(L0_ffn_router_b),
        "emap": on_all(np.asarray(L0_ffn_expert_map)),
        "cos": cos,
        "sin": sin,
        "mask": mask,
        "ident": np.eye(P, dtype=f32),
        "lower": on_all((j < i).astype(f32)),
        "numbers": on_all(np.tile(np.arange(EXP, dtype=f32)[:, None], (1, NR))),
    }
    arrays = {n: np.ascontiguousarray(a) for n, a in arrays.items()}
    nc = bacc.Bacc("TRN2", target_bir_lowering=False, num_devices=1)
    d = {n: nc.dram_tensor(n, a.shape, mybir.dt.from_np(a.dtype), kind="ExternalInput").ap()
         for n, a in arrays.items()}
    for n, shape in (("wq_pair", (PAIRS, P, 2, 2 * P)), ("wvo", (P, PAIRS, DM)), ("g_t", (TILES, P, HID)),
                     ("y", (TILES, P, DM)), ("o_t", (P, PAIRS, TOKP)), ("h", (TILES, P, DM))):
        d[n] = nc.dram_tensor(n, shape, F32, kind="Internal").ap()
    d["out"] = nc.dram_tensor("out", (TILES, P, DM), F32, kind="ExternalOutput").ap()
    build(nc, d)
    r = run_bass_kernel_spmd(nc, [arrays], core_ids=[0])
    return r.results[0]["out"].reshape(TOKP, DM)[:TOK].reshape(BATCH, SEQ, DM)
```

```python
import math
from contextlib import ExitStack

import numpy as np

import concourse.bass as bass
from concourse import mybir

F32 = mybir.dt.float32
F32R = mybir.dt.float32r
BF16 = mybir.dt.bfloat16
I32 = mybir.dt.int32
ALU = mybir.AluOpType
ACT = mybir.ActivationFunctionType
AX = mybir.AxisListType

P = 128
BATCH, SEQ = 32, 94
TOK = BATCH * SEQ
TILES = -(-TOK // P)
TOKP = TILES * P
DIN = 2560
KIN = DIN // P
HID = 512
DM = 1024
KM = DM // P
QR, KR, RO = 256, 64, 64
NH = 32
PAIRS = NH // 2
NOPE, VD = 64, 128
GROUPS, GB = 8, 4
GT = GB * SEQ
EXP, RANK = 8, 16
NR = 2 * EXP - 1
RMS_EPS, LN_EPS = 1e-6, 1e-5
SCALE = float((NOPE + RO) ** -0.5 * (0.1 * math.log(128.0) + 1.0) ** 2)
KCH = 5
NCH = KIN // KCH
SPARE = 1
MASKED = -1.0e30


def stage(k, m, d, unroll, n):
    place = (m - d) % unroll
    body = k + (m - d - place) // unroll
    item = body * unroll + place
    if isinstance(k, int) and not 0 <= item < n:
        return None
    return item, place, body


def first(item, n):
    return isinstance(item, int) and item < n


def run_steps(eng, n, depth, unroll, body, last=0):
    peel = -(-(depth + 2) // unroll)
    for k in range(peel):
        for m in range(unroll):
            body(k, m)
    with eng.Fori(peel, n // unroll - last) as k:
        for m in range(unroll):
            body(k, m)
    for k in range(n // unroll - last, n // unroll):
        for m in range(unroll):
            body(k, m)
    for s in range(n, n + depth):
        body(s // unroll, s % unroll)


class Link:

    def __init__(self, eng, sem, per_step):
        self.eng, self.sem, self.per_step = eng, sem, per_step
        self.base, self.n = 0, 0

    def step(self, number):
        self.base, self.n = number * self.per_step, 0

    def __call__(self, ins):
        self.n += 1
        ins.then_inc(self.sem, 1)
        self.eng.wait_ge(self.sem, self.base + self.n)

    def settle(self):
        self.n += 1
        self.eng.sem_inc(self.sem, 1)

    def fill(self):
        left = self.per_step - self.n
        assert left >= 0, self.n
        if left:
            self.eng.sem_inc(self.sem, left)


def newton(nc, link, w, y, t):
    link(nc.vector.scalar_tensor_tensor(t, y, y, w, ALU.mult, ALU.mult))
    link(nc.vector.scalar_tensor_tensor(y, t, 1.5, y, ALU.add, ALU.mult))


def inv_sqrt(nc, link, v, w, y, t):
    vi, yi = v.bitcast(I32), y.bitcast(I32)
    nc.vector.tensor_scalar(w, v, -0.5, None, ALU.mult)
    link(nc.vector.tensor_scalar(yi, vi, 1, None, ALU.arith_shift_right))
    link(nc.vector.tensor_scalar(yi, yi, -1, 0x5F3759DF, ALU.mult, ALU.add))
    for _ in range(3):
        newton(nc, link, w, y, t)


INV_SQRT_LINKS = 8


class Memory:

    whole = None

    def __init__(self, nc, ctx, name):
        self.nc, self.ctx, self.name = nc, ctx, name

    def sb(self, name, shape, dt=F32):
        return self.ctx.enter_context(self.nc.sbuf_tensor(f"{self.name}_{name}", shape, dt))

    def ps(self, name, shape, dt=F32):
        return self.ctx.enter_context(self.nc.psum_tensor(f"{self.name}_{name}", shape, dt))

    def sem(self, name):
        return self.ctx.enter_context(self.nc.semaphore(f"{self.name}_{name}"))

    def stored(self, name, n):
        return [Memory.whole.enter_context(self.nc.semaphore(f"{self.name}_{name}{i}")) for i in range(n)]

    def sems(self, name, n):
        return [self.sem(f"{name}{i}") for i in range(n)]


class Splitter:

    RING = 4
    MOST = 8

    def __init__(self, nc):
        self.nc = nc
        mem = Memory(nc, Memory.whole, "split")
        self.loaded = mem.sems("loaded", self.MOST)
        self.hi_done = mem.sem("hi_done")
        self.lo_done = mem.sem("lo_done")
        self.loads = [0] * self.MOST
        self.done = 0

    def pieces(self, raw, sources):
        part = WeightPieces()
        part.of, part.raw, part.sources = self, raw, sources
        part.before, part.loads, part.ring = self.done, list(self.loads), len(raw)
        self.done += len(sources)
        assert part.before % self.RING == 0
        for n in range(len(sources)):
            self.loads[n % len(raw)] += 16
        return part


class WeightPieces:
    def into(self, parts):
        self.parts = parts

    def load(self, sp, n):
        split = self.before + n - self.ring + 1
        if split > 0:
            sp.wait_ge(self.of.lo_done, split)
        sp.dma_start(self.at(n), self.sources[n]).then_inc(self.of.loaded[n % self.ring], 16)

    def at(self, n):
        return self.raw[n % self.ring][:, 0:self.sources[n].shape[-1]]

    def split_hi(self, act, n):
        hi, _, factor = self.parts[n]
        r = self.ring
        act.wait_ge(self.of.loaded[n % r], self.loads[n % r] + 16 * (n // r + 1))
        by = {} if factor is None else {"scale": factor}
        self.of.nc.scalar.activation(hi, self.at(n), ACT.Copy, **by).then_inc(self.of.hi_done, 1)

    def split_lo(self, dve, n):
        hi, lo, factor = self.parts[n]
        nc = self.of.nc
        dve.wait_ge(self.of.hi_done, self.before + n + 1)
        if factor is None:
            ins = nc.vector.tensor_tensor(lo, self.at(n), hi, ALU.subtract)
        else:
            ins = nc.vector.scalar_tensor_tensor(lo, self.at(n), factor, hi, ALU.mult, ALU.subtract)
        ins.then_inc(self.of.lo_done, 1)

    def wait(self, eng, n):
        eng.wait_ge(self.of.lo_done, self.before + n + 1)


def three_pass(nc, outs, xhi, xlo, his, los, start, stop, onto=False):
    for x, ws, a, b in ((xlo, his, start, False), (xhi, los, False, False), (xhi, his, False, stop)):
        for o, w in zip(outs, ws):
            last = nc.tensor.matmul(o, x, w, start=a, stop=b, skip_group_check=onto)
    return last


def tok_up(nc, d, split, ident):
    with ExitStack() as ctx:
        mem = Memory(nc, ctx, "up")
        w_hi = mem.sb("w_hi", [P, KIN, 2 * HID], F32R)
        w_lo = mem.sb("w_lo", [P, KIN, 2 * HID], F32R)
        CW = KCH * P
        raw = [mem.sb(f"raw{c}", [P, KCH, P]) for c in range(NCH)]
        x_hi = [mem.sb(f"x_hi{c}", [P, KCH, P], F32R) for c in range(NCH)]
        x_lo = [mem.sb(f"x_lo{c}", [P, KCH, P], F32R) for c in range(NCH)]
        xs = [mem.sb(f"xs{i}", [P, CW]) for i in range(2)]
        junk = mem.sb("junk", [P, CW], BF16)
        ssq = mem.sb("ssq", [P, NCH])
        r = [mem.sb(f"r{i}", [P, 1]) for i in range(2)]
        var = mem.sb("var", [P, 3])
        sil = [mem.sb(f"sil{i}", [P, HID]) for i in range(2)]
        g = sil
        gt = [mem.sb(f"gt{i}", [P, HID]) for i in range(2)]
        fac = mem.sb("fac", [P, KIN])
        spare = [mem.sb(f"spare{i}", [P, HID]) for i in range(SPARE)]
        halves = [(n, slice(a, a + HID)) for n in range(KIN) for a in (0, HID)]
        w1 = split.pieces([*sil, *gt, *spare], [d["w1"][:, n, a] for n, a in halves])
        w1.into([(w_hi[:, n, a], w_lo[:, n, a], fac[:, n:n + 1]) for n, a in halves])
        PER = 2 * KCH
        ps_h = [mem.ps(f"ps_h{i}", [P, 2 * HID]) for i in range(2)]
        ps_t = [mem.ps(f"ps_t{i}", [P, HID]) for i in range(2)]
        raw_in = mem.sems("raw_in", NCH)
        xs_in = mem.sems("xs_in", 2)
        hi_done = mem.sem("hi_done")
        lo_done = mem.sem("lo_done")
        x_used = mem.sem("x_used")
        sq_done = mem.sem("sq_done")
        r_done = mem.sem("r_done")
        sil_done = mem.sem("sil_done")
        g_done = mem.sem("g_done")
        t_done = mem.sem("t_done")
        gt_done = mem.sem("gt_done")
        gt_stored = mem.sems("gt_stored", 2)
        link_sem = mem.sem("link")
        fac_in = mem.sem("fac_in")
        ident_in = mem.sem("ident_in")
        block = ctx.enter_context(nc.Block())
        DEPTH = 1

        @block.sync
        def _(sp):
            def body(k, m):
                s = stage(k, m, 0, 2, TILES)
                if s is not None:
                    load(s[0])
                s = stage(k, m, 1, 2, TILES)
                if s is not None:
                    t, b, _ = s
                    sp.wait_ge(gt_done, t + 1)
                    sp.dma_start(d["g_t"][t], gt[b][:]).then_inc(gt_stored[b], 16)

            def load(t):
                for c in range(NCH):
                    if not first(t, 1):
                        sp.wait_ge(lo_done, 4 * t + (c - 3))
                    sp.dma_start(raw[c][:], d["x_t"][t, :, KCH * c:KCH * c + KCH, :]).then_inc(raw_in[c], 16)
                    if first(t, 1) and c == 0:
                        sp.dma_start(fac[:], d["pre_ln"]).then_inc(fac_in, 16)
                        sp.dma_start(ident[:], d["ident"]).then_inc(ident_in, 16)
                    if not (first(t, 1) and c < 2):
                        sp.wait_ge(sq_done, 4 * t + (c - 1))
                    if first(t, 1):
                        for n in range(PER * c, PER * c + PER):
                            w1.load(sp, n)
                    sp.dma_start(xs[c % 2][:], d["x_rows"][t, :, CW * c:CW * c + CW]).then_inc(xs_in[c % 2], 16)

            run_steps(sp, TILES, DEPTH, 2, body)
            for b in range(2):
                sp.wait_ge(gt_stored[b], 16 * TILES // 2)

        @block.scalar
        def _(act):
            act.wait_ge(fac_in, 16)

            def body(k, m):
                s = stage(k, m, 0, 2, TILES)
                if s is not None:
                    t, b, _ = s
                    for c in range(NCH):
                        act.wait_ge(raw_in[c], 16 * t + 16)
                        if not first(t, 1):
                            act.wait_ge(x_used, 4 * t + (c - 3))
                        nc.scalar.activation(x_hi[c][:], raw[c][:], ACT.Copy).then_inc(hi_done, 1)
                        if first(t, 1):
                            for n in range(PER * c, PER * c + PER):
                                w1.split_hi(act, n)
                        if c == 0 and not first(t, 1):
                            act.wait_ge(r_done, t)
                        act.wait_ge(xs_in[c % 2], 32 * t + 16 * (c // 2) + 16)
                        if not (first(t, 1) and c == 0):
                            act.wait_ge(sq_done, 4 * t + c)
                        nc.scalar.activation(junk[:], xs[c % 2][:], ACT.Square,
                                             accum_out=ssq[:, c:c + 1]).then_inc(sq_done, 1)
                s = stage(k, m, 1, 2, TILES)
                if s is not None:
                    t, b, kb = s
                    act.wait_ge(x_used, 4 * t + 4)
                    act.wait_ge(r_done, t + 1)
                    if not first(t, 2):
                        act.wait_ge(t_done, t - 1)
                    nc.scalar.activation(sil[b][:], ps_h[b][:, HID:2 * HID], ACT.Silu,
                                         scale=r[b][:, 0:1]).then_inc(sil_done, 1)
                    act.wait_ge(t_done, t + 1)
                    if not first(t, 2):
                        act.wait_ge(gt_stored[b], 16 * kb)
                    nc.scalar.activation(gt[b][:], ps_t[b][:], ACT.Copy).then_inc(gt_done, 1)

            run_steps(act, TILES, DEPTH, 2, body)

        @block.vector
        def _(dve):
            link = Link(dve, link_sem, INV_SQRT_LINKS + 2)
            dve.wait_ge(fac_in, 16)

            def body(k, m):
                s = stage(k, m, 0, 2, TILES)
                if s is not None:
                    t, b, _ = s
                    link.step(t)
                    for c in range(NCH):
                        dve.wait_ge(hi_done, 4 * t + c + 1)
                        nc.vector.tensor_tensor(x_lo[c][:], raw[c][:], x_hi[c][:], ALU.subtract).then_inc(lo_done, 1)
                        if first(t, 1):
                            for n in range(PER * c, PER * c + PER):
                                w1.split_lo(dve, n)
                s1 = stage(k, m, 1, 2, TILES)
                if s1 is not None:
                    t, b, _ = s1
                    dve.wait_ge(sil_done, t + 1)
                    nc.vector.scalar_tensor_tensor(g[b][:], ps_h[b][:, 0:HID], r[b][:, 0:1], sil[b][:],
                                                   ALU.mult, ALU.mult).then_inc(g_done, 1)
                if s is not None:
                    t, b, _ = s
                    dve.wait_ge(sq_done, 4 * t + 4)
                    link(nc.vector.reduce_sum(var[:, 0:1], ssq[:], AX.X))
                    link(nc.vector.tensor_scalar(var[:, 0:1], var[:, 0:1], 1.0 / DIN, RMS_EPS, ALU.mult, ALU.add))
                    inv_sqrt(nc, link, var[:, 0:1], var[:, 1:2], r[b][:], var[:, 2:3])
                    link.fill()
                    dve.sem_inc(r_done, 1)

            run_steps(dve, TILES, DEPTH, 2, body)

        @block.tensor
        def _(pe):
            pe.wait_ge(ident_in, 16)

            def body(k, m):
                s = stage(k, m, 0, 2, TILES)
                s1 = stage(k, m, 1, 2, TILES)
                for c in range(NCH):
                    if s is not None:
                        t, b, _ = s
                        if c == 0 and not first(t, 2):
                            pe.wait_ge(g_done, t - 1)
                        pe.wait_ge(lo_done, 4 * t + c + 1)
                        outs = [ps_h[b][:, 0:HID], ps_h[b][:, HID:2 * HID]]
                        for j in range(KCH):
                            n = KCH * c + j
                            if first(t, 1):
                                w1.wait(pe, 2 * n + 1)
                            last = three_pass(nc, outs, x_hi[c][:, j, :], x_lo[c][:, j, :],
                                              [w_hi[:, n, 0:HID], w_hi[:, n, HID:2 * HID]],
                                              [w_lo[:, n, 0:HID], w_lo[:, n, HID:2 * HID]], n == 0, n == KIN - 1)
                        last.then_inc(x_used, 1)
                    if c == 0 and s1 is not None:
                        t, b, _ = s1
                        pe.wait_ge(g_done, t + 1)
                        if not first(t, 2):
                            pe.wait_ge(gt_done, t - 1)
                        for j in range(HID // P):
                            last = nc.tensor.transpose(ps_t[b][:, P * j:P * j + P], g[b][:, P * j:P * j + P], ident[:])
                        last.then_inc(t_done, 1)

            run_steps(pe, TILES, DEPTH, 2, body)


def tok_down(nc, d, split, ring, ident, qn_hi, qn_lo, k_t):
    W = QR + KR + RO
    with ExitStack() as ctx:
        mem = Memory(nc, ctx, "down")
        w2_hi = mem.sb("w2_hi", [P, 4, DM], F32R)
        w2_lo = mem.sb("w2_lo", [P, 4, DM], F32R)
        wa_hi = mem.sb("wa_hi", [P, KM, W], F32R)
        wa_lo = mem.sb("wa_lo", [P, KM, W], F32R)
        post = mem.sb("post", [P, DM])
        kvw = mem.sb("kvw", [P, KR])
        g_raw = [mem.sb(f"g_raw{i}", [P, 4, P]) for i in range(2)]
        g_hi = [mem.sb(f"g_hi{i}", [P, 4, P], F32R) for i in range(2)]
        g_lo = [mem.sb(f"g_lo{i}", [P, 4, P], F32R) for i in range(2)]
        junk = mem.sb("junk", [P, DM], BF16)
        junk_a = mem.sb("junk_a", [P, QR + KR], BF16)
        ms = [mem.sb(f"ms{i}", [P, 3]) for i in range(2)]
        root = [mem.sb(f"root{i}", [P, 4]) for i in range(2)]
        vec = [mem.sb(f"vec{i}", [P, 16]) for i in range(2)]
        bn = mem.sb("bn", [P, 12])
        z = mem.sb("z", [P, DM])
        y = [mem.sb(f"y{i}", [P, DM]) for i in range(2)]
        xn = [mem.sb(f"xn{i}", [P, DM]) for i in range(2)]
        xt_hi = mem.sb("xt_hi", [P, KM, P], F32R)
        xt_lo = mem.sb("xt_lo", [P, KM, P], F32R)
        qk = [mem.sb(f"qk{i}", [P, W]) for i in range(2)]
        kr = [mem.sb(f"kr{i}", [P, RO]) for i in range(2)]
        turns = [mem.sb(f"turns{i}", [P, 2, RO]) for i in range(2)]
        by_cos = mem.sb("by_cos", [P, RO])
        by_sin = mem.sb("by_sin", [P, RO])
        wqn = [mem.sb(f"wqn{i}", [P, QR]) for i in range(2)]
        wk = [mem.sb(f"wk{i}", [P, KR]) for i in range(2)]
        wqp = [mem.sb(f"wqp{i}", [P, 2, P]) for i in range(2)]
        wv = [mem.sb(f"wv{i}", [P, 2, KR]) for i in range(2)]
        wo = [[ring[2 * i + h][:, 0:DM] for h in range(2)] for i in range(2)]
        qln = mem.sb("qln", [P, 2])
        wq_out = [mem.sb(f"wq_out{i}", [P, 2, 2 * P]) for i in range(2)]
        wv_out = [mem.sb(f"wv_out{i}", [P, DM]) for i in range(2)]
        NW = 4 + KM
        ws = split.pieces(ring, [d["w2"][:, n, :] for n in range(4)] + [d["wa"][:, n, :] for n in range(KM)])
        ws.into([(w2_hi[:, n, :], w2_lo[:, n, :], None) for n in range(4)] +
                [(wa_hi[:, n, :], wa_lo[:, n, :], None) for n in range(KM)])
        ps_y = mem.ps("ps_y", [P, DM])
        ps_x = [mem.ps(f"ps_x{i}", [P, 4, P]) for i in range(2)]
        ps_a = [mem.ps(f"ps_a{i}", [P, 512]) for i in range(2)]
        ps_d = mem.ps("ps_d", [P, 512])
        ps_f = mem.ps("ps_f", [P, 512])
        eps = mem.sb("eps", [P, 1])
        eps_set = mem.sem("eps_set")
        const_in = mem.sem("const_in")
        g_in = mem.sems("g_in", 2)
        ghi_done = mem.sem("ghi_done")
        glo_done = mem.sem("glo_done")
        y_made = mem.sem("y_made")
        ysq_done = mem.sem("ysq_done")
        yroot_done = mem.sem("yroot_done")
        z_done = mem.sem("z_done")
        r_done = mem.sem("r_done")
        y_done = mem.sem("y_done")
        yvar_done = mem.sem("yvar_done")
        yvroot_done = mem.sem("yvroot_done")
        xn_done = mem.sem("xn_done")
        x_turned = mem.sem("x_turned")
        xhi_done = mem.sem("xhi_done")
        xlo_done = mem.sem("xlo_done")
        a_made = mem.sem("a_made")
        asq_done = mem.sem("asq_done")
        aroot_done = mem.sem("aroot_done")
        avar_done = mem.sem("avar_done")
        qk_done = mem.sem("qk_done")
        turns_in = mem.sems("turns_in", 2)
        key_link = mem.sem("key_link")
        key_done = mem.sem("key_done")
        qk_turned = mem.sem("qk_turned")
        qhi_done = mem.sem("qhi_done")
        qlo_done = mem.sem("qlo_done")
        y_stored = mem.stored("y_stored", 2)
        fold_in = mem.sems("fold_in", 2)
        fa_made = mem.sem("fa_made")
        f_made = mem.sem("f_made")
        f_out = mem.sem("f_out")
        rope_out = mem.sem("rope_out")
        wq_stored = mem.stored("wq_stored", 2)
        wv_stored = mem.stored("wv_stored", 2)
        link_sem = mem.sem("link")
        block = ctx.enter_context(nc.Block())
        D_Y, D_X, D_A, D_Q = 1, 3, 3, 4
        DEPTH = 4
        U = 6
        D_F = 2
        FOLD = {0: 0, 1: 1, 3: 2, 4: 3}
        assert PAIRS == TILES // U * len(FOLD)

        def fold(k, m):
            s = stage(k, m, D_F, U, TILES)
            if s is None or s[1] not in FOLD:
                return None
            f = FOLD[s[1]]
            return s[2] * len(FOLD) + f, f % 2, s[2] * (len(FOLD) // 2) + f // 2

        def nth(kb, u):
            return kb * (U // 2) + u // 2 + 1

        @block.sync
        def _(sp):
            def body(k, m):
                s = stage(k, m, 0, U, TILES)
                if s is not None:
                    t, u, kb = s
                    if not first(t, 2):
                        sp.wait_ge(glo_done, t - 1)
                    sp.dma_start(g_raw[u % 2][:], d["g_t"][t].rearrange("p (j c) -> p j c", j=4)).then_inc(g_in[u % 2], 16)
                    if first(t, 1):
                        for n in range(NW):
                            ws.load(sp, n)
                            if n == Splitter.RING - 1:
                                for dst, name in ((post, "post_ln"), (kvw, "kv_ln"), (qln, "q_ln")):
                                    sp.dma_start(dst[:], d[name]).then_inc(const_in, 16)
                s = stage(k, m, D_A, U, TILES)
                if s is not None:
                    t, u, kb = s
                    if not first(t, 2):
                        sp.wait_ge(key_done, t - 1)
                    sp.dma_start(turns[u % 2][:], d["turns"][t]).then_inc(turns_in[u % 2], 16)
                s = fold(k, m)
                if s is not None:
                    p, b, turn = s
                    if not first(p, 2):
                        sp.wait_ge(wv_stored[b], 16 * turn)
                    for dst, name in ((wqn, "wq_nope"), (wk, "wk"), (wqp, "wq_rope"), (wv, "wv")):
                        sp.dma_start(dst[b][:], d[name][p]).then_inc(fold_in[b], 16)
                    if first(p, 1):
                        ws.wait(sp, NW - 1)
                    for h in range(2):
                        sp.dma_start(wo[b][h], d["wo"][p][:, h, :]).then_inc(fold_in[b], 16)

            run_steps(sp, TILES, DEPTH, U, body)

        @block.gpsimd
        def _(pool):
            nc.gpsimd.memset(eps[:], RMS_EPS).then_inc(eps_set, 1)
            pool.wait_ge(const_in, 48)

            def body(k, m):
                s = fold(k, m)
                if s is not None:
                    p, b, turn = s
                    pool.wait_ge(fold_in[b], 96 * turn + 96)
                    if not first(p, 2):
                        pool.wait_ge(wq_stored[b], 16 * turn)
                    nc.gpsimd.tensor_tensor(wq_out[b][:, :, P:2 * P], wqp[b][:], qln[:].unsqueeze(2).broadcast_to((P, 2, P)),
                                            ALU.mult).then_inc(rope_out, 1)
                s1 = stage(k, m, D_Y, U, TILES)
                if s1 is not None:
                    t, u, kb = s1
                    pool.wait_ge(y_done, t + 1)
                    pool.dma_start(d["y"][t], y[u % 2][:]).then_inc(y_stored[u % 2], 16)
                if s is not None:
                    p, b, turn = s
                    pool.wait_ge(rope_out, p + 1)
                    pool.wait_ge(f_out, 3 * p + 1)
                    pool.dma_start(d["wq_pair"][p], wq_out[b][:]).then_inc(wq_stored[b], 16)
                s = stage(k, m, D_A, U, TILES)
                if s is not None:
                    t, u, kb = s
                    b = u % 2
                    link = Link(pool, key_link, 2)
                    link.step(t)
                    if not first(t, 1):
                        pool.wait_ge(key_done, t)
                    pool.wait_ge(turns_in[b], 16 * nth(kb, u))
                    pool.wait_ge(qk_done, t + 1)
                    if not first(t, 2):
                        pool.wait_ge(qk_turned, t - 1)
                    nc.gpsimd.tensor_tensor(by_cos[:], kr[b][:], turns[b][:, 0, :], ALU.mult)
                    pairs = [x.rearrange("p (i two) -> p i two", two=2) for x in (by_sin[:], kr[b][:], turns[b][:, 1, :])]
                    for one in range(2):
                        out, x, sines = pairs[0][:, :, one], pairs[1][:, :, 1 - one], pairs[2][:, :, one]
                        last = nc.gpsimd.tensor_tensor(out, x, sines, ALU.mult)
                        if one == 0:
                            last.then_inc(key_link, 1)
                    link.n += 1
                    link(last)
                    nc.gpsimd.tensor_tensor(qk[b][:, QR + KR:W], by_cos[:], by_sin[:], ALU.add).then_inc(key_done, 1)
                s = fold(k, m)
                if s is not None:
                    p, b, turn = s
                    pool.wait_ge(f_out, 3 * p + 3)
                    pool.dma_start(d["wvo"][:, p, :], wv_out[b][:]).then_inc(wv_stored[b], 16)

            run_steps(pool, TILES, DEPTH, U, body)
            for b in range(2):
                pool.wait_ge(y_stored[b], 16 * TILES // 2)
                pool.wait_ge(wq_stored[b], 16 * PAIRS // 2)
                pool.wait_ge(wv_stored[b], 16 * PAIRS // 2)

        @block.scalar
        def _(act):
            act.wait_ge(eps_set, 1)

            def fold_half(f, n):
                p, b, turn = f
                act.wait_ge(f_made, 3 * p + 2 + n)
                if n == 0 and not first(p, 2):
                    act.wait_ge(wv_stored[b], 16 * turn)
                nc.scalar.activation(wv_out[b][:, 512 * n:512 * n + 512], ps_f[:], ACT.Copy).then_inc(f_out, 1)

            def body(k, m):
                s = stage(k, m, D_X, U, TILES)
                if s is not None:
                    t, u, kb = s
                    if not first(t, 1):
                        act.wait_ge(a_made, t)
                    for h in range(2):
                        act.wait_ge(x_turned, 2 * t + h + 1)
                        nc.scalar.activation(xt_hi[:, 4 * h:4 * h + 4, :], ps_x[h][:], ACT.Copy).then_inc(xhi_done, 1)
                s = stage(k, m, 0, U, TILES)
                if s is not None:
                    t, u, kb = s
                    act.wait_ge(g_in[u % 2], 16 * nth(kb, u))
                    if not first(t, 2):
                        act.wait_ge(y_made, t - 1)
                    nc.scalar.activation(g_hi[u % 2][:], g_raw[u % 2][:], ACT.Copy).then_inc(ghi_done, 1)
                    if first(t, 1):
                        for n in range(NW):
                            ws.split_hi(act, n)
                f = fold(k, m)
                if f is not None:
                    p, b, turn = f
                    act.wait_ge(f_made, 3 * p + 1)
                    if first(p, 1):
                        act.wait_ge(const_in, 48)
                    if not first(p, 2):
                        act.wait_ge(wq_stored[b], 16 * turn)
                    for c in range(2):
                        last = nc.scalar.activation(wq_out[b][:, c, 0:P], ps_f[:, P * c:P * c + P], ACT.Copy,
                                                    scale=qln[:, c:c + 1])
                    last.then_inc(f_out, 1)
                s = stage(k, m, D_Y, U, TILES)
                if s is not None:
                    t, u, kb = s
                    b = u % 2
                    act.wait_ge(y_made, t + 1)
                    if not first(t, 1):
                        act.wait_ge(ysq_done, t)
                    if not first(t, 2):
                        act.wait_ge(xn_done, t - 1)
                    act.wait_ge(z_done, t + 1)
                    nc.scalar.activation(junk[:], ps_y[:], ACT.Square, scale=DM ** -0.5,
                                         accum_out=ms[b][:, 0:1]).then_inc(ysq_done, 1)
                    act.wait_ge(ysq_done, t + 1)
                    nc.scalar.activation(root[b][:, 0:1], ms[b][:, 0:1], ACT.Sqrt, bias=eps[:, 0:1]).then_inc(yroot_done, 1)
                if f is not None:
                    fold_half(f, 0)
                if s is not None:
                    act.wait_ge(r_done, t + 1)
                    if not first(t, 2):
                        act.wait_ge(y_stored[b], 16 * nth(kb, u) - 16)
                    nc.scalar.activation(y[b][:], z[:], ACT.Copy, scale=vec[b][:, 1:2]).then_inc(y_done, 1)
                    act.wait_ge(yvar_done, t + 1)
                    nc.scalar.activation(root[b][:, 3:4], vec[b][:, 6:7], ACT.Sqrt).then_inc(yvroot_done, 1)
                s = stage(k, m, D_A, U, TILES)
                if s is not None:
                    t, u, kb = s
                    b = u % 2
                    act.wait_ge(a_made, t + 1)
                    if not first(t, 2):
                        act.wait_ge(qk_done, t - 1)
                    if not first(t, 1):
                        act.wait_ge(asq_done, 2 * t)
                    nc.scalar.activation(junk_a[:, 0:QR], ps_a[b][:, 0:QR], ACT.Square, scale=QR ** -0.5,
                                         accum_out=ms[b][:, 1:2]).then_inc(asq_done, 1)
                    nc.scalar.activation(junk_a[:, QR:QR + KR], ps_a[b][:, QR:QR + KR], ACT.Square, scale=KR ** -0.5,
                                         accum_out=ms[b][:, 2:3]).then_inc(asq_done, 1)
                    act.wait_ge(asq_done, 2 * t + 2)
                    nc.scalar.activation(root[b][:, 1:3], ms[b][:, 1:3], ACT.Sqrt, bias=eps[:, 0:1]).then_inc(aroot_done, 1)
                if f is not None:
                    fold_half(f, 1)
                s = stage(k, m, D_Q, U, TILES)
                if s is not None:
                    t, u, kb = s
                    act.wait_ge(qk_turned, t + 1)
                    cols = bass.ts(t, P)
                    nc.scalar.activation(qn_hi[:, :, cols], ps_d[:, 0:2 * P].rearrange("p (c n) -> p c n", c=2),
                                         ACT.Copy).then_inc(qhi_done, 1)
                    nc.scalar.activation(k_t[:, cols], ps_d[:, 2 * P:3 * P], ACT.Copy).then_inc(qhi_done, 1)

            run_steps(act, TILES, DEPTH, U, body)

        @block.vector
        def _(dve):
            link = Link(dve, link_sem, 19)

            def body(k, m):
                s = stage(k, m, D_X, U, TILES)
                if s is not None:
                    t, u, kb = s
                    for h in range(2):
                        dve.wait_ge(xhi_done, 2 * t + h + 1)
                        nc.vector.tensor_tensor(xt_lo[:, 4 * h:4 * h + 4, :], ps_x[h][:], xt_hi[:, 4 * h:4 * h + 4, :],
                                                ALU.subtract).then_inc(xlo_done, 1)
                s = stage(k, m, 0, U, TILES)
                if s is not None:
                    t, u, kb = s
                    dve.wait_ge(ghi_done, t + 1)
                    nc.vector.tensor_tensor(g_lo[u % 2][:], g_raw[u % 2][:], g_hi[u % 2][:],
                                            ALU.subtract).then_inc(glo_done, 1)
                    if first(t, 1):
                        for n in range(NW):
                            ws.split_lo(dve, n)
                s = stage(k, m, D_Y, U, TILES)
                if s is not None:
                    t, u, kb = s
                    b = u % 2
                    v = vec[b]
                    dve.wait_ge(y_made, t + 1)
                    if not first(t, 1):
                        dve.wait_ge(y_done, t)
                        dve.wait_ge(xn_done, t)
                    if first(t, 1):
                        dve.wait_ge(const_in, 48)
                    nc.vector.tensor_tensor(z[:], ps_y[:], post[:], ALU.mult).then_inc(z_done, 1)
                    dve.wait_ge(z_done, t + 1)
                    nc.vector.bn_stats(bn[:, 0:6], z[:, 0:512])
                    link(nc.vector.bn_stats(bn[:, 6:12], z[:, 512:1024]))
                    dve.wait_ge(yroot_done, t + 1)
                    if not first(t, 2):
                        dve.wait_ge(yvroot_done, t - 1)
                    nc.vector.tensor_scalar(v[:, 0:1], ms[b][:, 0:1], RMS_EPS, -0.5, ALU.add, ALU.mult)
                    link(nc.vector.reciprocal(v[:, 1:2], root[b][:, 0:1]))
                    newton(nc, link, v[:, 0:1], v[:, 1:2], v[:, 2:3])
                    dve.sem_inc(r_done, 1)
                    link.settle()
                    link(nc.vector.bn_aggr(v[:, 4:6], bn[:]))
                    link(nc.vector.scalar_tensor_tensor(v[:, 3:4], v[:, 1:2], v[:, 1:2], v[:, 5:6], ALU.mult, ALU.mult))
                    nc.vector.tensor_scalar(v[:, 6:7], v[:, 3:4], LN_EPS, None, ALU.add).then_inc(yvar_done, 1)
                    dve.wait_ge(yvroot_done, t + 1)
                    nc.vector.tensor_scalar(v[:, 15:16], v[:, 6:7], -0.5, None, ALU.mult)
                    link(nc.vector.reciprocal(v[:, 7:8], root[b][:, 3:4]))
                    newton(nc, link, v[:, 15:16], v[:, 7:8], v[:, 8:9])
                    link(nc.vector.tensor_tensor(v[:, 7:8], v[:, 7:8], v[:, 1:2], ALU.mult))
                    if not first(t, 2):
                        dve.wait_ge(x_turned, 2 * t - 2)
                    nc.vector.tensor_scalar(xn[b][:], z[:], v[:, 4:5], v[:, 7:8], ALU.subtract,
                                            ALU.mult).then_inc(xn_done, 1)
                s = stage(k, m, D_A, U, TILES)
                if s is not None:
                    t, u, kb = s
                    b = u % 2
                    v = vec[b]
                    dve.wait_ge(aroot_done, t + 1)
                    nc.vector.tensor_scalar(v[:, 9:11], ms[b][:, 1:3], RMS_EPS, None, ALU.add)
                    link(nc.vector.reciprocal(v[:, 11:13], root[b][:, 1:3]))
                    link(nc.vector.tensor_tensor(v[:, 13:15], v[:, 11:13], v[:, 11:13], ALU.mult))
                    link(nc.vector.tensor_tensor(v[:, 13:15], v[:, 13:15], v[:, 9:11], ALU.mult))
                    link(nc.vector.tensor_scalar(v[:, 13:15], v[:, 13:15], -0.5, 1.5, ALU.mult, ALU.add))
                    link(nc.vector.tensor_tensor(v[:, 11:13], v[:, 11:13], v[:, 13:15], ALU.mult))
                    if not first(t, 2):
                        dve.wait_ge(qk_turned, t - 1)
                        dve.wait_ge(key_done, t - 1)
                    nc.vector.tensor_scalar(qk[b][:, 0:QR], ps_a[b][:, 0:QR], v[:, 11:12], None, ALU.mult)
                    nc.vector.scalar_tensor_tensor(qk[b][:, QR:QR + KR], ps_a[b][:, QR:QR + KR], v[:, 12:13],
                                                   kvw[:], ALU.mult, ALU.mult)
                    nc.vector.tensor_copy(kr[b][:], ps_a[b][:, QR + KR:W]).then_inc(qk_done, 1)
                s = stage(k, m, D_Q, U, TILES)
                if s is not None:
                    t, u, kb = s
                    cols = bass.ts(t, P)
                    dve.wait_ge(qhi_done, 2 * t + 2)
                    nc.vector.tensor_tensor(qn_lo[:, :, cols], ps_d[:, 0:2 * P].rearrange("p (c n) -> p c n", c=2),
                                            qn_hi[:, :, cols], ALU.subtract).then_inc(qlo_done, 1)

            def step(k, m):
                link.step(k * U + m)
                body(k, m)
                link.fill()

            run_steps(dve, TILES, DEPTH, U, step)

        @block.tensor
        def _(pe):
            def fold_q(f, h):
                p, b, turn = f
                if h == 0:
                    pe.wait_ge(fold_in[b], 96 * turn + 96)
                    if not first(p, 1):
                        pe.wait_ge(f_out, 3 * p)
                else:
                    pe.wait_ge(fa_made, p + 1)
                rows = slice(64 * h, 64 * h + 64)
                for c in range(2):
                    at = P * c + 64 * h
                    last = nc.tensor.matmul(ps_f[:, at:at + 64], wqn[b][rows, P * c:P * c + P], wk[b][rows, :],
                                            start=True, stop=True)
                last.then_inc(f_made if h == 1 else fa_made, 1)

            def fold_v(f, n):
                p, b, turn = f
                pe.wait_ge(f_out, 3 * p + 1 + n)
                for h in range(2):
                    last = nc.tensor.matmul(ps_f[64 * h:64 * h + 64, :], wv[b][:, h, :],
                                            wo[b][h][:, 512 * n:512 * n + 512], start=True, stop=True)
                last.then_inc(f_made, 1)

            def body(k, m):
                f = fold(k, m)
                s = stage(k, m, D_X, U, TILES)
                if s is not None:
                    t, u, kb = s
                    pe.wait_ge(xn_done, t + 1)
                    for h in range(2):
                        if not first(t, 1):
                            pe.wait_ge(xlo_done, 2 * t + (h - 1))
                        for j in range(4):
                            n = 4 * h + j
                            last = nc.tensor.transpose(ps_x[h][:, j, :], xn[u % 2][:, P * n:P * n + P], ident[:])
                        last.then_inc(x_turned, 1)
                late = f is not None and first(f[0], 1)
                if f is not None and not late:
                    fold_q(f, 0)
                s = stage(k, m, D_Y, U, TILES)
                if s is not None:
                    t, u, kb = s
                    pe.wait_ge(glo_done, t + 1)
                    if not first(t, 1):
                        pe.wait_ge(z_done, t)
                        pe.wait_ge(ysq_done, t)
                    outs = [ps_y[:, 0:512], ps_y[:, 512:1024]]
                    for n in range(4):
                        if n == 2 and f is not None and not late:
                            fold_q(f, 1)
                        if first(t, 1):
                            ws.wait(pe, n)
                        last = three_pass(nc, outs, g_hi[u % 2][:, n, :], g_lo[u % 2][:, n, :],
                                          [w2_hi[:, n, 0:512], w2_hi[:, n, 512:1024]],
                                          [w2_lo[:, n, 0:512], w2_lo[:, n, 512:1024]], n == 0, n == 3)
                    last.then_inc(y_made, 1)
                if late:
                    fold_q(f, 0)
                if late or (s is None and f is not None):
                    fold_q(f, 1)
                if f is not None:
                    fold_v(f, 0)
                s = stage(k, m, D_A, U, TILES)
                if s is not None:
                    t, u, kb = s
                    if not first(t, 2):
                        pe.wait_ge(qk_done, t - 1)
                    for n in range(KM):
                        if n % 4 == 0:
                            pe.wait_ge(xlo_done, 2 * t + n // 4 + 1)
                        if first(t, 1):
                            ws.wait(pe, 4 + n)
                        last = three_pass(nc, [ps_a[u % 2][:, 0:W]], xt_hi[:, n, :], xt_lo[:, n, :],
                                          [wa_hi[:, n, :]], [wa_lo[:, n, :]], n == 0, n == KM - 1)
                    last.then_inc(a_made, 1)
                if f is not None:
                    fold_v(f, 1)
                s = stage(k, m, D_Q, U, TILES)
                if s is not None:
                    t, u, kb = s
                    pe.wait_ge(qk_done, t + 1)
                    pe.wait_ge(key_done, t + 1)
                    if not first(t, 1):
                        pe.wait_ge(qlo_done, t)
                        pe.wait_ge(qhi_done, 2 * t)
                    for j in range(3):
                        last = nc.tensor.transpose(ps_d[:, P * j:P * j + P], qk[u % 2][:, P * j:P * j + P], ident[:])
                    last.then_inc(qk_turned, 1)

            run_steps(pe, TILES, DEPTH, U, body)


def attention(nc, d, wvo, ident, qn_hi, qn_lo, k_t):
    with ExitStack() as ctx:
        mem = Memory(nc, ctx, "attn")
        cos = mem.sb("cos", [P, GT])
        sin = mem.sb("sin", [P, GT])
        k_tb = mem.sb("k_tb", [P, TOK])
        v = mem.sb("v", [P, BATCH, KR])
        mask = mem.sb("mask", [P, SEQ])
        swap = [p ^ 1 for p in range(32)]
        w_raw = [mem.sb(f"w_raw{i}", [P, 2, 2 * P]) for i in range(2)]
        w_hi = [mem.sb(f"w_hi{i}", [P, 2, 2 * P], F32R) for i in range(2)]
        w_lo = [mem.sb(f"w_lo{i}", [P, 2, 2 * P], F32R) for i in range(2)]
        q_a = [mem.sb(f"q_a{i}", [P, GT]) for i in range(2)]
        q_b = [mem.sb(f"q_b{i}", [P, GT]) for i in range(2)]
        by_cos = mem.sb("by_cos", [P, GT])
        swapped = mem.sb("swapped", [P, GT])
        by_sin = mem.sb("by_sin", [P, GT])
        top = mem.sb("top", [P, 8])
        bias = [mem.sb(f"bias{i}", [P, 8]) for i in range(2)]
        total = [mem.sb(f"total{i}", [P, 8]) for i in range(2)]
        share = [mem.sb(f"share{i}", [P, 8]) for i in range(2)]
        NPR = 4
        prob = [mem.sb(f"prob{i}", [P, 2, GT]) for i in range(NPR)]
        prob_t = [mem.sb(f"prob_t{i}", [P, 2, GT]) for i in range(2)]
        o_t = [mem.sb(f"o_t{i}", [P, GT]) for i in range(2)]
        zero = mem.sb("zero", [P, PAIRS, TOKP - TOK])
        ps_l = mem.ps("ps_l", [P, 512])
        ps_r = mem.ps("ps_r", [P, 512])
        ps_s = mem.ps("ps_s", [P, 2, 512])
        ps_t = mem.ps("ps_t", [P, 2, 512])
        ps_o = mem.ps("ps_o", [P, 512])
        ps_v = [ps_s[:, 0, :], ps_s[:, 1, :], ps_t[:, 0, :], ps_t[:, 1, :]]
        w_in = mem.sems("w_in", 2)
        w_hi_done = mem.sem("w_hi_done")
        w_lo_done = mem.sem("w_lo_done")
        rope_made = mem.sem("rope_made")
        latent_made = mem.sem("latent_made")
        latent_done = mem.sem("latent_done")
        swap_done = mem.sem("swap_done")
        sin_done = mem.sem("sin_done")
        rope_a_done = mem.sem("rope_a_done")
        rope_b_done = mem.sem("rope_b_done")
        scored = mem.sem("scored")
        masked = mem.sem("masked")
        top_done = mem.sem("top_done")
        bias_done = mem.sem("bias_done")
        exp_done = mem.sem("exp_done")
        share_done = mem.sem("share_done")
        prob_done = mem.sem("prob_done")
        turned = mem.sem("turned")
        prob_t_done = mem.sem("prob_t_done")
        weighed = mem.sem("weighed")
        o_done = mem.sem("o_done")
        o_stored = mem.sems("o_stored", 2)
        zeroed = mem.sem("zeroed")
        table_in = mem.sem("table_in")
        v_made = mem.sem("v_made")
        v_done = mem.sem("v_done")
        keys_done = mem.sem("keys_done")
        pad_stored = mem.stored("pad_stored", 1)[0]
        block = ctx.enter_context(nc.Block())

        N = PAIRS * GROUPS
        U = 2 * GROUPS
        D_S, D_N, D_T, D_V, D_O = 1, 2, 4, 5, 6
        DEPTH = D_O
        PREP = 4

        def weights_of(k, m, at):
            if m % GROUPS != at:
                return None
            return stage(k, m // GROUPS, -1, 2, PAIRS)

        def bodied(n, kb, u, per):
            return kb * (U // per) + u // per + n

        @block.sync
        def _(sp):
            sp.dma_start(w_raw[0][:], d["wq_pair"][0]).then_inc(w_in[0], 16)
            for dst, name in ((sin, "sin"), (cos, "cos"), (mask, "mask")):
                sp.dma_start(dst[:], d[name]).then_inc(table_in, 16)
            for n in range(Splitter.RING):
                wvo.load(sp, n)

            def body(k, m):
                s = stage(k, m // GROUPS, -1, 2, PAIRS) if m % GROUPS == 0 else None
                if s is not None:
                    p, w, kb = s
                    if not first(p, 2):
                        sp.wait_ge(w_lo_done, 2 * p - 2)
                    sp.dma_start(w_raw[w][:], d["wq_pair"][p]).then_inc(w_in[w], 16)
                s = stage(k, m, D_O, U, N)
                if s is not None:
                    j, u, kb = s
                    g = u % GROUPS
                    sp.wait_ge(o_done, j + 1)
                    sp.dma_start(d["o_t"][:, 2 * kb + u // GROUPS, GT * g:GT * g + GT],
                                 o_t[u % 2][:]).then_inc(o_stored[u % 2], 16)

            run_steps(sp, N, DEPTH, U, body, last=1)
            for b in range(2):
                sp.wait_ge(o_stored[b], 16 * N // 2)

        @block.tensor
        def _(pe):
            for b in range(BATCH):
                last = nc.tensor.transpose(ps_v[b // 8][0:SEQ, KR * (b % 8):KR * (b % 8) + KR],
                                           k_t[0:KR, SEQ * b:SEQ * b + SEQ], ident[0:KR, 0:KR])
                if b % 8 == 7:
                    last.then_inc(v_made, 1)

            def body(k, m):
                s = stage(k, m, 0, U, N)
                if s is not None:
                    j, u, kb = s
                    w, g = u // GROUPS, u % GROUPS
                    if g == 0:
                        pe.wait_ge(w_lo_done, 4 * kb + (2 * w + 2))
                    cols = slice(GT * g, GT * g + GT)
                    for ps, at, sem, free in ((ps_r, P, rope_made, swap_done), (ps_l, 0, latent_made, latent_done)):
                        if not first(j, 1):
                            pe.wait_ge(free, j)
                        for c in range(2):
                            wh, wl = w_hi[w][:, c, at:at + P], w_lo[w][:, c, at:at + P]
                            nc.tensor.matmul(ps[:, 0:GT], wl, qn_hi[:, c, cols], start=(c == 0), stop=False)
                            nc.tensor.matmul(ps[:, 0:GT], wh, qn_lo[:, c, cols], start=False, stop=False)
                            last = nc.tensor.matmul(ps[:, 0:GT], wh, qn_hi[:, c, cols], start=False, stop=(c == 1))
                        last.then_inc(sem, 1)
                s = stage(k, m, D_S, U, N)
                if s is not None:
                    j, u, kb = s
                    g = u % GROUPS
                    if not first(j, 1):
                        pe.wait_ge(masked, j)
                    else:
                        pe.wait_ge(v_done, 4)
                        pe.wait_ge(keys_done, 2)
                    pe.wait_ge(latent_done, j + 1)
                    pe.wait_ge(rope_a_done, j + 1)
                    pe.wait_ge(rope_b_done, j + 1)
                    for h, (q, keys) in enumerate(((q_a[u % 2], k_t), (q_b[u % 2], k_tb))):
                        for b in range(GB):
                            at = GT * g + SEQ * b
                            last = nc.tensor.matmul(ps_s[0:SEQ, h, SEQ * b:SEQ * b + SEQ], q[:, SEQ * b:SEQ * b + SEQ],
                                                    keys[:, at:at + SEQ], start=True, stop=True)
                    last.then_inc(scored, 1)
                s = stage(k, m, D_T, U, N)
                if s is not None:
                    j, u, kb = s
                    pe.wait_ge(prob_done, j + 1)
                    if not first(j, 1):
                        pe.wait_ge(prob_t_done, j)
                    for h in range(2):
                        for b in range(GB):
                            part = slice(SEQ * b, SEQ * b + SEQ)
                            last = nc.tensor.transpose(ps_t[0:SEQ, h, part], prob[u % NPR][0:SEQ, h, part],
                                                       ident[0:SEQ, 0:SEQ])
                    last.then_inc(turned, 1)
                s = stage(k, m, D_V, U, N)
                if s is not None:
                    j, u, kb = s
                    g = u % GROUPS
                    pe.wait_ge(prob_t_done, j + 1)
                    if not first(j, 1):
                        pe.wait_ge(o_done, j)
                    for b in range(GB):
                        for h in range(2):
                            last = nc.tensor.matmul(ps_o[64 * h:64 * h + 64, SEQ * b:SEQ * b + SEQ],
                                                    v[0:96, GB * g + b, :], prob_t[u % 2][0:96, h, SEQ * b:SEQ * b + SEQ],
                                                    start=True, stop=True)
                    last.then_inc(weighed, 1)

            run_steps(pe, N, DEPTH, U, body)

        @block.scalar
        def _(act):
            for i in range(4):
                act.wait_ge(v_made, i + 1)
                if i == 0:
                    act.wait_ge(zeroed, 1)
                nc.scalar.activation(v[0:SEQ, 8 * i:8 * i + 8, :], ps_v[i][0:SEQ, :].rearrange("p (b r) -> p b r", b=8),
                                     ACT.Copy).then_inc(v_done, 1)
            act.wait_ge(w_in[0], 16)
            for c in range(2):
                nc.scalar.activation(w_hi[0][:, c, :], w_raw[0][:, c, :], ACT.Copy).then_inc(w_hi_done, 1)

            def body(k, m):
                s = stage(k, m, 0, U, N)
                if s is not None:
                    j, u, kb = s
                    act.wait_ge(latent_made, j + 1)
                    if not first(j, 2):
                        act.wait_ge(scored, j - 1)
                    nc.scalar.activation(q_a[u % 2][0:64, :], ps_l[0:64, 0:GT], ACT.Copy)
                    nc.scalar.activation(q_b[u % 2][64:P, :], ps_l[64:P, 0:GT], ACT.Copy).then_inc(latent_done, 1)
                    for c in range(2):
                        s = weights_of(k, m, PREP + c)
                        if s is not None:
                            p, w, kb = s
                            if c == 0:
                                act.wait_ge(w_in[w], 16 * kb + 16)
                                if not first(p, 2):
                                    act.wait_ge(latent_made, GROUPS * (p - 1))
                            nc.scalar.activation(w_hi[w][:, c, :], w_raw[w][:, c, :], ACT.Copy).then_inc(w_hi_done, 1)
                s = stage(k, m, D_T, U, N)
                if s is not None:
                    j, u, kb = s
                    act.wait_ge(turned, j + 1)
                    if not first(j, 2):
                        act.wait_ge(weighed, j - 1)
                    nc.scalar.activation(prob_t[u % 2][0:SEQ, :, :], ps_t[0:SEQ, :, 0:GT],
                                         ACT.Copy).then_inc(prob_t_done, 1)
                s = stage(k, m, D_S, U, N)
                if s is not None:
                    j, u, kb = s
                    act.wait_ge(bias_done, j + 1)
                    for h in range(2):
                        for b in range(GB):
                            n = GB * h + b
                            part = slice(SEQ * b, SEQ * b + SEQ)
                            last = nc.scalar.activation(prob[u % NPR][0:SEQ, h, part], prob[u % NPR][0:SEQ, h, part], ACT.Exp,
                                                        bias=bias[u % 2][0:SEQ, n:n + 1], scale=SCALE,
                                                        accum_out=total[u % 2][0:SEQ, n:n + 1])
                    last.then_inc(exp_done, 1)

            act.wait_ge(zeroed, 4)
            nc.scalar.activation(k_tb[64:P, :], k_t[0:64, 0:TOK], ACT.Copy).then_inc(keys_done, 1)
            run_steps(act, N, DEPTH, U, body, last=1)

        @block.vector
        def _(dve):
            nc.vector.memset(v[64:P], 0.0).then_inc(zeroed, 1)
            for i in range(2):
                nc.vector.memset(prob_t[i][64:P], 0.0).then_inc(zeroed, 1)
            nc.vector.memset(zero[:], 0.0).then_inc(zeroed, 1)

            def split(w, p, c):
                dve.wait_ge(w_hi_done, 2 * p + (c + 1))
                nc.vector.tensor_tensor(w_lo[w][:, c, :], w_raw[w][:, c, :], w_hi[w][:, c, :],
                                        ALU.subtract).then_inc(w_lo_done, 1)

            nc.vector.tensor_copy(k_tb[0:64, :], k_t[64:P, 0:TOK]).then_inc(keys_done, 1)
            dve.wait_ge(table_in, 48)
            split(0, 0, 0)
            split(0, 0, 1)

            def body(k, m):
                s = stage(k, m, 0, U, N)
                if s is not None:
                    j, u, kb = s
                    dve.wait_ge(rope_made, j + 1)
                    if not first(j, 1):
                        dve.wait_ge(rope_a_done, j)
                        dve.wait_ge(rope_b_done, j)
                    nc.vector.tensor_tensor(by_cos[:], ps_r[:, 0:GT], cos[:], ALU.mult)
                    nc.vector.stream_shuffle(swapped[:], ps_r[:, 0:GT], swap).then_inc(swap_done, 1)
                    for c in range(2):
                        s = weights_of(k, m, PREP + 1 + c)
                        if s is not None:
                            p, w, kb = s
                            split(w, p, c)
                s = stage(k, m, D_O, U, N)
                if s is not None:
                    j, u, kb = s
                    dve.wait_ge(weighed, j + 1)
                    if not first(j, 2):
                        dve.wait_ge(o_stored[u % 2], 16 * bodied(0, kb, u, 2))
                    nc.vector.tensor_copy(o_t[u % 2][:], ps_o[:, 0:GT]).then_inc(o_done, 1)
                s = stage(k, m, D_S, U, N)
                if s is not None:
                    j, u, kb = s
                    dve.wait_ge(scored, j + 1)
                    if not first(j, NPR):
                        dve.wait_ge(turned, j - NPR + 1)
                    p4 = prob[u % NPR][0:SEQ, :, :].rearrange("p h (b k) -> p h b k", b=GB)
                    nc.vector.tensor_tensor(p4, ps_s[0:SEQ, :, 0:GT].rearrange("p h (b k) -> p h b k", b=GB),
                                            mask[0:SEQ, :].unsqueeze(1).unsqueeze(1).broadcast_to((SEQ, 2, GB, SEQ)),
                                            ALU.add).then_inc(masked, 1)
                s = stage(k, m, 0, U, N)
                if s is not None:
                    j, u, kb = s
                    dve.wait_ge(sin_done, j + 1)
                    if not first(j, 2):
                        dve.wait_ge(scored, j - 1)
                    nc.vector.tensor_tensor(q_b[u % 2][0:64, :], by_cos[0:64, :], by_sin[0:64, :],
                                            ALU.add).then_inc(rope_b_done, 1)
                s = stage(k, m, D_S, U, N)
                if s is not None:
                    j, u, kb = s
                    p4 = prob[u % NPR][0:SEQ, :, :].rearrange("p h (b k) -> p h b k", b=GB)
                    dve.wait_ge(masked, j + 1)
                    nc.vector.tensor_reduce(top[0:SEQ, :].rearrange("p (h b) -> p h b", h=2), p4, AX.X,
                                            ALU.max).then_inc(top_done, 1)
                    dve.wait_ge(top_done, j + 1)
                    if not first(j, 2):
                        dve.wait_ge(exp_done, j - 1)
                    nc.vector.tensor_scalar(bias[u % 2][0:SEQ, :], top[0:SEQ, :], -SCALE, None,
                                            ALU.mult).then_inc(bias_done, 1)
                s = stage(k, m, D_N, U, N)
                if s is not None:
                    j, u, kb = s
                    dve.wait_ge(exp_done, j + 1)
                    if not first(j, 2):
                        dve.wait_ge(prob_done, j - 1)
                    nc.vector.reciprocal(share[u % 2][0:SEQ, :], total[u % 2][0:SEQ, :]).then_inc(share_done, 1)

            run_steps(dve, N, DEPTH, U, body, last=1)

        @block.gpsimd
        def _(pool):
            pool.wait_ge(zeroed, 4)
            pool.dma_start(d["o_t"][:, :, TOK:TOKP], zero[:]).then_inc(pad_stored, 16)
            pool.wait_ge(table_in, 48)

            def body(k, m):
                s = stage(k, m, 0, U, N)
                if s is not None:
                    j, u, kb = s
                    pool.wait_ge(swap_done, j + 1)
                    if not first(j, 1):
                        pool.wait_ge(rope_b_done, j)
                    nc.gpsimd.tensor_tensor(by_sin[:], swapped[:], sin[:], ALU.mult).then_inc(sin_done, 1)
                    pool.wait_ge(sin_done, j + 1)
                    if not first(j, 2):
                        pool.wait_ge(scored, j - 1)
                    nc.gpsimd.tensor_tensor(q_a[u % 2][64:P, :], by_cos[64:P, :], by_sin[64:P, :],
                                            ALU.add).then_inc(rope_a_done, 1)
                s = stage(k, m, D_N, U, N)
                if s is not None:
                    j, u, kb = s
                    pool.wait_ge(share_done, j + 1)
                    pool.wait_ge(rope_a_done, min(j + D_N + 1, N) if isinstance(j, int) else j + D_N + 1)
                    p4 = prob[u % NPR][0:SEQ, :, :].rearrange("p h (b k) -> p (h b) k", b=GB)
                    nc.gpsimd.tensor_tensor(p4, p4, share[u % 2][0:SEQ, :].unsqueeze(2).broadcast_to((SEQ, 8, SEQ)),
                                            ALU.mult).then_inc(prob_done, 1)

            run_steps(pool, N, DEPTH, U, body)
            pool.wait_ge(pad_stored, 16)


def attn_out(nc, d, wvo, wf, h_next, h_next_in):
    CH = 4
    NC = PAIRS // CH
    with ExitStack() as ctx:
        mem = Memory(nc, ctx, "out")
        w_hi = mem.sb("w_hi", [P, PAIRS, DM], F32R)
        w_lo = mem.sb("w_lo", [P, PAIRS, DM], F32R)
        wvo.into([(w_hi[:, n, :], w_lo[:, n, :], None) for n in range(PAIRS)])
        raw = [mem.sb(f"raw{c}", [P, CH, P]) for c in range(NC)]
        x_hi = [mem.sb(f"x_hi{c}", [P, CH, P], F32R) for c in range(NC)]
        x_lo = [mem.sb(f"x_lo{c}", [P, CH, P], F32R) for c in range(NC)]
        y = [mem.sb(f"y{i}", [P, DM]) for i in range(2)]
        h = [mem.sb(f"h{i}", [P, DM]) for i in range(2)]
        ps_h = [mem.ps(f"ps_h{i}", [P, DM]) for i in range(2)]
        raw_in = mem.sems("raw_in", NC)
        y_in = mem.sems("y_in", 2)
        hi_done = mem.sem("hi_done")
        lo_done = mem.sem("lo_done")
        x_used = mem.sem("x_used")
        h_done = mem.sem("h_done")
        h_stored = mem.sems("h_stored", 2)
        block = ctx.enter_context(nc.Block())
        DEPTH = 1

        @block.sync
        def _(sp):
            def body(k, m):
                s = stage(k, m, 0, 2, TILES)
                if s is not None:
                    load(s)
                s = stage(k, m, 1, 2, TILES)
                if s is not None:
                    t, b, kb = s
                    sp.wait_ge(h_done, t + 1)
                    sp.dma_start(d["h"][t], h[b][:]).then_inc(h_stored[b], 16)

            def load(s):
                t, b, kb = s
                for c in range(NC):
                    if not first(t, 1):
                        sp.wait_ge(lo_done, NC * t + (c - NC + 1))
                    sp.dma_start(raw[c][:], d["o_t"][:, CH * c:CH * c + CH, bass.ts(t, P)]).then_inc(raw_in[c], 16)
                    if first(t, 1):
                        for n in range(max(CH * c, Splitter.RING), CH * c + CH):
                            wvo.load(sp, n)
                if not first(t, 2):
                    sp.wait_ge(h_done, t - 1)
                sp.dma_start(y[b][:], d["y"][t]).then_inc(y_in[b], 16)
                if isinstance(t, int) and t == 1:
                    for n in range(Splitter.RING):
                        wf.load(sp, n)

            run_steps(sp, TILES, DEPTH, 2, body)
            for t in range(3):
                sp.dma_start(h_next[t][:], d["h"][t]).then_inc(h_next_in[t], 16)
            for b in range(2):
                sp.wait_ge(h_stored[b], 16 * TILES // 2)

        @block.scalar
        def _(act):
            def body(k, m):
                s = stage(k, m, 0, 2, TILES)
                if s is None:
                    return
                t, b, kb = s
                for c in range(NC):
                    act.wait_ge(raw_in[c], 16 * t + 16)
                    if not first(t, 1):
                        act.wait_ge(x_used, NC * t + (c - NC + 1))
                    nc.scalar.activation(x_hi[c][:], raw[c][:], ACT.Copy).then_inc(hi_done, 1)
                    if first(t, 1):
                        for n in range(CH * c, CH * c + CH):
                            wvo.split_hi(act, n)

            run_steps(act, TILES, DEPTH, 2, body)

        @block.vector
        def _(dve):
            def body(k, m):
                s = stage(k, m, 0, 2, TILES)
                if s is not None:
                    t, b, kb = s
                    for c in range(NC):
                        dve.wait_ge(hi_done, NC * t + c + 1)
                        nc.vector.tensor_tensor(x_lo[c][:], raw[c][:], x_hi[c][:], ALU.subtract).then_inc(lo_done, 1)
                        if first(t, 1):
                            for n in range(CH * c, CH * c + CH):
                                wvo.split_lo(dve, n)
                s = stage(k, m, 1, 2, TILES)
                if s is not None:
                    t, b, kb = s
                    dve.wait_ge(x_used, NC * t + NC)
                    dve.wait_ge(y_in[b], 16 * kb + 16)
                    if not first(t, 2):
                        dve.wait_ge(h_stored[b], 16 * kb)
                    nc.vector.tensor_tensor(h[b][:], ps_h[b][:], y[b][:], ALU.add).then_inc(h_done, 1)

            run_steps(dve, TILES, DEPTH, 2, body)

        @block.tensor
        def _(pe):
            def body(k, m):
                s = stage(k, m, 0, 2, TILES)
                if s is None:
                    return
                t, b, kb = s
                outs = [ps_h[b][:, 0:512], ps_h[b][:, 512:1024]]
                if not first(t, 2):
                    pe.wait_ge(h_done, t - 1)
                for c in range(NC):
                    pe.wait_ge(lo_done, NC * t + c + 1)
                    for j in range(CH):
                        n = CH * c + j
                        if first(t, 1):
                            wvo.wait(pe, n)
                        last = three_pass(nc, outs, x_hi[c][:, j, :], x_lo[c][:, j, :],
                                          [w_hi[:, n, 0:512], w_hi[:, n, 512:1024]],
                                          [w_lo[:, n, 0:512], w_lo[:, n, 512:1024]], n == 0, n == PAIRS - 1)
                    last.then_inc(x_used, 1)

            run_steps(pe, TILES, DEPTH, 2, body)


ER = EXP * RANK
FW = DM + ER + NR + 1
CUT = [0, 390, 780, FW]
A_AT = DM - CUT[2]
R_AT = A_AT + ER


def ffn(nc, d, wf, h, h_in, ident):
    with ExitStack() as ctx:
        mem = Memory(nc, ctx, "ffn")
        w_hi = mem.sb("w_hi", [P, KM, FW], F32R)
        w_lo = mem.sb("w_lo", [P, KM, FW], F32R)
        b_hi = mem.sb("b_hi", [P, 1, DM], F32R)
        b_lo = mem.sb("b_lo", [P, 1, DM], F32R)
        wf.into([(w_hi[:, n, :], w_lo[:, n, :], None) for n in range(KM)] + [(b_hi[:, 0, :], b_lo[:, 0, :], None)])
        EARLY = Splitter.RING
        bias = mem.sb("bias", [P, DM])
        rbias = mem.sb("rbias", [P, NR])
        lower = mem.sb("lower", [P, NR, NR])
        numbers = mem.sb("numbers", [P, EXP, NR])
        emap = mem.sb("emap", [P, NR], I32)
        emapf = mem.sb("emapf", [P, NR])
        place = mem.sb("place", [P, EXP, NR])
        res = [mem.sb(f"res{i}", [P, DM]) for i in range(3)]
        o = [mem.sb(f"o{i}", [P, DM]) for i in range(2)]
        xn = [mem.sb(f"xn{i}", [P, DM]) for i in range(2)]
        xt_hi = [mem.sb(f"xt_hi{i}", [P, KM, P], F32R) for i in range(2)]
        xt_lo = [mem.sb(f"xt_lo{i}", [P, KM, P], F32R) for i in range(2)]
        bn = mem.sb("bn", [P, 12])
        vec = mem.sb("vec", [P, 16])
        lg = mem.sb("lg", [P, NR])
        ex = mem.sb("ex", [P, NR])
        pr = mem.sb("pr", [P, NR])
        over = mem.sb("over", [P, NR, NR])
        tie = mem.sb("tie", [P, NR, NR])
        rank = mem.sb("rank", [P, NR])
        kept = mem.sb("kept", [P, NR])
        pick = mem.sb("pick", [P, EXP, NR])
        we = mem.sb("we", [P, EXP])
        hw = mem.sb("hw", [P, ER])
        ht_hi = mem.sb("ht_hi", [P, P], F32R)
        ht_lo = mem.sb("ht_lo", [P, P], F32R)
        ps_o = [[mem.ps(f"ps_o{i}_{c}", [P, 512]) for c in range(3)] for i in range(2)]
        ps_x = [mem.ps(f"ps_x{i}", [P, 4, P]) for i in range(2)]
        const_in = mem.sem("const_in")
        bias_in = mem.sem("bias_in")
        xn_done = mem.sem("xn_done")
        x_turned = mem.sem("x_turned")
        xhi_done = mem.sem("xhi_done")
        xlo_done = mem.sem("xlo_done")
        base_made = mem.sem("base_made")
        logits_done = mem.sem("logits_done")
        exp_done = mem.sem("exp_done")
        hw_done = mem.sem("hw_done")
        hw_turned = mem.sem("hw_turned")
        hhi_done = mem.sem("hhi_done")
        hlo_done = mem.sem("hlo_done")
        lora_made = mem.sem("lora_made")
        res_done = mem.sem("res_done")
        o_done = mem.sem("o_done")
        o_stored = mem.sems("o_stored", 2)
        link_sem = mem.sem("link")
        table_sem = mem.sem("table")
        block = ctx.enter_context(nc.Block())
        D_X, D_M, D_L = 1, 2, 3
        DEPTH = 4
        U = 6

        def nth(kb, u, per):
            return kb * (U // per) + u // per + 1

        @block.sync
        def _(sp):
            def body(k, m):
                s = stage(k, m, D_L + 1, U, TILES)
                if s is not None:
                    t, u, kb = s
                    sp.wait_ge(o_done, t + 1)
                    sp.dma_start(d["out"][t], o[u % 2][:]).then_inc(o_stored[u % 2], 16)
                s = stage(k, m, 0, U, TILES)
                if s is None:
                    return
                t, u, kb = s
                if not first(t, 3):
                    sp.wait_ge(res_done, t - 2)
                    sp.wait_ge(xn_done, t - 2)
                    sp.dma_start(h[u % 3][:], d["h"][t]).then_inc(h_in[u % 3], 16)
                if first(t, 1):
                    sp.dma_start(bias[:], d["base_b"]).then_inc(bias_in, 16)
                if isinstance(t, int) and t == 1:
                    for n in range(EARLY, KM + 1):
                        wf.load(sp, n)
                    for dst, name in ((rbias, "router_b"), (lower, "lower"), (numbers, "numbers"), (emap, "emap")):
                        sp.dma_start(dst[:], d[name]).then_inc(const_in, 16)

            run_steps(sp, TILES, DEPTH, U, body)
            for b in range(2):
                sp.wait_ge(o_stored[b], 16 * TILES // 2)

        @block.gpsimd
        def _(pool):
            pool.wait_ge(bias_in, 16)

            def body(k, m):
                s = stage(k, m, 0, U, TILES)
                if s is not None:
                    t, u, kb = s
                    pool.wait_ge(h_in[u % 3], 16 * nth(kb, u, 3))
                    if not first(t, 3):
                        pool.wait_ge(o_done, t - 2)
                    nc.gpsimd.tensor_tensor(res[u % 3][:], h[u % 3][:], bias[:], ALU.add).then_inc(res_done, 1)

            run_steps(pool, TILES, DEPTH, U, body)

        @block.scalar
        def _(act):
            for n in range(EARLY):
                wf.split_hi(act, n)

            def body(k, m):
                s = stage(k, m, D_L, U, TILES)
                if s is not None:
                    t, u, kb = s
                    act.wait_ge(logits_done, t + 1)
                    nc.scalar.activation(ex[:], lg[:], ACT.Exp, bias=vec[:, 4:5],
                                         accum_out=vec[:, 5:6]).then_inc(exp_done, 1)
                s = stage(k, m, D_X, U, TILES)
                if s is not None:
                    t, u, kb = s
                    if not first(t, 2):
                        act.wait_ge(base_made, t - 1)
                    for c in range(2):
                        act.wait_ge(x_turned, 2 * t + c + 1)
                        nc.scalar.activation(xt_hi[u % 2][:, 4 * c:4 * c + 4, :], ps_x[c][:],
                                             ACT.Copy).then_inc(xhi_done, 1)
                    if first(t, 1):
                        for n in range(EARLY, KM + 1):
                            wf.split_hi(act, n)
                s = stage(k, m, D_L, U, TILES)
                if s is not None:
                    t, u, kb = s
                    act.wait_ge(hw_turned, t + 1)
                    if not first(t, 1):
                        act.wait_ge(lora_made, t)
                    nc.scalar.activation(ht_hi[:], ps_x[0][:, 0, :], ACT.Copy).then_inc(hhi_done, 1)

            run_steps(act, TILES, DEPTH, U, body)

        @block.vector
        def _(dve):
            link = Link(dve, link_sem, INV_SQRT_LINKS + 4 + 11)
            table_link = Link(dve, table_sem, 0)

            def body(k, m):
                s = stage(k, m, D_L, U, TILES)
                if s is not None:
                    t, u, kb = s
                    ps = ps_o[u % 2][2]
                    if first(t, 1):
                        dve.wait_ge(const_in, 64)
                        table_link(nc.vector.tensor_copy(emapf[:], emap[:]))
                        table_link(nc.vector.tensor_tensor(place[:],
                                                           emapf[:].unsqueeze(1).broadcast_to((P, EXP, NR)),
                                                           numbers[:], ALU.is_equal))
                        table_link(nc.vector.tensor_scalar(place[:], place[:], 2.0, None, ALU.mult))
                    dve.wait_ge(base_made, t + 1)
                    link(nc.vector.tensor_tensor(lg[:], ps[:, R_AT:R_AT + NR], rbias[:], ALU.add))
                    link(nc.vector.tensor_reduce(vec[:, 3:4], lg[:], AX.X, ALU.max))
                    nc.vector.tensor_scalar(vec[:, 4:5], vec[:, 3:4], -1.0, None, ALU.mult).then_inc(logits_done, 1)
                    dve.wait_ge(exp_done, t + 1)
                    link(nc.vector.reciprocal(vec[:, 6:7], vec[:, 5:6]))
                    link(nc.vector.tensor_scalar(pr[:], ex[:], vec[:, 6:7], None, ALU.mult))
                    pj = pr[:].unsqueeze(1).broadcast_to((P, NR, NR))
                    pi = pr[:].unsqueeze(2).broadcast_to((P, NR, NR))
                    nc.vector.tensor_tensor(over[:], pj, pi, ALU.is_gt)
                    link(nc.vector.tensor_tensor(tie[:], pj, pi, ALU.is_equal))
                    link(nc.vector.tensor_tensor(tie[:], tie[:], lower[:], ALU.mult))
                    link(nc.vector.tensor_tensor(over[:], over[:], tie[:], ALU.add))
                    link(nc.vector.tensor_reduce(rank[:], over[:], AX.X, ALU.add))
                    link(nc.vector.scalar_tensor_tensor(kept[:], rank[:], float(EXP) - 0.5, pr[:], ALU.is_lt, ALU.mult))
                    link(nc.vector.tensor_tensor(pick[:], kept[:].unsqueeze(1).broadcast_to((P, EXP, NR)), place[:],
                                                 ALU.mult))
                    if not first(t, 1):
                        dve.wait_ge(hw_turned, t)
                    nc.vector.tensor_reduce(we[:], pick[:], AX.X, ALU.add).then_inc(link_sem, 1)
                    link.n += 1
                    dve.wait_ge(link_sem, link.base + link.n)
                    nc.vector.tensor_tensor(hw[:].rearrange("p (e r) -> p e r", e=EXP),
                                            ps[:, A_AT:A_AT + ER].rearrange("p (e r) -> p e r", e=EXP),
                                            we[:].unsqueeze(2).broadcast_to((P, EXP, RANK)), ALU.mult).then_inc(hw_done, 1)
                s = stage(k, m, D_X, U, TILES)
                if s is not None:
                    t, u, kb = s
                    for c in range(2):
                        dve.wait_ge(xhi_done, 2 * t + c + 1)
                        nc.vector.tensor_tensor(xt_lo[u % 2][:, 4 * c:4 * c + 4, :], ps_x[c][:],
                                                xt_hi[u % 2][:, 4 * c:4 * c + 4, :], ALU.subtract).then_inc(xlo_done, 1)
                s = stage(k, m, 0, U, TILES)
                if s is not None:
                    t, u, kb = s
                    hh = h[u % 3]
                    dve.wait_ge(h_in[u % 3], 16 * nth(kb, u, 3))
                    nc.vector.bn_stats(bn[:, 0:6], hh[:, 0:512])
                    link(nc.vector.bn_stats(bn[:, 6:12], hh[:, 512:1024]))
                    link.settle()
                    link(nc.vector.bn_aggr(vec[:, 8:10], bn[:]))
                    link(nc.vector.tensor_scalar(vec[:, 10:11], vec[:, 9:10], LN_EPS, None, ALU.add))
                    inv_sqrt(nc, link, vec[:, 10:11], vec[:, 13:14], vec[:, 11:12], vec[:, 12:13])
                    if not first(t, 2):
                        dve.wait_ge(x_turned, 2 * t - 2)
                    nc.vector.tensor_scalar(xn[u % 2][:], hh[:], vec[:, 8:9], vec[:, 11:12], ALU.subtract,
                                            ALU.mult).then_inc(xn_done, 1)
                    if first(t, 1):
                        for n in range(EARLY):
                            wf.split_lo(dve, n)
                    if isinstance(t, int) and t == 1:
                        for n in range(EARLY, KM + 1):
                            wf.split_lo(dve, n)
                s = stage(k, m, D_L, U, TILES)
                if s is not None:
                    t, u, kb = s
                    dve.wait_ge(hhi_done, t + 1)
                    nc.vector.tensor_tensor(ht_lo[:], ps_x[0][:, 0, :], ht_hi[:], ALU.subtract).then_inc(hlo_done, 1)
                    dve.wait_ge(lora_made, t + 1)
                    dve.wait_ge(res_done, t + 1)
                    if not first(t, 2):
                        dve.wait_ge(o_stored[u % 2], 16 * nth(kb, u, 2) - 16)
                    for c in range(3):
                        a, e = CUT[c], min(CUT[c + 1], DM)
                        last = nc.vector.tensor_tensor(o[u % 2][:, a:e], ps_o[u % 2][c][:, 0:e - a],
                                                       res[u % 3][:, a:e], ALU.add)
                    last.then_inc(o_done, 1)

            def step(k, m):
                link.step(k * U + m)
                body(k, m)
                link.fill()

            run_steps(dve, TILES, DEPTH, U, step)

        @block.tensor
        def _(pe):
            def base(s, blocks):
                t, u, kb = s
                for n in blocks:
                    if n % 4 == 0:
                        pe.wait_ge(xlo_done, 2 * t + n // 4 + 1)
                    if first(t, 1):
                        wf.wait(pe, n)
                    last = three_pass(nc, [ps_o[u % 2][c][:, 0:CUT[c + 1] - CUT[c]] for c in range(3)],
                                      xt_hi[u % 2][:, n, :], xt_lo[u % 2][:, n, :],
                                      [w_hi[:, n, CUT[c]:CUT[c + 1]] for c in range(3)],
                                      [w_lo[:, n, CUT[c]:CUT[c + 1]] for c in range(3)], n == 0, n == KM - 1)
                if n == KM - 1:
                    last.then_inc(base_made, 1)

            def turn(s):
                t, u, kb = s
                pe.wait_ge(xn_done, t + 1)
                if not first(t, D_L - D_X + 1):
                    pe.wait_ge(hlo_done, t - (D_L - D_X))
                for c in range(2):
                    if not first(t, 1):
                        pe.wait_ge(xlo_done, 2 * t + (c - 1))
                    for j in range(4):
                        n = 4 * c + j
                        last = nc.tensor.transpose(ps_x[c][:, j, :], xn[u % 2][:, P * n:P * n + P], ident[:])
                    last.then_inc(x_turned, 1)

            def body(k, m):
                x = stage(k, m, D_X, U, TILES)
                s = stage(k, m, D_M, U, TILES)
                if x is not None and not (s is not None and first(s[0], 1)):
                    turn(x)
                if s is not None:
                    if not first(s[0], 2):
                        pe.wait_ge(o_done, s[0] - 1)
                    base(s, range(0, 4))
                    if first(s[0], 1):
                        turn(x)
                sl = stage(k, m, D_L, U, TILES)
                if sl is not None:
                    t, u, kb = sl
                    pe.wait_ge(hw_done, t + 1)
                    pe.wait_ge(xlo_done, min(2 * t + 2 * (D_L - D_X) + 1, 2 * TILES) if isinstance(t, int)
                               else 2 * t + 2 * (D_L - D_X) + 1)
                    nc.tensor.transpose(ps_x[0][:, 0, :], hw[:], ident[:]).then_inc(hw_turned, 1)
                if s is not None:
                    base(s, range(4, 7))
                if sl is not None:
                    t, u, kb = sl
                    pe.wait_ge(hlo_done, t + 1)
                    if first(t, 1):
                        wf.wait(pe, KM)
                    ends = [(CUT[c], min(CUT[c + 1], DM)) for c in range(3)]
                    last = three_pass(nc, [ps_o[u % 2][c][:, 0:e - a] for c, (a, e) in enumerate(ends)], ht_hi[:],
                                      ht_lo[:], [b_hi[:, 0, a:e] for a, e in ends], [b_lo[:, 0, a:e] for a, e in ends],
                                      False, True, onto=True)
                    last.then_inc(lora_made, 1)
                if s is not None:
                    base(s, range(7, KM))

            run_steps(pe, TILES, DEPTH, U, body)


def build(nc, d):
    with ExitStack() as ctx:
        Memory.whole = ctx
        mem = Memory(nc, ctx, "all")
        ident = mem.sb("ident", [P, P])
        split = Splitter(nc)
        tok_up(nc, d, split, ident)
        shared = Memory(nc, ctx, "shared")
        ring = [shared.sb(f"ring{i}", [P, FW]) for i in range(split.RING)]
        with ExitStack() as kept:
            mem = Memory(nc, kept, "kept")
            qn_hi = mem.sb("qn_hi", [P, 2, TOKP], F32R)
            qn_lo = mem.sb("qn_lo", [P, 2, TOKP], F32R)
            k_t = mem.sb("k_t", [P, TOKP])
            tok_down(nc, d, split, ring, ident, qn_hi, qn_lo, k_t)
            wvo = split.pieces(ring, [d["wvo"][:, n, :] for n in range(PAIRS)])
            attention(nc, d, wvo, ident, qn_hi, qn_lo, k_t)
        wf = split.pieces(ring, [d["wf"][:, n, :] for n in range(KM)] + [d["lora_b"][:, 0, :]])
        h = [shared.sb(f"h{i}", [P, DM]) for i in range(3)]
        h_in = shared.sems("h_in", 3)
        attn_out(nc, d, wvo, wf, h, h_in)
        ffn(nc, d, wf, h, h_in, ident)


def rope_tables():
    dim, base, factor, orig = RO, 10000.0, 128.0, 2048

    def corr(rot):
        return dim * math.log(orig / (rot * 2 * math.pi)) / (2 * math.log(base))

    low, high = max(math.floor(corr(32.0)), 0), min(math.ceil(corr(1.0)), dim - 1)
    hi = high + 0.001 if low == high else float(high)
    ramp = np.clip((np.arange(dim // 2, dtype=np.float32) - low) / (hi - low), 0.0, 1.0)
    keep = 1.0 - ramp
    extra = 1.0 / base ** (np.arange(0, dim, 2, dtype=np.float32) / dim)
    freq = extra / factor * (1.0 - keep) + extra * keep
    angle = np.outer(np.arange(512, dtype=np.float32), freq)[:SEQ]
    row = np.arange(P) % RO
    cos = np.cos(angle)[:, row // 2].T
    sin = np.sin(angle)[:, row // 2].T * np.where(row % 2 == 0, -1.0, 1.0)[:, None]
    return (np.ascontiguousarray(np.tile(cos, (1, GB)), dtype=np.float32),
            np.ascontiguousarray(np.tile(sin, (1, GB)), dtype=np.float32))


def blocks(w):
    return w.reshape(-1, P, w.shape[1]).transpose(1, 0, 2)


def kernel(x, L0_tok_w1, L0_tok_w2, L0_tok_ln_pre_w, L0_tok_ln_post_w, L0_attn_wq_a, L0_attn_q_a_ln_w,
           L0_attn_wq_b, L0_attn_wkv_a, L0_attn_kv_a_ln_w, L0_attn_wkv_b, L0_attn_wo, L0_ffn_base_W,
           L0_ffn_base_b, L0_ffn_router_W, L0_ffn_router_b, L0_ffn_A, L0_ffn_B, L0_ffn_expert_map):
    import concourse.bacc as bacc
    from concourse.bass_utils import run_bass_kernel_spmd

    f32 = np.float32
    rows = np.zeros((BATCH, SEQ * 8, 320), f32)
    rows[:, :750] = np.asarray(x)
    flat = np.zeros((TOKP, DIN), f32)
    flat[:TOK] = rows.reshape(TOK, DIN)
    x_rows = flat.reshape(TILES, P, DIN)
    x_t = x_rows.reshape(TILES, P, KIN, P).transpose(0, 3, 2, 1)

    wq_b = np.asarray(L0_attn_wq_b).reshape(PAIRS, 2, NOPE + RO, QR)
    wkv_b = np.asarray(L0_attn_wkv_b).reshape(PAIRS, 2, NOPE + VD, KR)
    wq_rope = wq_b[:, ::-1, NOPE:, :]
    wq_rope = wq_rope.reshape(PAIRS, 2 * RO, 2, P).transpose(0, 3, 2, 1)
    wo = np.asarray(L0_attn_wo).T.reshape(PAIRS, 2, VD, DM).transpose(0, 2, 1, 3)
    wf = np.zeros((DM, FW), f32)
    wf[:, :DM] = np.asarray(L0_ffn_base_W).T
    wf[:, DM:DM + ER] = np.asarray(L0_ffn_A).reshape(ER, DM).T
    wf[:, DM + ER:DM + ER + NR] = np.asarray(L0_ffn_router_W).T
    cos, sin = rope_tables()
    q, key = np.arange(SEQ)[:, None], np.arange(SEQ)[None, :]
    mask = np.zeros((P, SEQ), f32)
    mask[:SEQ] = np.where(key <= q, 0.0, MASKED)
    i, j = np.arange(NR)[:, None], np.arange(NR)[None, :]

    def on_all(a):
        return np.broadcast_to(np.asarray(a)[None], (P, *np.asarray(a).shape))

    turns = np.stack([a[:RO, np.arange(TOKP) % SEQ].T for a in (cos, sin)], axis=1).reshape(TILES, P, 2, RO)
    arrays = {
        "x_rows": x_rows,
        "x_t": x_t,
        "w1": blocks(np.asarray(L0_tok_w1).T),
        "pre_ln": np.asarray(L0_tok_ln_pre_w).reshape(KIN, P).T,
        "w2": blocks(np.asarray(L0_tok_w2).T),
        "post_ln": on_all(L0_tok_ln_post_w),
        "wa": blocks(np.concatenate([np.asarray(L0_attn_wq_a).T, np.asarray(L0_attn_wkv_a).T], axis=1)),
        "q_ln": np.asarray(L0_attn_q_a_ln_w).reshape(2, P).T,
        "kv_ln": on_all(L0_attn_kv_a_ln_w),
        "wq_nope": wq_b[:, :, :NOPE].reshape(PAIRS, P, QR),
        "wq_rope": wq_rope,
        "wk": wkv_b[:, :, :NOPE].reshape(PAIRS, P, KR),
        "wv": wkv_b[:, :, NOPE:].transpose(0, 2, 1, 3),
        "wo": wo,
        "wf": blocks(wf),
        "lora_b": np.asarray(L0_ffn_B).transpose(0, 2, 1).reshape(P, 1, DM),
        "base_b": on_all(L0_ffn_base_b),
        "router_b": on_all(L0_ffn_router_b),
        "emap": on_all(np.asarray(L0_ffn_expert_map)),
        "cos": cos,
        "turns": turns,
        "sin": sin,
        "mask": mask,
        "ident": np.eye(P, dtype=f32),
        "lower": on_all((j < i).astype(f32)),
        "numbers": on_all(np.tile(np.arange(EXP, dtype=f32)[:, None], (1, NR))),
    }
    arrays = {n: np.ascontiguousarray(a) for n, a in arrays.items()}
    nc = bacc.Bacc("TRN2", target_bir_lowering=False, num_devices=1)
    d = {n: nc.dram_tensor(n, a.shape, mybir.dt.from_np(a.dtype), kind="ExternalInput").ap()
         for n, a in arrays.items()}
    for n, shape in (("wq_pair", (PAIRS, P, 2, 2 * P)), ("wvo", (P, PAIRS, DM)), ("g_t", (TILES, P, HID)),
                     ("y", (TILES, P, DM)), ("o_t", (P, PAIRS, TOKP)), ("h", (TILES, P, DM))):
        d[n] = nc.dram_tensor(n, shape, F32, kind="Internal").ap()
    d["out"] = nc.dram_tensor("out", (TILES, P, DM), F32, kind="ExternalOutput").ap()
    build(nc, d)
    r = run_bass_kernel_spmd(nc, [arrays], core_ids=[0])
    return r.results[0]["out"].reshape(TOKP, DM)[:TOK].reshape(BATCH, SEQ, DM)
```
